# Optimizing a Trainium2 kernel written in Bass

```python
import numpy as np
import jax
import jax.numpy as jnp

def _softmax(x, axis=-1):
    return jax.nn.softmax(x, axis=axis)

def _gelu(x):
    return jax.nn.gelu(x, approximate=True)

def _silu(x):
    return jax.nn.silu(x)

def _sigmoid(x):
    return jax.nn.sigmoid(x)

def _layernorm(x, axis=-1, eps=1e-05):
    m = jnp.mean(x, axis=axis, keepdims=True)
    v = jnp.var(x, axis=axis, keepdims=True)
    return (x - m) / jnp.sqrt(v + eps)

def _scatter_add(tgt, idx, src, axis=0):
    return tgt.at[idx].add(src)

def _segment_sum(src, seg, n):
    return jax.ops.segment_sum(src, seg, n)
kernel_name = 'mk_xattn_ffn_d2_seqx_r8_640e4c'

def setup_inputs(seed: int=0):
    np.random.seed(seed)
    _w = jnp.asarray

    def _rec_inputs():
        import jax
        import jax.numpy as jnp
        _rk = jax.random.key(seed)
        x = -0.000125 + 0.9999 * jax.random.normal(jax.random.fold_in(_rk, 1), (2, 256, 512), jnp.float32)
        _lenS = 256 - jax.random.randint(jax.random.fold_in(_rk, 7), (2,), 0, max(1, 256 // 4) + 1, jnp.int32)
        _lenS2 = 512 - jax.random.randint(jax.random.fold_in(_rk, 8), (2,), 0, max(1, 512 // 4) + 1, jnp.int32)
        _ctx_4096P = jax.random.normal(jax.random.fold_in(_rk, 11), (2, 16, 512), jnp.float32)
        _ctx_4096c = jax.random.dirichlet(jax.random.fold_in(_rk, 511), 0.3 * jnp.ones((16,), jnp.float32), (2, 512))
        _ctx_4096t = jnp.einsum('bsk,bkd->bsd', _ctx_4096c, _ctx_4096P)
        _ctx_4096t = _ctx_4096t * jax.lax.rsqrt(jnp.mean(jnp.square(_ctx_4096t)) + 1e-12) * 0.953939
        ctx_4096 = -5.72187e-05 + 0.999849 * (_ctx_4096t + 0.3 * jax.random.normal(jax.random.fold_in(_rk, 611), (2, 512, 512), jnp.float32))
        _validS = jnp.arange(256)[None, :] < _lenS[:, None]
        _validS2 = jnp.arange(512)[None, :] < _lenS2[:, None]
        _causal = jnp.tril(jnp.ones((256, 256), dtype=bool))
        mask_1x1xSxS2_ff0 = jnp.where(jnp.ones((1, 1, 256, 512), dtype=bool), 0.0, -1000000000.0).astype(jnp.float32)
        return (x, ctx_4096, mask_1x1xSxS2_ff0)
    x, ctx_4096, mask_1x1xSxS2_ff0 = _rec_inputs()

    def _L0_xattn_setup():
        import jax, jax.numpy as jnp
        import numpy as np
        QMIN = 0.0
        QMAX = 255.0

        def fake_quant(x, scale, zp):
            s = scale.reshape(())
            z = zp.reshape(())
            q = jnp.clip(jnp.round(x / s + z), QMIN, QMAX)
            return (q - z) * s
        key = jax.random.key(seed)
        k1, k2 = jax.random.split(key)
        B, M, K, N = (4, 256, 512, 512)
        x1 = jax.random.normal(k1, (B, M, K), dtype=jnp.float32)
        x2 = jax.random.normal(k2, (B, K, N), dtype=jnp.float32)
        x1_scale = jnp.full((1,), 8.0 / 255.0, dtype=jnp.float32)
        x1_zp = jnp.full((1,), 128.0, dtype=jnp.float32)
        x2_scale = jnp.full((1,), 8.0 / 255.0, dtype=jnp.float32)
        x2_zp = jnp.full((1,), 128.0, dtype=jnp.float32)
        return {'x1': x1, 'x2': x2, 'x1_scale': x1_scale, 'x1_zp': x1_zp, 'x2_scale': x2_scale, 'x2_zp': x2_zp}
    _L0_xattn_all = _L0_xattn_setup()
    _L0_xattn_in = {k: v for k, v in _L0_xattn_all.items() if k in ('x1_scale', 'x1_zp', 'x2_scale', 'x2_zp')}
    del _L0_xattn_all

    def _L0_ffn_setup():
        import jax, jax.numpy as jnp
        import numpy as np
        BLOCK = 32
        WBITS = 4
        ABITS = 16

        def _ste(x, dq):
            return x + jax.lax.stop_gradient(dq - x)

        def block_qdq_weight(w, block=BLOCK, bits=WBITS):
            out_f, in_f = w.shape
            wb = w.reshape(out_f, in_f // block, block)
            qmax = 2 ** (bits - 1) - 1
            scale = jnp.maximum(jnp.max(jnp.abs(wb), axis=-1, keepdims=True) / qmax, 1e-12)
            wq = jnp.clip(jnp.round(wb / scale), -qmax - 1, qmax) * scale
            return _ste(w, wq.reshape(out_f, in_f))

        def act_qdq(x, bits=ABITS):
            qmax = 2 ** bits - 1
            mn = jnp.minimum(jnp.min(x), 0.0)
            mx = jnp.maximum(jnp.max(x), 0.0)
            scale = jnp.maximum((mx - mn) / qmax, 1e-12)
            zp = jnp.clip(jnp.round(-mn / scale), 0, qmax)
            q = jnp.clip(jnp.round(x / scale) + zp, 0, qmax)
            return _ste(x, (q - zp) * scale)

        def fixed_qdq(x, scale, zp=0.0, bits=ABITS):
            qmax = 2 ** bits - 1
            q = jnp.clip(jnp.round(x / scale) + zp, 0, qmax)
            return _ste(x, (q - zp) * scale)
        key = jax.random.key(seed)
        k1, k2, k3, k4 = jax.random.split(key, 4)
        H, I = (512, 1376)
        x = jax.random.normal(k1, (2, 256, H), dtype=jnp.float32)
        w_gate = jax.random.normal(k2, (I, H), dtype=jnp.float32) * H ** (-0.5)
        w_up = jax.random.normal(k3, (I, H), dtype=jnp.float32) * H ** (-0.5)
        w_down = jax.random.normal(k4, (H, I), dtype=jnp.float32) * I ** (-0.5)
        return {'x': x, 'w_gate': w_gate, 'w_up': w_up, 'w_down': w_down}
    _L0_ffn_all = _L0_ffn_setup()
    _L0_ffn_in = {k: v for k, v in _L0_ffn_all.items() if k in ('w_gate', 'w_up', 'w_down')}
    del _L0_ffn_all

    def _L1_xattn_setup():
        import jax, jax.numpy as jnp
        import numpy as np
        NUM_HEADS = 32
        NUM_KV_HEADS = 8
        HEAD_DIM = 128
        HIDDEN = 512
        EPS = 1e-05

        def rmsnorm(x, w, eps=EPS):
            xf = x.astype(jnp.float32)
            var = jnp.mean(xf * xf, axis=-1, keepdims=True)
            return w * (xf * jax.lax.rsqrt(var + eps)).astype(x.dtype)
        key = jax.random.key(seed)
        ks = jax.random.split(key, 10)
        B, Q, KV = (1, 128, 6404)
        s = 1.0 / np.sqrt(HIDDEN)
        return {'hidden_states': jax.random.normal(ks[0], (B, Q, HIDDEN), jnp.float32), 'cross_attention_states': jax.random.normal(ks[1], (B, KV, HIDDEN), jnp.float32), 'attention_mask': jnp.zeros((B, 1, Q, KV), jnp.float32), 'q_proj_w': jax.random.normal(ks[2], (NUM_HEADS * HEAD_DIM, HIDDEN), jnp.float32) * s, 'k_proj_w': jax.random.normal(ks[3], (NUM_KV_HEADS * HEAD_DIM, HIDDEN), jnp.float32) * s, 'v_proj_w': jax.random.normal(ks[4], (NUM_KV_HEADS * HEAD_DIM, HIDDEN), jnp.float32) * s, 'o_proj_w': jax.random.normal(ks[5], (HIDDEN, NUM_HEADS * HEAD_DIM), jnp.float32) * s, 'q_norm_w': jnp.ones((HEAD_DIM,), jnp.float32), 'k_norm_w': jnp.ones((HEAD_DIM,), jnp.float32)}
    _L1_xattn_all = _L1_xattn_setup()
    _L1_xattn_in = {k: v for k, v in _L1_xattn_all.items() if k in ('q_proj_w', 'k_proj_w', 'v_proj_w', 'o_proj_w', 'q_norm_w', 'k_norm_w')}
    del _L1_xattn_all

    def _L1_ffn_setup():
        import jax, jax.numpy as jnp
        import numpy as np
        DIM = 512
        INTER = 128
        E = 16
        GROUPS = 4
        LIM = 2
        K = 2
        SHARED_INTER = 2 * INTER
        SCALE = 1.0
        key = jax.random.key(seed)
        ks = jax.random.split(key, 16)

        def n(k, shape, s=0.02):
            return jax.random.normal(k, shape, jnp.float32) * s
        return {'x': jax.random.normal(ks[0], (1, 256, DIM), jnp.float32), 'router_w': n(ks[1], (DIM, E)), 'router_b': n(ks[2], (E,)), 'router_bias': n(ks[3], (E,), 1.0), 'ew1': n(ks[4], (E, DIM, INTER)), 'eb1': n(ks[5], (E, INTER)), 'ew2': n(ks[6], (E, DIM, INTER)), 'eb2': n(ks[7], (E, INTER)), 'ew3': n(ks[8], (E, INTER, DIM)), 'eb3': n(ks[9], (E, DIM)), 'sw1': n(ks[10], (DIM, SHARED_INTER)), 'sb1': n(ks[11], (SHARED_INTER,)), 'sw2': n(ks[12], (DIM, SHARED_INTER)), 'sb2': n(ks[13], (SHARED_INTER,)), 'sw3': n(ks[14], (SHARED_INTER, DIM)), 'sb3': n(ks[15], (DIM,))}
    _L1_ffn_all = _L1_ffn_setup()
    _L1_ffn_in = {k: v for k, v in _L1_ffn_all.items() if k in ('router_w', 'router_b', 'router_bias', 'ew1', 'eb1', 'ew2', 'eb2', 'ew3', 'eb3', 'sw1', 'sb1', 'sw2', 'sb2', 'sw3', 'sb3')}
    del _L1_ffn_all
    return {'x': x, 'ctx_4096': ctx_4096, 'mask_1x1xSxS2_ff0': mask_1x1xSxS2_ff0, 'L0_xattn_x1_scale': _L0_xattn_in['x1_scale'], 'L0_xattn_x1_zp': _L0_xattn_in['x1_zp'], 'L0_xattn_x2_scale': _L0_xattn_in['x2_scale'], 'L0_xattn_x2_zp': _L0_xattn_in['x2_zp'], 'L0_ffn_w_gate': _L0_ffn_in['w_gate'], 'L0_ffn_w_up': _L0_ffn_in['w_up'], 'L0_ffn_w_down': _L0_ffn_in['w_down'], 'L1_xattn_q_proj_w': _L1_xattn_in['q_proj_w'], 'L1_xattn_k_proj_w': _L1_xattn_in['k_proj_w'], 'L1_xattn_v_proj_w': _L1_xattn_in['v_proj_w'], 'L1_xattn_o_proj_w': _L1_xattn_in['o_proj_w'], 'L1_xattn_q_norm_w': _L1_xattn_in['q_norm_w'], 'L1_xattn_k_norm_w': _L1_xattn_in['k_norm_w'], 'L1_ffn_router_w': _L1_ffn_in['router_w'], 'L1_ffn_router_b': _L1_ffn_in['router_b'], 'L1_ffn_router_bias': _L1_ffn_in['router_bias'], 'L1_ffn_ew1': _L1_ffn_in['ew1'], 'L1_ffn_eb1': _L1_ffn_in['eb1'], 'L1_ffn_ew2': _L1_ffn_in['ew2'], 'L1_ffn_eb2': _L1_ffn_in['eb2'], 'L1_ffn_ew3': _L1_ffn_in['ew3'], 'L1_ffn_eb3': _L1_ffn_in['eb3'], 'L1_ffn_sw1': _L1_ffn_in['sw1'], 'L1_ffn_sb1': _L1_ffn_in['sb1'], 'L1_ffn_sw2': _L1_ffn_in['sw2'], 'L1_ffn_sb2': _L1_ffn_in['sb2'], 'L1_ffn_sw3': _L1_ffn_in['sw3'], 'L1_ffn_sb3': _L1_ffn_in['sb3']}

def reference(x, ctx_4096, mask_1x1xSxS2_ff0, L0_xattn_x1_scale, L0_xattn_x1_zp, L0_xattn_x2_scale, L0_xattn_x2_zp, L0_ffn_w_gate, L0_ffn_w_up, L0_ffn_w_down, L1_xattn_q_proj_w, L1_xattn_k_proj_w, L1_xattn_v_proj_w, L1_xattn_o_proj_w, L1_xattn_q_norm_w, L1_xattn_k_norm_w, L1_ffn_router_w, L1_ffn_router_b, L1_ffn_router_bias, L1_ffn_ew1, L1_ffn_eb1, L1_ffn_ew2, L1_ffn_eb2, L1_ffn_ew3, L1_ffn_eb3, L1_ffn_sw1, L1_ffn_sb1, L1_ffn_sw2, L1_ffn_sb2, L1_ffn_sw3, L1_ffn_sb3):
    import jax
    import jax.numpy as jnp

    def _L0_xattn_ref(x1, x2, x1_scale, x1_zp, x2_scale, x2_zp):
        import jax, jax.numpy as jnp
        import numpy as np
        QMIN = 0.0
        QMAX = 255.0

        def fake_quant(x, scale, zp):
            s = scale.reshape(())
            z = zp.reshape(())
            q = jnp.clip(jnp.round(x / s + z), QMIN, QMAX)
            return (q - z) * s
        q1 = fake_quant(x1, x1_scale, x1_zp)
        q2 = fake_quant(x2, x2_scale, x2_zp)
        return jnp.matmul(q1, q2)

    def _L0_ffn_ref(x, w_gate, w_up, w_down):
        import jax, jax.numpy as jnp
        import numpy as np
        BLOCK = 32
        WBITS = 4
        ABITS = 16

        def _ste(x, dq):
            return x + jax.lax.stop_gradient(dq - x)

        def block_qdq_weight(w, block=BLOCK, bits=WBITS):
            out_f, in_f = w.shape
            wb = w.reshape(out_f, in_f // block, block)
            qmax = 2 ** (bits - 1) - 1
            scale = jnp.maximum(jnp.max(jnp.abs(wb), axis=-1, keepdims=True) / qmax, 1e-12)
            wq = jnp.clip(jnp.round(wb / scale), -qmax - 1, qmax) * scale
            return _ste(w, wq.reshape(out_f, in_f))

        def act_qdq(x, bits=ABITS):
            qmax = 2 ** bits - 1
            mn = jnp.minimum(jnp.min(x), 0.0)
            mx = jnp.maximum(jnp.max(x), 0.0)
            scale = jnp.maximum((mx - mn) / qmax, 1e-12)
            zp = jnp.clip(jnp.round(-mn / scale), 0, qmax)
            q = jnp.clip(jnp.round(x / scale) + zp, 0, qmax)
            return _ste(x, (q - zp) * scale)

        def fixed_qdq(x, scale, zp=0.0, bits=ABITS):
            qmax = 2 ** bits - 1
            q = jnp.clip(jnp.round(x / scale) + zp, 0, qmax)
            return _ste(x, (q - zp) * scale)
        sigmoid_scale = 1.0 / 65536.0
        wg = block_qdq_weight(w_gate)
        wu = block_qdq_weight(w_up)
        wd = block_qdq_weight(w_down)
        xq = act_qdq(x)
        up = act_qdq(jnp.einsum('bsh,ih->bsi', xq, wu))
        gate = act_qdq(jnp.einsum('bsh,ih->bsi', xq, wg))
        sig = fixed_qdq(jax.nn.sigmoid(gate), sigmoid_scale)
        gate = act_qdq(gate * sig)
        o = act_qdq(gate * up)
        return jnp.einsum('bsi,hi->bsh', o, wd)

    def _L1_xattn_ref(hidden_states, cross_attention_states, attention_mask, q_proj_w, k_proj_w, v_proj_w, o_proj_w, q_norm_w, k_norm_w):
        import jax, jax.numpy as jnp
        import numpy as np
        NUM_HEADS = 32
        NUM_KV_HEADS = 8
        HEAD_DIM = 128
        HIDDEN = 512
        EPS = 1e-05

        def rmsnorm(x, w, eps=EPS):
            xf = x.astype(jnp.float32)
            var = jnp.mean(xf * xf, axis=-1, keepdims=True)
            return w * (xf * jax.lax.rsqrt(var + eps)).astype(x.dtype)
        B, Q, _ = hidden_states.shape
        KV = cross_attention_states.shape[1]
        n_rep = NUM_HEADS // NUM_KV_HEADS
        q = (hidden_states @ q_proj_w.T).reshape(B, Q, NUM_HEADS, HEAD_DIM).transpose(0, 2, 1, 3)
        k = (cross_attention_states @ k_proj_w.T).reshape(B, KV, NUM_KV_HEADS, HEAD_DIM).transpose(0, 2, 1, 3)
        v = (cross_attention_states @ v_proj_w.T).reshape(B, KV, NUM_KV_HEADS, HEAD_DIM).transpose(0, 2, 1, 3)
        q = rmsnorm(q, q_norm_w)
        k = jnp.repeat(k, n_rep, axis=1)
        v = jnp.repeat(v, n_rep, axis=1)
        k = rmsnorm(k, k_norm_w)
        scale = 1.0 / np.sqrt(HEAD_DIM)
        scores = jnp.einsum('bhqd,bhkd->bhqk', q, k) * scale + attention_mask
        attn = jax.nn.softmax(scores.astype(jnp.float32), axis=-1).astype(q.dtype)
        out = jnp.einsum('bhqk,bhkd->bhqd', attn, v)
        out = out.transpose(0, 2, 1, 3).reshape(B, Q, NUM_HEADS * HEAD_DIM)
        return out @ o_proj_w.T

    def _L1_ffn_ref(x, router_w, router_b, router_bias, ew1, eb1, ew2, eb2, ew3, eb3, sw1, sb1, sw2, sb2, sw3, sb3):
        import jax, jax.numpy as jnp
        import numpy as np
        DIM = 512
        INTER = 128
        E = 16
        GROUPS = 4
        LIM = 2
        K = 2
        SHARED_INTER = 2 * INTER
        SCALE = 1.0
        shape = x.shape
        xt = x.reshape(-1, DIM)
        T = xt.shape[0]
        logits = xt @ router_w + router_b
        scores = jax.nn.softmax(logits.astype(jnp.float32), axis=-1) + router_bias
        g = scores.reshape(T, GROUPS, E // GROUPS)
        _, gidx = jax.lax.top_k(g.max(axis=-1), LIM)
        keep = jnp.zeros((T, GROUPS), bool).at[jnp.arange(T)[:, None], gidx].set(True)
        masked = jnp.where(keep[:, :, None], g, -jnp.inf).reshape(T, E)
        _, idx = jax.lax.top_k(masked, K)
        vals = (jnp.take_along_axis(scores, idx, axis=1) * SCALE).astype(x.dtype)
        gate = jnp.zeros((T, E), x.dtype).at[jnp.arange(T)[:, None], idx].add(vals)

        def step(y, p):
            w1, b1, w2, b2, w3, b3, ge = p
            h = jax.nn.silu(xt @ w1 + b1) * (xt @ w2 + b2)
            return (y + ge[:, None] * (h @ w3 + b3), None)
        y, _ = jax.lax.scan(step, jnp.zeros_like(xt), (ew1, eb1, ew2, eb2, ew3, eb3, gate.T))
        z = jax.nn.silu(xt @ sw1 + sb1) * (xt @ sw2 + sb2) @ sw3 + sb3
        return (y + z).reshape(shape)
    x = x + _L0_xattn_ref(_layernorm(x, axis=-1), ctx_4096, L0_xattn_x1_scale, L0_xattn_x1_zp, L0_xattn_x2_scale, L0_xattn_x2_zp)
    x = x + _L0_ffn_ref(_layernorm(x, axis=-1), L0_ffn_w_gate, L0_ffn_w_up, L0_ffn_w_down)
    x = x + _L1_xattn_ref(_layernorm(x, axis=-1), ctx_4096, mask_1x1xSxS2_ff0, L1_xattn_q_proj_w, L1_xattn_k_proj_w, L1_xattn_v_proj_w, L1_xattn_o_proj_w, L1_xattn_q_norm_w, L1_xattn_k_norm_w)
    x = x + _L1_ffn_ref(_layernorm(x, axis=-1), L1_ffn_router_w, L1_ffn_router_b, L1_ffn_router_bias, L1_ffn_ew1, L1_ffn_eb1, L1_ffn_ew2, L1_ffn_eb2, L1_ffn_ew3, L1_ffn_eb3, L1_ffn_sw1, L1_ffn_sb1, L1_ffn_sw2, L1_ffn_sb2, L1_ffn_sw3, L1_ffn_sb3)
    return x

_drawn_inputs = setup_inputs


def setup_inputs(seed=0):
    import zlib

    import numpy as np

    out = dict(_drawn_inputs(seed))
    spreads = {'L1_xattn_q_norm_w': (1.0, 0.6), 'L1_xattn_k_norm_w': (1.0, 0.6)}
    factors = {'L1_ffn_router_w': 40.554,
     'L1_ffn_router_b': 64.0,
     'L1_ffn_router_bias': 8.0,
     'L1_ffn_ew1': 8.0,
     'L1_ffn_eb1': 8.0,
     'L1_ffn_ew2': 8.0,
     'L1_ffn_eb2': 8.0,
     'L1_ffn_ew3': 8.0,
     'L1_ffn_eb3': 47.459,
     'L1_ffn_sw1': 8.0,
     'L1_ffn_sb1': 64.0,
     'L1_ffn_sw2': 8.0,
     'L1_ffn_sb2': 64.0,
     'L1_ffn_sw3': 8.0,
     'L1_ffn_sb3': 64.0}
    for name, (base, spread) in spreads.items():
        noise = np.random.default_rng([zlib.crc32(name.encode()), seed]).standard_normal(out[name].shape)
        drawn = base * np.exp(spread * noise) if base else spread * noise
        out[name] = jnp.asarray(drawn.astype(out[name].dtype))
    for name, factor in factors.items():
        out[name] = (out[name] * factor).astype(out[name].dtype)
    return out
```

```python
import concourse.bass as bass
from concourse import mybir
from contextlib import ExitStack

F32 = mybir.dt.float32
F16 = mybir.dt.float16
BF16 = mybir.dt.bfloat16
ALU = mybir.AluOpType
ACT = mybir.ActivationFunctionType
AX = mybir.AxisListType

P = 128
B, SQ, D = 2, 256, 512
SKV = 512
TOK, KV = B * SQ, B * SKV
NT = TOK // P
KD = D // P
MT = KV // P
F = 1376
FT = (F + P - 1) // P
QB = 32
NCH = 3 * FT
H, HK, DH = 32, 8, 128
R = H // HK
NE, NS, INTER = 16, 2, 128
EX = NE + NS
EPS = 1e-5
MAGIC = 12582912.0
QMAX = 65535.0
TINY = 1e-12

SX = 16.0
SW = 64.0
SXW = SX * SW
SINT = 2.0 ** -8
SP = 1024.0

RAW = 3
K_AHEAD = 3
KB = 4
KW = 4
WS = FT
SC = 4


class Chain:

    def __init__(self, eng, sem):
        self.eng, self.sem, self.n, self.k = eng, sem, 0, 0

    def mark(self, ins):
        ins.then_inc(self.sem, 1)
        self.n, self.k = self.n + 1, self.k + 1
        return self.n

    def link(self, ins):
        self.eng.wait_ge(self.sem, self.mark(ins))

    def wait(self, value):
        self.eng.wait_ge(self.sem, value)

    def loop(self, lo, hi, per, body):
        base, k = self.n, self.k
        with self.eng.Fori(lo, hi) as i:
            self.n = base + (i - lo) * per
            body(i)
            assert self.k - k == per, (self.k - k, per)
        self.n = base + (hi - lo) * per


def plain_loop(eng, lo, hi, body):
    with eng.Fori(lo, hi) as i:
        body(i)


def held(eng, value):
    return value if isinstance(value, int) else eng.snap(value)


def wait_apart(eng, sem, value, there):
    if not isinstance(value, int):
        eng.compute_val(value)
        eng.wait_ge(*there)
    eng.wait_ge(sem, value)


def block_kernel(nc, x, ctx, ctx_t, quant_par, ident_in, ffn_w, kv_w, mask, norm_w, wq, wo,
                 router_w, router_b, moe_w, moe_b, moe_b3, tri_in, out):
    es = ExitStack()
    with es:
        arena = es.enter_context(nc.sbuf_tensor("arena", [P, 202 * 256], F32))

        def carve(kib, shape, dtype=F32):
            n = 1
            for s in shape:
                n *= s
            words = n if dtype == F32 else n // 2
            start = int(kib * 256)
            v = arena[:, start:start + words]
            if dtype != F32:
                v = v.bitcast(dtype)
            if len(shape) == 2:
                v = v.rearrange("p (a b) -> p a b", a=shape[0])
            if len(shape) == 3:
                v = v.rearrange("p (a b c) -> p a b c", a=shape[0], b=shape[1])
            return v

        xres = carve(0, (NT, D))
        xn = carve(8, (NT, D))
        xt = [carve(16, (KD, TOK), F16), carve(20, (KD, TOK), F16)]
        ct = [carve(24, (KD, KV), F16), carve(32, (KD, KV), F16)]
        kt = [carve(40, (HK, KV), F16), carve(56, (HK, KV), F16)]
        vv = [carve(72, (MT, HK * DH), F16), carve(88, (MT, HK * DH), F16)]
        ctx_t_raw = carve(88, (KD, KV))
        ctx_raw = carve(150, (MT, D))
        q2 = carve(166, (MT, D), BF16)
        q1 = carve(174, (NT, D), BF16)
        q1t = carve(178, (KD, TOK), BF16)
        wf = [carve(104, (WS, D), F16), carve(115, (WS, D), F16)]
        kw_raw = carve(126, (KD, D))
        kw = [carve(134, (2, KD * D), F16), carve(142, (2, KD * D), F16)]
        up = carve(150, (FT, TOK))
        gate = carve(172, (FT, TOK))
        og = [carve(150, (FT, TOK), F16), carve(161, (FT, TOK), F16)]
        raw = carve(194, (RAW, D))
        deq = carve(200, (1, D))
        sq0 = carve(182, (2, D))
        kn0 = carve(186, (1, D))
        vf = carve(24 - 16, (2, D))
        sig = carve(12, (2, TOK))
        aq_raw = carve(24, (1, KD * D))
        ao_raw = carve(32, (1, R * D))
        aq = [carve(104, (2, KD * D), F16), carve(112, (2, KD * D), F16)]
        ao = [carve(120, (2, R * D), F16), carve(128, (2, R * D), F16)]
        sc = carve(136, (R, SKV))
        pr = carve(144, (R, SKV))
        pt = [carve(152, (KD, R * P), F16), carve(156, (KD, R * P), F16)]
        sqa = carve(160, (1, D))
        qn = carve(162, (1, D))
        qt = [carve(164, (R, P), F16), carve(165, (R, P), F16)]
        ot = [carve(166, (R, P), F16), carve(167, (R, P), F16)]
        mk = carve(168, (2, SKV))
        me_raw = carve(172, (2, 3 * D))
        me = [carve(184, (2, 3 * D), F16), carve(190, (2, 3 * D), F16)]
        sg = carve(136, (2, TOK))
        hu = carve(140, (2, TOK))
        hv = carve(144, (2, TOK))
        ht = [carve(148, (2, TOK), F16), carve(150, (2, TOK), F16)]
        b3 = carve(152, (1, D))
        gt = carve(154, (1, TOK))
        rw_raw = carve(156, (KD, NE))
        rw = [carve(156.25, (KD, NE), F16), carve(156.375, (KD, NE), F16)]
        lg, score, masked = carve(156.5, (NT, NE)), carve(156.75, (NT, NE)), carve(157, (NT, NE))
        gmax, keep, kbig = carve(157.25, (NT, 4)), carve(157.5, (NT, 4)), carve(157.75, (NT, 4))
        lmax, lsum, linv = carve(158, (NT,)), carve(158.125, (NT,)), carve(158.25, (NT,))
        rank = carve(158.5, (NT, NE))
        gts, gsc = carve(158.75, (NT, EX)), carve(159.25, (NT, EX))
        tri = carve(168, (NE, NE))
        rbb = carve(169, (2, NE))
        rt_a = carve(160, (NT, NE * NE))
        rt_b = carve(164, (NT, NE * NE))

        def small(name, shape, dtype=F32):
            return es.enter_context(nc.sbuf_tensor(name, [P] + list(shape), dtype))

        ident = small("ident", [P])
        identb = small("identb", [P], BF16)
        onesf = small("onesf", [P])
        ones = small("ones", [P], BF16)
        nh = small("nh", [16])
        par = small("par", [4])
        pc = small("pc", [8])
        st6 = small("st6", [NT, 6])
        mv = small("mv", [NT, 2])
        ve = small("ve", [NT])
        rs = small("rs", [NT])
        rq = small("rq", [NT])
        rsum = small("rsum", [NT])
        mm2 = small("mm2", [2, FT])
        ext = small("ext", [2])
        row2 = small("row2", [4])
        aqp = small("aqp", [5, 8])
        dsc = small("dsc", [SC, 16])
        dsi = small("dsi", [SC, 16])
        ss = small("ss", [2, R])
        rk = small("rk", [2, R])
        nw = small("nw", [2])
        nws = small("nws", [2])
        mneg = small("mneg", [R])
        den = small("den", [R])
        rden = small("rden", [R])
        mb = small("mb", [2, EX])
        mbs = small("mbs", [2, EX])

        def one(v, i):
            return v[:, bass.ds(i, 1)].squeeze(1) if not isinstance(i, int) else v[:, i]

        def cols(v, a, n):
            return v[:, bass.ds(a, n)]

        ps = es.enter_context(nc.psum_tensor("ps", [P, 8, 512], F32))

        def bank(i):
            return one(ps, i)

        def quarters(v):
            return v.rearrange("p (a b) -> p a b", a=4)

        names = set()

        def sem(name):
            assert name not in names
            names.add(name)
            return es.enter_context(nc.semaphore(name))

        in_x, in_par, in_ctx, in_ctt = sem("in_x"), sem("in_par"), sem("in_ctx"), sem("in_ctt")
        in_raw, in_kw, in_mask, in_aq, in_ao = sem("in_raw"), sem("in_kw"), sem("in_mask"), sem("in_aq"), sem("in_ao")
        in_me, in_mp, stored = sem("in_me"), sem("in_mp"), sem("stored")
        own_v, own_a, own_g = sem("own_v"), sem("own_a"), sem("own_g")
        const_g, const_v = sem("const_g"), sem("const_v")
        var_ready, rstd_ready = sem("var_ready"), sem("rstd_ready")
        q1_ready, q1t_ps, q1t_ready = sem("q1_ready"), sem("q1t_ps"), sem("q1t_ready")
        q2_ready, col_ps, x1_ps, x1_done = sem("q2_ready"), sem("col_ps"), sem("x1_ps"), sem("x1_done")
        ext_ready, ext_t, row_ready, ext_b, ext_used = (sem("ext_ready"), sem("ext_t"), sem("row_ready"),
                                                        sem("ext_b"), sem("ext_used"))
        par_ready = sem("par_ready")
        xn_ready, xt_ps, xt_hi, xt_lo = sem("xn_ready"), sem("xt_ps"), sem("xt_hi"), sem("xt_lo")
        ct_hi, ct_lo, kw_sc, kw_hi, kw_lo = sem("ct_hi"), sem("ct_lo"), sem("kw_sc"), sem("kw_hi"), sem("kw_lo")
        k_ps, k_sq, k_ms, k_rs, k_nm, k_t, k_hi, k_lo = (sem("k_ps"), sem("k_sq"), sem("k_ms"), sem("k_rs"),
                                                         sem("k_nm"), sem("k_t"), sem("k_hi"), sem("k_lo"))
        v_ps, v_cp, v_lo = sem("v_ps"), sem("v_cp"), sem("v_lo")
        w_inv, w_div, w_rnd, w_deq, w_t, w_hi, w_lo = (sem("w_inv"), sem("w_div"), sem("w_rnd"), sem("w_deq"),
                                                       sem("w_t"), sem("w_hi"), sem("w_lo"))
        f_ps, f_cp, f_mm = sem("f_ps"), sem("f_cp"), sem("f_mm")
        u_y, u_dq = sem("u_y"), sem("u_dq")
        g_y, g_dq, s_y, s_cl, gs_done = sem("g_y"), sem("g_dq"), sem("s_y"), sem("s_cl"), sem("gs_done")
        p_y, p_done = sem("p_y"), sem("p_done")
        o_y, o_int, o_hi, o_lo, d_ps, x2_done = (sem("o_y"), sem("o_int"), sem("o_hi"), sem("o_lo"), sem("d_ps"),
                                                 sem("x2_done"))
        aw_sc, aw_hi, aw_lo = sem("aw_sc"), sem("aw_hi"), sem("aw_lo")
        a_q, a_sq, a_ms, a_rs, a_qn, a_qt, a_qh, a_ql = (sem("a_q"), sem("a_sq"), sem("a_ms"), sem("a_rs"),
                                                         sem("a_qn"), sem("a_qt"), sem("a_qh"), sem("a_ql"))
        a_s, a_sm, a_e, a_rd, a_p, a_pt, a_ph, a_pl = (sem("a_s"), sem("a_sm"), sem("a_e"), sem("a_rd"),
                                                       sem("a_p"), sem("a_pt"), sem("a_ph"), sem("a_pl"))
        a_o, a_oh, a_ol, a_y, a_x = sem("a_o"), sem("a_oh"), sem("a_ol"), sem("a_y"), sem("a_x")
        r_ws, r_ps, r_sub, r_exp, gates_ready, g_t, g_c = (sem("r_ws"), sem("r_ps"), sem("r_sub"), sem("r_exp"),
                                                           sem("gates_ready"), sem("g_t"), sem("g_c"))
        b3_ps, b3_x = sem("b3_ps"), sem("b3_x")
        m_sc, m_hi, m_lo, m_h, m_sg, m_u, m_v, m_hh, m_hl, m_y, m_x = (
            sem("m_sc"), sem("m_hi"), sem("m_lo"), sem("m_h"), sem("m_sg"), sem("m_u"), sem("m_v"), sem("m_hh"),
            sem("m_hl"), sem("m_y"), sem("m_x"))

        block = es.enter_context(nc.Block())

        def split_count(e, k):
            if isinstance(e, int) and e == 0:
                return k + 1
            if k == 2:
                return 3 * e + (5 if not (isinstance(e, int) and e == EX - 1) else 3)
            return 3 * e + k + (1 if isinstance(e, int) and e == 1 else 0)


        @block.sync
        def _(sp):
            sp.dma_start(xres, x).then_inc(in_x, 16)
            for t, s in ((par, quant_par), (ident, ident_in), (nw, norm_w)):
                sp.dma_start(t[:, :], s).then_inc(in_par, 16)
            sp.dma_start(ctx_raw, ctx).then_inc(in_ctx, 16)
            sp.dma_start(ctx_t_raw, ctx_t).then_inc(in_ctt, 16)

            def sp_wait(s, value):
                wait_apart(sp, s, value, (in_x, 16))

            def ring(n):
                if not isinstance(n, int) or n >= 1:
                    sp_wait(in_raw, n * 16)
                if not isinstance(n, int) or n >= RAW:
                    sp_wait(w_deq, n - RAW + 1)
                sp.dma_start(one(raw, n % RAW), one(ffn_w, n)).then_inc(in_raw, 16)

            def kw_load(c):
                if c >= 1:
                    sp.wait_ge(kw_lo, c)
                sp.dma_start(kw_raw, kv_w[c]).then_inc(in_kw, 16)

            kw_load(0)
            for n in range(RAW):
                ring(n)
            kw_load(1)
            kw_load(2)
            plain_loop(sp, RAW, NCH - FT, ring)
            kw_load(3)
            plain_loop(sp, NCH - FT, NCH, ring)
            sp.wait_ge(v_ps, 2 * MT)
            sp.dma_start(aq_raw[:, 0], wq[0]).then_inc(in_aq, 16)
            sp.dma_start(ao_raw[:, 0], wo[0]).then_inc(in_ao, 16)
            sp.wait_ge(d_ps, NT)
            sp.dma_start(mk, mask).then_inc(in_mask, 16)
            sp.dma_start(mb[:, :, :], moe_b).then_inc(in_mp, 16)

            def attention_weights(g):
                sp_wait(aw_lo, g * 8 - 4)
                sp.dma_start(aq_raw[:, 0], wq[bass.ds(g, 1)].squeeze(0)).then_inc(in_aq, 16)
                sp_wait(aw_lo, g * 8)
                sp.dma_start(ao_raw[:, 0], wo[bass.ds(g, 1)].squeeze(0)).then_inc(in_ao, 16)

            plain_loop(sp, 1, HK, attention_weights)
            for e in range(2):
                if e >= 1:
                    sp.wait_ge(in_me, 16 * e)
                sp.dma_start(me_raw[:, e], moe_w[e]).then_inc(in_me, 16)
            sp.wait_ge(a_x, H // R * NT)
            sp.dma_start(b3[0:NE + 1, 0], moe_b3).then_inc(in_mp, 16)
            sp.dma_start(rw_raw, router_w).then_inc(in_mp, 16)
            sp.dma_start(rbb, router_b).then_inc(in_mp, 16)
            sp.dma_start(tri, tri_in).then_inc(in_mp, 16)

            def expert_weights(e):
                sp_wait(in_me, e * 16)
                sp_wait(m_lo, split_count(e - 2, 2))
                sp.dma_start(one(me_raw, e % 2), moe_w[bass.ds(e, 1)].squeeze(0)).then_inc(in_me, 16)

            expert_weights(2)
            plain_loop(sp, 3, EX, expert_weights)
            for t in range(NT):
                sp.wait_ge(m_x, (EX - 1) * NT + t + 1)
                sp.dma_start(out[:, t], xres[:, t]).then_inc(stored, 16)
            sp.wait_ge(stored, 16 * NT)

        @block.gpsimd
        def _(g):
            own = Chain(g, own_g)
            g.memset(nh[:, :], -0.5).then_inc(const_g, 1)
            g.memset(ones[:, :], 1.0).then_inc(const_g, 1)
            g.wait_ge(const_g, 1)

            def rstd(k):
                g.wait_ge(var_ready, k + 1)
                g.tensor_tensor(rs[:, :], ve[:, :], nh[:, 0:NT], ALU.pow).then_inc(rstd_ready, 1)

            rstd(0)

            def kw_split(c):
                g.wait_ge(in_kw, 16 * (c + 1))
                v = kw_raw.rearrange("p a b -> p (a b)")
                if c >= 2:
                    g.wait_ge(k_ps, (c - 1) * MT)
                g.tensor_scalar(v, v, SW, 1.0, ALU.mult, ALU.mult).then_inc(kw_sc, 1)
                g.wait_ge(kw_hi, c + 1)
                g.tensor_tensor(kw[1][:, c % 2], v, kw[0][:, c % 2], ALU.subtract).then_inc(kw_lo, 1)

            kw_split(0)
            rstd(1)
            kw_split(1)

            def k_pow(u):
                g.wait_ge(k_ms, u + 1)
                if not isinstance(u, int) or u >= 2:
                    g.wait_ge(k_nm, u - 1)
                g.tensor_tensor(one(rk, u % 2), one(ss, u % 2), nh[:, 0:R], ALU.pow).then_inc(k_rs, 1)

            k_pow(0)
            k_pow(1)
            plain_loop(g, 2, 2 * MT, k_pow)

            def divide(n):
                g.wait_ge(w_inv, n + 1)
                v = one(raw, n % RAW).rearrange("p (a b) -> p a b", b=QB)
                s = one(dsi, n % SC).unsqueeze(2).broadcast_to([P, D // QB, QB])
                g.tensor_tensor(v, v, s, ALU.mult).then_inc(w_div, 1)

            def scale_back(n):
                g.wait_ge(w_rnd, n + 1)
                v = one(raw, n % RAW).rearrange("p (a b) -> p a b", b=QB)
                s = one(dsc, n % SC).unsqueeze(2).broadcast_to([P, D // QB, QB])
                if not isinstance(n, int) or n >= 1:
                    g.wait_ge(w_t, n)
                g.tensor_tensor(deq[:, 0].rearrange("p (a b) -> p a b", b=QB), v, s, ALU.mult).then_inc(w_deq, 1)

            def weights(lo, hi, extra=None):
                def turn(n):
                    divide(n + 1)
                    scale_back(n)
                    if extra and not (isinstance(n, int) and n == lo):
                        extra(n - lo - 1)
                divide(lo)
                turn(lo)
                plain_loop(g, lo + 1, hi - 1, turn)
                scale_back(hi - 1)
                if extra:
                    extra(hi - 2 - lo)
                    extra(hi - 1 - lo)

            weights(0, FT)
            weights(FT, 2 * FT)
            kw_split(2)

            def v_low(u):
                g.wait_ge(v_cp, u + 1)
                c, m = u // MT, u % MT
                g.tensor_tensor(cols(one(vv[1], m), c * D, D), one(vf, u % 2), cols(one(vv[0], m), c * D, D),
                                ALU.subtract).then_inc(v_lo, 1)

            kw_split(3)
            weights(2 * FT, NCH, v_low)
            plain_loop(g, FT, 2 * MT, v_low)

            rstd(2)

            def attention_split(g_, part, k):
                src = (aq_raw, ao_raw)[part][:, 0, k * D:(k + 1) * D]
                lo, hi = (cols(one(w, g_ % 2), k * D, D) for w in ((aq, ao)[part][1], (aq, ao)[part][0]))
                if k == 0:
                    wait_apart(g, (in_aq, in_ao)[part], (g_ + 1) * 16, (const_g, 2))
                g.tensor_scalar(src, src, SW, 1.0, ALU.mult, ALU.mult).then_inc(aw_sc, 1)
                g.wait_ge(aw_hi, g_ * 8 + part * 4 + k + 1)
                g.tensor_tensor(lo, src, hi, ALU.subtract).then_inc(aw_lo, 1)

            for part in range(2):
                for k in range(4):
                    attention_split(0, part, k)

            def q_pow(u):
                g.wait_ge(a_ms, u + 1)
                g.tensor_tensor(rk[:, 0], ss[:, 0], nh[:, 0:R], ALU.pow).then_inc(a_rs, 1)

            def attention_step(j, s):
                u = 4 * j + s
                for h in range(R):
                    wait_apart(g, a_rd, 4 * u + h + 1, (const_g, 2))
                    g.tensor_scalar(pr[:, h], pr[:, h], rden[:, h:h + 1], SP, ALU.mult, ALU.mult)\
                     .then_inc(a_p, 1)
                if not isinstance(j, int) or u + 1 < HK * NT:
                    q_pow(u + 1)
                if not isinstance(j, int):
                    for i in range(2):
                        attention_split(j + 1, (s - 1) // 2, 2 * ((s - 1) % 2) + i)

            q_pow(0)
            attention_step(0, 0)
            with g.Fori(0, HK - 1) as j:
                for s in range(1, 5):
                    attention_step(j, s)
            for s in range(1, 4):
                attention_step(HK - 1, s)

            def expert_split(e, q, k):
                if k == 0:
                    wait_apart(g, in_me, (e + 1) * 16, (const_g, 2))
                if not isinstance(e, int) or e >= 2:
                    if k == 0:
                        wait_apart(g, m_h, (e - 1) * 2, (const_g, 2))
                    if k == 2:
                        wait_apart(g, m_y, (e - 1) * NT, (const_g, 2))
                src = me_raw[:, q, k * D:(k + 1) * D]
                g.tensor_scalar(src, src, SW, 1.0, ALU.mult, ALU.mult).then_inc(m_sc, 1)
                g.wait_ge(m_hi, split_count(e, k))
                g.tensor_tensor(me[1][:, q, k * D:(k + 1) * D], src, me[0][:, q, k * D:(k + 1) * D],
                                ALU.subtract).then_inc(m_lo, 1)

            for k in range(3):
                expert_split(0, 0, k)
            rstd(3)
            expert_split(1, 1, 0)
            expert_split(1, 1, 1)

            def expert_turn(j):
                for s in range(2):
                    expert_split(2 * j + s, s, 0)
                    expert_split(2 * j + s, s, 1)
                    expert_split(2 * j + s - 1, 1 - s, 2)
            expert_turn(1)
            plain_loop(g, 2, EX // 2, expert_turn)
            expert_split(EX - 1, 1, 2)

        @block.scalar
        def _(a):
            def copy(out_, in_, scale=1.0, bias=0.0):
                return a.activation(out_, in_, ACT.Copy, scale=scale, bias=bias)

            a.wait_ge(in_ctt, 16)
            for k in range(KD):
                copy(ct[0][:, k], ctx_t_raw[:, k], SX).then_inc(ct_hi, 1)

            def kw_high(c):
                a.wait_ge(kw_sc, c + 1)
                copy(kw[0][:, c % 2], kw_raw.rearrange("p a b -> p (a b)")).then_inc(kw_hi, 1)

            kw_high(0)
            for k in range(KD):
                a.wait_ge(q1t_ps, k + 1)
                copy(q1t[:, k], bank(k).bitcast(BF16)[:, 0:TOK]).then_inc(q1t_ready, 1)
            kw_high(1)

            def hidden_high(n, scale):
                for k in range(KD):
                    a.wait_ge(xt_ps, KD * n + k + 1)
                    copy(xt[0][:, k], bank(k), scale).then_inc(xt_hi, 1)

            hidden_high(0, 1.0)

            def k_square(u):
                a.wait_ge(k_ps, u + 1)
                if not isinstance(u, int) or u >= 2:
                    a.wait_ge(k_ms, u - 1)
                a.activation(one(sq0, u % 2), bank(u % KB), ACT.Square).then_inc(k_sq, 1)

            def k_high(u):
                a.wait_ge(k_t, u + 1)
                c, m = u // MT, u % MT
                copy(kt[0][:, bass.ds(4 * c, 4), bass.ds(m * P, P)], quarters(bank(6)), nws[:, 1:2]).then_inc(k_hi, 1)

            a.wait_ge(const_v, 3)
            k_square(0)
            k_square(1)

            def k_turn(u):
                k_square(u + 2)
                k_high(u)
            k_turn(0)
            plain_loop(a, 1, 2 * MT - 2, k_turn)
            k_high(2 * MT - 2)
            k_high(2 * MT - 1)

            def weight_high(n, reused=True):
                a.wait_ge(w_t, n + 1)
                if reused:
                    a.wait_ge(f_ps, n - WS + 1)
                copy(one(wf[0], n % WS), bank(2), SW).then_inc(w_hi, 1)

            def tile_out(n, dst, scale):
                a.wait_ge(f_ps, n + 1)
                copy(one(dst, n % FT), bank(n % 2), scale).then_inc(f_cp, 1)

            sx4 = aqp[:, 0, 4:5]

            def up_turn(n):
                weight_high(n + 1, reused=False)
                tile_out(n, up, sx4)

            weight_high(0, reused=False)
            plain_loop(a, 0, FT - 1, up_turn)
            tile_out(FT - 1, up, sx4)

            def quantise(src, j, i, done):
                copy(one(src, i), one(src, i), aqp[:, j, 0:1], MAGIC).then_inc(done, 1)

            weight_high(FT)
            a.wait_ge(par_ready, 2)

            def gate_turn(n):
                weight_high(n + 1)
                tile_out(n, gate, sx4)
                quantise(up, 1, n - FT, u_y)
            plain_loop(a, FT, 2 * FT - 1, gate_turn)
            tile_out(2 * FT - 1, gate, sx4)
            quantise(up, 1, FT - 1, u_y)

            kw_high(2)

            def v_out(u):
                c, m = u // MT, u % MT
                a.wait_ge(v_ps, u + 1)
                copy(cols(one(vv[0], m), c * D, D), bank(4 + u % 2), 1.0 / SW)
                if not isinstance(u, int) or u >= 2:
                    a.wait_ge(v_lo, u - 1)
                copy(one(vf, u % 2), bank(4 + u % 2), 1.0 / SW).then_inc(v_cp, 1)

            kw_high(3)

            def down_turn(n):
                weight_high(n)
                v_out(n - 2 * FT)
            down_turn(2 * FT)
            down_turn(2 * FT + 1)
            plain_loop(a, 2 * FT + 2, NCH, down_turn)
            plain_loop(a, FT, 2 * MT, v_out)

            def gate_front(i):
                quantise(gate, 2, i, g_y)

            def gate_sigmoid(i):
                wait_apart(a, g_dq, i + 1, (in_ctt, 16))
                a.activation(one(sig, i % 2), one(gate, i), ACT.Sigmoid).then_inc(own_a, 1)
                wait_apart(a, own_a, i + 1, (in_ctt, 16))
                copy(one(sig, i % 2), one(sig, i % 2), 65536.0, MAGIC).then_inc(s_y, 1)

            a.wait_ge(par_ready, 3)
            gate_front(0)
            gate_front(1)
            gate_sigmoid(0)
            gate_front(2)
            gate_sigmoid(1)

            def gate_step(i):
                gate_front(i)
                a.wait_ge(gs_done, i - 2)
                gate_sigmoid(i - 1)
            plain_loop(a, 3, FT, gate_step)
            a.wait_ge(gs_done, FT - 2)
            gate_sigmoid(FT - 1)

            a.wait_ge(par_ready, 4)
            plain_loop(a, 0, FT, lambda i: quantise(gate, 3, i, p_y))
            a.wait_ge(par_ready, 5)

            def out_quant(i):
                quantise(gate, 4, i, o_y)

            def out_high(i):
                a.wait_ge(o_int, i + 1)
                copy(one(og[0], i), one(gate, i)).then_inc(o_hi, 1)
            out_quant(0)

            def out_turn(i):
                out_quant(i + 1)
                out_high(i)
            plain_loop(a, 0, FT - 1, out_turn)
            out_high(FT - 1)

            def attention_high(g_, part, k):
                n = g_ * 8 + part * 4 + k
                a.wait_ge(aw_sc, n + 1)
                copy(cols(one((aq, ao)[part][0], g_ % 2), k * D, D),
                     (aq_raw, ao_raw)[part][:, 0, k * D:(k + 1) * D]).then_inc(aw_hi, 1)

            for part in range(2):
                for k in range(4):
                    attention_high(0, part, k)
            hidden_high(1, SX)

            def q_square(u):
                a.wait_ge(a_q, u + 1)
                a.activation(sqa[:, 0], bank(4), ACT.Square).then_inc(a_sq, 1)

            def q_high(u):
                a.wait_ge(a_qt, u + 1)
                copy(qt[0], quarters(bank(5)), nws[:, 0:1]).then_inc(a_qh, 1)

            def o_high(u):
                a.wait_ge(a_o, u + 1)
                copy(ot[0], quarters(bank(6)), 1.0 / SP).then_inc(a_oh, 1)

            def attention_step(j, s):
                u = 4 * j + s
                for h in range(R):
                    a.wait_ge(a_sm, 4 * u + h + 1)
                    if h == 0 and not (isinstance(j, int) and u == 0):
                        a.wait_ge(a_pt, 4 * u)
                    a.activation(pr[:, h], sc[:, h], ACT.Exp, bias=mneg[:, h:h + 1], scale=-1.0,
                                 accum_out=den[:, h:h + 1]).then_inc(a_e, 1)
                more = not isinstance(j, int) or u + 1 < HK * NT
                if more:
                    q_square(u + 1)
                if not isinstance(j, int) or u >= 1:
                    o_high(u - 1)
                for h in range(R):
                    if more and h == R - 1:
                        q_high(u + 1)
                    a.wait_ge(a_pt, 4 * u + h + 1)
                    if h == 0 and (not isinstance(j, int) or u >= 1):
                        a.wait_ge(a_o, u)
                    copy(pt[0][:, :, h * P:(h + 1) * P], quarters(bank(h))).then_inc(a_ph, 1)
                if not isinstance(j, int):
                    for i in range(2):
                        attention_high(j + 1, (s - 1) // 2, 2 * ((s - 1) % 2) + i)

            q_square(0)
            q_high(0)
            attention_step(0, 0)
            with a.Fori(0, HK - 1) as j:
                for s in range(1, 5):
                    attention_step(j, s)
            for s in range(1, 4):
                attention_step(HK - 1, s)
            o_high(HK * NT - 1)

            def expert_high(e, q, k):
                a.wait_ge(m_sc, split_count(e, k))
                copy(me[0][:, q, k * D:(k + 1) * D], me_raw[:, q, k * D:(k + 1) * D]).then_inc(m_hi, 1)

            for k in range(3):
                expert_high(0, 0, k)
            hidden_high(2, SX)
            a.wait_ge(r_sub, 1)
            a.activation(lg, lg, ACT.Exp).then_inc(r_exp, 1)
            expert_high(1, 1, 0)
            expert_high(1, 1, 1)
            a.wait_ge(g_t, 1)
            copy(gt[0:NE + 1, 0], bank(5)[0:NE + 1, :]).then_inc(g_c, 1)

            def expert_step(j, s):
                e, q = 2 * j + s, s % 2
                a.wait_ge(m_h, 2 * e + 1)
                if not isinstance(j, int) or e >= 2:
                    a.wait_ge(m_u, e - 1)
                a.activation(sg[:, q], bank(2 * q), ACT.Sigmoid, bias=mb[:, 0, bass.ds(e, 1)], scale=1.0 / SXW).then_inc(m_sg, 1)
                a.wait_ge(m_v, e + 1)
                if not isinstance(j, int) or e >= 2:
                    a.wait_ge(m_y, (e - 1) * NT)
                copy(ht[0][:, q], hv[:, q], 2.0 ** -16).then_inc(m_hh, 1)
                if not isinstance(j, int) or e + 2 < EX:
                    expert_high(e + 2, q, 0)
                    expert_high(e + 2, q, 1)
                if not isinstance(j, int) or e + 1 < EX:
                    expert_high(e + 1, 1 - q, 2)

            expert_step(0, 0)
            expert_step(0, 1)
            with a.Fori(1, EX // 2 - 1) as j:
                for s in range(2):
                    expert_step(j, s)
            expert_step(EX // 2 - 1, 0)
            expert_step(EX // 2 - 1, 1)

        @block.tensor
        def _(pe):
            def product(out_, lhs, rhs, first, last):
                pe.matmul(out_, lhs[0], rhs[0], start=first, stop=False)
                pe.matmul(out_, lhs[0], rhs[1], start=False, stop=False)
                return pe.matmul(out_, lhs[1], rhs[0], start=False, stop=last)

            pe.wait_ge(const_v, 1)
            pe.wait_ge(q1_ready, 1)
            for k in range(KD):
                for t in range(NT):
                    mm = pe.transpose(bank(k).bitcast(BF16)[:, t * P:(t + 1) * P], q1[:, t, k * P:(k + 1) * P],
                                      identb[:, :])
                mm.then_inc(q1t_ps, 1)
            pe.wait_ge(const_g, 2)
            pe.wait_ge(q2_ready, 1)
            for b in range(B):
                for k in range(KD):
                    mm = pe.matmul(bank(6 + b), ones[:, :], q2[:, b * KD + k], start=k == 0, stop=k == KD - 1)
                mm.then_inc(col_ps, 1)
            pe.wait_ge(q1t_ready, KD)
            for t in range(NT):
                for k in range(KD):
                    mm = pe.matmul(bank((4, 5, 0, 1)[t]), q1t[:, k, t * P:(t + 1) * P], q2[:, t // 2 * KD + k],
                                   start=k == 0, stop=k == KD - 1)
                mm.then_inc(x1_ps, 1)

            def spread(k):
                pe.wait_ge(ext_ready, k + 1)
                pe.transpose(bank(7)[0:2, 0:P], ext[:, :], ident[:, :]).then_inc(ext_t, 1)
                pe.wait_ge(row_ready, k + 1)
                pe.matmul(bank(7)[:, P:P + 2], onesf[0:2, :], row2[0:2, 2:4], start=True, stop=True).then_inc(ext_b, 1)

            spread(0)

            def hidden_transposes(n):
                pe.wait_ge(xn_ready, n + 1)
                for k in range(KD):
                    for t in range(NT):
                        mm = pe.transpose(bank(k)[:, t * P:(t + 1) * P], xn[:, t, k * P:(k + 1) * P], ident[:, :])
                    mm.then_inc(xt_ps, 1)

            hidden_transposes(0)

            def kv_product(c, m, dst):
                for k in range(KD):
                    lhs = [cols(h[:, k], m * P, P) for h in ct]
                    rhs = [cols(one(h, c), k * D, D) for h in kw]
                    mm = product(dst, lhs, rhs, k == 0, k == KD - 1)
                return mm

            def k_unit(c, m):
                u = c * MT + m
                if m == 0:
                    pe.wait_ge(kw_lo, c + 1)
                if not isinstance(c, int) or u >= KB:
                    pe.wait_ge(k_nm, u - KB + 1)
                elif c == 0:
                    pe.wait_ge(xt_lo, m + 1)
                kv_product(c, m, bank(m % KB)).then_inc(k_ps, 1)

            def k_transposes(u):
                pe.wait_ge(k_nm, u + 1)
                if not isinstance(u, int) or u >= 1:
                    pe.wait_ge(k_lo, u)
                for h in range(4):
                    mm = pe.transpose(bank(6)[:, h * P:(h + 1) * P], kn0[:, 0, h * P:(h + 1) * P], ident[:, :])
                mm.then_inc(k_t, 1)

            units = [(c, m) for c in range(KW // 2) for m in range(MT)]
            for u, (c, m) in enumerate(units):
                k_unit(c, m)
                if u >= K_AHEAD:
                    k_transposes(u - K_AHEAD)
            for u in range(len(units) - K_AHEAD, len(units)):
                k_transposes(u)

            def weight_transposes(n):
                pe.wait_ge(w_deq, n + 1)
                if not isinstance(n, int) or n >= 1:
                    pe.wait_ge(w_lo, n)
                for k in range(4):
                    mm = pe.transpose(bank(2)[:, k * P:(k + 1) * P], deq[:, 0, k * P:(k + 1) * P],
                                      ident[:, :])
                mm.then_inc(w_t, 1)

            def tile(base, i, odd):
                n = base + i
                pe.wait_ge(w_lo, n + 1)
                if not isinstance(n, int) or n >= 2:
                    pe.wait_ge(f_cp, n - 1)
                for k in range(KD):
                    lhs = [cols(one(h, i), k * P, P) for h in wf]
                    mm = product(bank(odd), lhs, [h[:, k] for h in xt], k == 0, k == KD - 1)
                mm.then_inc(f_ps, 1)

            pe.wait_ge(xt_lo, KD)
            weight_transposes(0)

            def tiles(base):
                def step(i, odd):
                    weight_transposes(base + i + 1)
                    tile(base, i, odd)
                for i in range(2):
                    step(i, (base + i) % 2)
                with pe.Fori(1, FT // 2) as j:
                    for s in range(2):
                        step(2 * j + s, (base + s) % 2)
                tile(base, FT - 1, (base + FT - 1) % 2)

            assert FT % 2 == 1
            tiles(0)
            spread(1)
            weight_transposes(FT)
            tiles(FT)
            spread(2)

            def v_unit(c, m, odd):
                u = c * MT + m
                pe.wait_ge(kw_lo, KW // 2 + c + 1)
                if not isinstance(u, int) or u >= 2:
                    pe.wait_ge(v_cp, u - 1)
                kv_product(c, m, bank(4 + odd)).then_inc(v_ps, 1)

            def v_turn(c, m, odd):
                weight_transposes(2 * FT + c * MT + m)
                v_unit(c, m, odd)

            def by_two(c, lo, hi, turn):
                with pe.Fori(lo // 2, hi // 2) as j:
                    for s in range(2):
                        turn(c, 2 * j + s, s)

            for m in range(2):
                v_turn(0, m, m)
            by_two(0, 2, MT, v_turn)
            for m in range(FT - MT):
                v_turn(1, m, m % 2)
            v_unit(1, FT - MT, (FT - MT) % 2)
            by_two(1, FT - MT + 1, MT, v_unit)
            spread(3)
            spread(4)

            def down(i, first=False, last=False):
                pe.wait_ge(o_lo, i + 1)
                for t in range(NT):
                    lhs = [cols(one(h, i), t * P, P) for h in og]
                    mm = product(bank(t), lhs, [one(h, i) for h in wf], first, last)
                    if last:
                        mm.then_inc(d_ps, 1)
            pe.wait_ge(w_lo, NCH)
            down(0, first=True)
            plain_loop(pe, 1, FT - 1, down)
            down(FT - 1, last=True)

            hidden_transposes(1)

            def q_unit(j, s):
                u, par_ = 4 * j + s, (j + s // 4) % 2
                if s % 4 == 0:
                    pe.wait_ge(aw_lo, (j + s // 4) * 8 + 4)
                if not isinstance(j, int) or u >= 1:
                    pe.wait_ge(a_qn, u)
                t = s % 4
                for k in range(KD):
                    rhs = [cols(one(h, par_), k * D, D) for h in aq]
                    mm = product(bank(4), [h[:, k, t * P:(t + 1) * P] for h in xt], rhs, k == 0, k == KD - 1)
                mm.then_inc(a_q, 1)

            def q_transposes(u):
                pe.wait_ge(a_qn, u + 1)
                if not isinstance(u, int) or u >= 1:
                    pe.wait_ge(a_ql, u)
                for h in range(R):
                    mm = pe.transpose(bank(5)[:, h * P:(h + 1) * P], qn[:, 0, h * P:(h + 1) * P], ident[:, :])
                mm.then_inc(a_qt, 1)

            def scores(j, s):
                u, grp, b = 4 * j + s, j + s // 4, s % 4 // 2
                pe.wait_ge(a_ql, u + 1)
                for h in range(R):
                    if not isinstance(j, int) or u >= 1:
                        pe.wait_ge(a_pl, 4 * u - 3 + h)
                    rhs = [cols(one(w, grp), b * SKV, SKV) for w in kt]
                    product(bank(h), [w[:, h] for w in qt], rhs, True, True).then_inc(a_s, 1)

            def values(j, s):
                u, grp, b = 4 * j + s, j + s // 4, s % 4 // 2
                pe.wait_ge(a_pl, 4 * u + 4)
                if not isinstance(j, int) or u >= 1:
                    pe.wait_ge(a_ol, u)
                for k in range(KD):
                    lhs = [cols(w[:, b * KD + k], grp * DH, DH) for w in vv]
                    mm = product(bank(6), lhs, [w[:, k] for w in pt], k == 0, k == KD - 1)
                mm.then_inc(a_o, 1)

            def p_transposes(u):
                for h in range(R):
                    pe.wait_ge(a_p, 4 * u + h + 1)
                    for k in range(KD):
                        mm = pe.transpose(bank(h)[:, k * P:(k + 1) * P], pr[:, h, k * P:(k + 1) * P], ident[:, :])
                    mm.then_inc(a_pt, 1)

            def project(j, s):
                u, par_ = 4 * j + s, (j + s // 4) % 2
                if s % 4 == 0:
                    pe.wait_ge(aw_lo, (j + s // 4) * 8 + 8)
                pe.wait_ge(a_ol, u + 1)
                if not isinstance(j, int) or u >= 1:
                    pe.wait_ge(a_x, u)
                for h in range(R):
                    rhs = [cols(one(w, par_), h * D, D) for w in ao]
                    mm = product(bank(7), [w[:, h] for w in ot], rhs, h == 0, h == R - 1)
                mm.then_inc(a_y, 1)

            def attention_step(j, s):
                u = 4 * j + s
                more = not isinstance(j, int) or u + 1 < HK * NT
                scores(j, s)
                if more:
                    q_unit(j, s + 1)
                if not isinstance(j, int) or u >= 1:
                    values(j, s - 1)
                p_transposes(u)
                if more:
                    q_transposes(u + 1)
                if not isinstance(j, int) or u >= 1:
                    project(j, s - 1)

            pe.wait_ge(xt_lo, 2 * KD)
            q_unit(0, 0)
            q_transposes(0)
            attention_step(0, 0)
            with pe.Fori(0, HK - 1) as j:
                for s in range(1, 5):
                    attention_step(j, s)
            for s in range(1, 4):
                attention_step(HK - 1, s)
            values(HK - 1, 3)
            project(HK - 1, 3)

            hidden_transposes(2)
            pe.wait_ge(xt_lo, 3 * KD)
            pe.wait_ge(r_ws, 2)
            for t in range(NT):
                for k in range(KD):
                    for i in range(2):
                        for w in range(2):
                            mm = pe.matmul(bank(4)[:, t * NE:(t + 1) * NE], xt[i][:, k, t * P:(t + 1) * P], rw[w][:, k],
                                           start=k + i + w == 0, stop=k == KD - 1 and i + w == 2)
            mm.then_inc(r_ps, 1)

            def hidden(e, q):
                pe.wait_ge(m_lo, split_count(e, 1))
                if not isinstance(e, int) or e >= 2:
                    pe.wait_ge(m_v, e - 1)
                for i in range(2):
                    for k in range(KD):
                        lhs = [w[:, q, i * D + k * P:i * D + (k + 1) * P] for w in me]
                        mm = product(bank(2 * q + i), lhs, [h[:, k] for h in xt], k == 0, k == KD - 1)
                    mm.then_inc(m_h, 1)

            def experts_out(e, q):
                pe.wait_ge(m_hl, e + 1)
                pe.wait_ge(m_lo, split_count(e, 2))
                for t in range(NT):
                    if not isinstance(e, int) or e >= 1:
                        pe.wait_ge(m_x, (e - 1) * NT + t + 1)
                    product(bank(4 + t), [h[:, q, t * P:(t + 1) * P] for h in ht],
                            [w[:, q, 2 * D:3 * D] for w in me], True, True).then_inc(m_y, 1)

            hidden(0, 0)
            hidden(1, 1)
            pe.wait_ge(gates_ready, 1)
            for t in range(NT):
                mm = pe.transpose(bank(5)[0:NE + 1, t * P:(t + 1) * P], gts[:, t, 1:EX], ident[:, :])
            mm.then_inc(g_t, 1)
            pe.wait_ge(g_c, 1)
            for t in range(NT):
                pe.matmul(bank(4 + t), gt[0:NE + 1, 0, t * P:(t + 1) * P], b3[0:NE + 1, 0], start=True,
                          stop=True).then_inc(b3_ps, 1)
            pe.wait_ge(b3_x, NT)
            experts_out(0, 0)
            with pe.Fori(0, EX // 2 - 1) as j:
                for s in range(1, 3):
                    hidden(2 * j + s + 1, (s + 1) % 2)
                    experts_out(2 * j + s, s % 2)
            experts_out(EX - 1, 1)

        @block.vector
        def _(v):
            own = Chain(v, own_v)

            def tt(out_, x_, y_, op):
                return v.tensor_tensor(out_, x_, y_, op)

            def ts(out_, x_, s1, o1, s2=None, o2=ALU.bypass):
                return v.tensor_scalar(out_, x_, s1, s2, o1, o2)

            def stt(out_, x_, s_, y_, o1, o2):
                return v.scalar_tensor_tensor(out_, x_, s_, y_, o1, o2)

            def flat(w):
                return w.rearrange("p a b -> p (a b)")

            v.memset(onesf[:, :], 1.0).then_inc(const_v, 1)
            v.wait_ge(in_par, 48)
            v.tensor_copy(identb[:, :], ident[:, :]).then_inc(const_v, 1)
            own.mark(ts(nws[:, 0:1], nw[:, 0:1], SW / DH ** 0.5, ALU.mult))
            ts(nws[:, 1:2], nw[:, 1:2], SX, ALU.mult).then_inc(const_v, 1)
            inv1, inv2, w1, w2, s12, c1, c2, k1 = (pc[:, i:i + 1] for i in range(8))
            own.mark(v.reciprocal(pc[:, 0:2], par[:, 0:2]))
            own.mark(ts(pc[:, 2:4], par[:, 2:4], -1.0, ALU.mult, 128.0, ALU.add))
            own.link(tt(s12, par[:, 0:1], par[:, 1:2], ALU.mult))
            own.mark(tt(c1, s12, w1, ALU.mult))
            own.mark(tt(c2, s12, w2, ALU.mult))
            own.link(ts(k1, w1, float(D), ALU.mult))

            def norm_stats(k, t):
                own.link(v.bn_stats(st6[:, t], xres[:, t]))
                own.link(v.bn_aggr(mv[:, t], st6[:, t]))

            def norm_var():
                ts(ve[:, :], mv[:, :, 1], EPS, ALU.add).then_inc(var_ready, 1)

            v.wait_ge(in_x, 16)
            for t in range(NT):
                own.mark(v.bn_stats(st6[:, t], xres[:, t]))
            own.wait(own.n)
            for t in range(NT):
                own.mark(v.bn_aggr(mv[:, t], st6[:, t]))
            own.wait(own.n)
            norm_var()
            v.wait_ge(in_ctx, 16)
            own.link(ts(flat(ctx_raw), flat(ctx_raw), inv2, ALU.mult, par[:, 3:4], ALU.add))
            v.wait_ge(rstd_ready, 1)
            own.link(ts(rq[:, :], rs[:, :], inv1, ALU.mult))
            for t in range(NT):
                own.mark(ts(xn[:, t], xres[:, t], mv[:, t, 0:1], ALU.subtract, rq[:, t:t + 1], ALU.mult))
            own.wait(own.n)
            own.link(ts(flat(xn), flat(xn), par[:, 2:3], ALU.add, MAGIC, ALU.add))
            own.link(ts(flat(xn), flat(xn), MAGIC, ALU.max, MAGIC + 255.0, ALU.min))
            ts(flat(q1), flat(xn), MAGIC + 128.0, ALU.subtract).then_inc(q1_ready, 1)
            own.link(ts(flat(ctx_raw), flat(ctx_raw), MAGIC, ALU.add, MAGIC, ALU.max))
            ts(flat(q2), flat(ctx_raw), MAGIC + 255.0, ALU.min, MAGIC + 128.0, ALU.subtract).then_inc(q2_ready, 1)
            v.wait_ge(q1_ready, 1)
            own.link(v.tensor_reduce(rsum[:, :], q1, AX.X, ALU.add))
            own.link(ts(rsum[:, :], rsum[:, :], k1, ALU.add, c2, ALU.mult))
            for t in range(NT):
                v.wait_ge(col_ps, t // 2 + 1)
                own.link(stt(xres[:, t], bank(6 + t // 2), c1, xres[:, t], ALU.mult, ALU.add))
                own.link(ts(xres[:, t], xres[:, t], rsum[:, t:t + 1], ALU.add))

            for k in range(KD):
                v.wait_ge(ct_hi, k + 1)
                stt(ct[1][:, k], ctx_t_raw[:, k], SX, ct[0][:, k], ALU.mult, ALU.subtract).then_inc(ct_lo, 1)

            for t in range(NT):
                v.wait_ge(x1_ps, t + 1)
                own.link(stt(xres[:, t], bank((4, 5, 0, 1)[t]), s12, xres[:, t], ALU.mult, ALU.add))
                own.link(v.bn_stats(st6[:, t], xres[:, t]))
                own.link(v.bn_aggr(mv[:, t], st6[:, t]))
            norm_var()

            def normalise(k):
                v.wait_ge(rstd_ready, k + 1)
                for t in range(NT):
                    i = ts(xn[:, t], xres[:, t], mv[:, t, 0:1], ALU.subtract, rs[:, t:t + 1], ALU.mult)
                    if k != 1 and t == NT - 1:
                        i.then_inc(xn_ready, 1)
                    else:
                        own.mark(i)

            normalise(1)
            own.wait(own.n)

            def extrema(src, col):
                own.mark(v.tensor_reduce(mm2[:, 0, bass.ds(col, 1)], src, AX.X, ALU.max))
                own.mark(v.tensor_reduce(mm2[:, 1, bass.ds(col, 1)], src, AX.X, ALU.min, negate=True))

            for t in range(NT):
                extrema(xn[:, t], t)
            own.wait(own.n)

            def parameters(k, n, factor):
                v.tensor_reduce(ext[:, :], mm2[:, :, 0:n], AX.X, ALU.max).then_inc(ext_ready, 1)
                v.wait_ge(ext_t, k + 1)
                own.link(v.tensor_reduce(row2[0:2, 0:1], bank(7)[0:2, 0:P], AX.X, ALU.max))
                ts(row2[0:2, 2:4], ident[0:2, 0:2], row2[0:2, 0:1], ALU.mult).then_inc(row_ready, 1)
                v.wait_ge(ext_b, k + 1)
                yinv, lo, hi, s, s4, inv, z = (aqp[:, k, i:i + 1] for i in range(7))
                own.link(ts(ext[:, :], bank(7)[:, P:P + 2], 0.0, ALU.max, factor, ALU.mult))
                own.link(tt(s, ext[:, 0:1], ext[:, 1:2], ALU.add))
                own.link(ts(s, s, 1.0 / QMAX, ALU.mult, TINY, ALU.max))
                own.link(v.reciprocal(inv, s))
                own.mark(ts(s4, s, 4.0, ALU.mult))
                own.mark(ts(yinv, inv, factor, ALU.mult))
                own.link(ts(z, ext[:, 1:2], inv, ALU.mult, MAGIC, ALU.add))
                own.link(ts(z, z, MAGIC + QMAX, ALU.min, MAGIC, ALU.subtract))
                own.link(ts(lo, z, -1.0, ALU.mult, MAGIC, ALU.add))
                ts(hi, lo, QMAX, ALU.add).then_inc(par_ready, 1)
                v.wait_ge(par_ready, k + 1)

            def clip(dst, k):
                return ts(dst, dst, aqp[:, k, 1:2], ALU.max, aqp[:, k, 2:3], ALU.min)

            parameters(0, NT, 1.0)
            own.link(ts(flat(xn), flat(xn), aqp[:, 0, 0:1], ALU.mult, MAGIC, ALU.add))
            own.link(clip(flat(xn), 0))
            ts(flat(xn), flat(xn), MAGIC, ALU.subtract, SINT, ALU.mult).then_inc(xn_ready, 1)

            def hidden_low(n, scale):
                for k in range(KD):
                    v.wait_ge(xt_hi, KD * n + k + 1)
                    stt(xt[1][:, k], bank(k), scale, xt[0][:, k], ALU.mult, ALU.subtract).then_inc(xt_lo, 1)

            hidden_low(0, 1.0)

            def k_mean(u):
                v.wait_ge(k_sq, u + 1)
                ms = one(ss, u % 2)
                own.link(v.tensor_reduce(ms, quarters(one(sq0, u % 2)), AX.X, ALU.add))
                ts(ms, ms, 1.0 / DH, ALU.mult, EPS * SXW * SXW, ALU.add).then_inc(k_ms, 1)

            def k_norm(u):
                v.wait_ge(k_rs, u + 1)
                if not isinstance(u, int) or u >= 1:
                    v.wait_ge(k_t, u)
                tt(quarters(kn0[:, 0]), quarters(bank(u % KB)), one(rk, u % 2).unsqueeze(2).broadcast_to([P, R, DH]),
                   ALU.mult).then_inc(k_nm, 1)

            def k_low(u):
                c, m = u // MT, u % MT
                v.wait_ge(k_hi, u + 1)
                dst = [w[:, bass.ds(4 * c, 4), bass.ds(m * P, P)] for w in kt]
                stt(dst[1], quarters(bank(6)), nws[:, 1:2], dst[0], ALU.mult, ALU.subtract).then_inc(k_lo, 1)

            def k_turn(u):
                k_mean(u + 2)
                k_norm(u + 1)
                k_low(u)
            k_mean(0)
            k_mean(1)
            k_norm(0)
            k_turn(0)
            own.loop(1, 2 * MT - 2, 1, k_turn)
            k_norm(2 * MT - 1)
            k_low(2 * MT - 2)
            k_low(2 * MT - 1)

            def block_scales(n):
                v.wait_ge(in_raw, 16 * (n + 1))
                s, i = one(dsc, n % SC), one(dsi, n % SC)
                src = one(raw, n % RAW).rearrange("p (a b) -> p a b", b=QB)
                own.link(v.tensor_reduce(s, src, AX.X, ALU.max, apply_absolute_value=True))
                own.link(ts(s, s, 1.0 / 7.0, ALU.mult, TINY, ALU.max))
                v.reciprocal(i, s).then_inc(w_inv, 1)

            def round_weights(n):
                v.wait_ge(w_div, n + 1)
                w = one(raw, n % RAW)
                own.link(ts(w, w, 7.0, ALU.min, -8.0, ALU.max))
                ts(w, w, MAGIC, ALU.add, MAGIC, ALU.subtract).then_inc(w_rnd, 1)

            def weight_low(n):
                v.wait_ge(w_hi, n + 1)
                stt(one(wf[1], n % WS), bank(2), SW, one(wf[0], n % WS), ALU.mult, ALU.subtract).then_inc(w_lo, 1)

            def weights(lo, hi, after=None, per=0):
                block_scales(lo)
                block_scales(lo + 1)
                round_weights(lo)

                block_scales(lo + 2)
                round_weights(lo + 1)
                weight_low(lo)

                def turn(n):
                    block_scales(n + 2)
                    round_weights(n + 1)
                    weight_low(n)
                    if after:
                        after(n - 1)
                own.loop(lo + 1, hi - 2, 3 + per, turn)
                round_weights(hi - 1)
                weight_low(hi - 2)
                if after:
                    after(hi - 3)
                weight_low(hi - 1)
                if after:
                    after(hi - 2)
                    after(hi - 1)

            def tile_extrema(src):
                def after(n):
                    v.wait_ge(f_cp, n + 1)
                    extrema(one(src, n % FT), n % FT)
                return after

            weights(0, FT, after=tile_extrema(up), per=2)
            own.wait(own.n)
            parameters(1, FT, 1.0)

            def dequantise(dst, k, i, ready, done):
                v.wait_ge(ready, i + 1)
                own.link(clip(one(dst, i), k))
                ts(one(dst, i), one(dst, i), MAGIC, ALU.subtract, aqp[:, k, 3:4], ALU.mult).then_inc(done, 1)

            def gate_after(n):
                tile_extrema(gate)(n)
                dequantise(up, 1, n - FT, u_y, u_dq)
            weights(FT, 2 * FT, after=gate_after, per=3)
            own.wait(own.n)
            parameters(2, FT, 1.0)
            weights(2 * FT, NCH)

            def gate_front(i):
                dequantise(gate, 2, i, g_y, g_dq)

            def gate_back(i):
                v.wait_ge(s_y, i + 1)
                sg_, gt_ = one(sig, i % 2), one(gate, i)
                own.link(ts(sg_, sg_, MAGIC, ALU.max, MAGIC + QMAX, ALU.min))
                own.link(stt(gt_, sg_, MAGIC, gt_, ALU.subtract, ALU.mult))
                extrema(gt_, i)

            def gate_turn(i):
                gate_front(i)
                v.wait_ge(s_y, i)
                sg_, gt_ = one(sig, (i - 1) % 2), one(gate, i - 1)
                own.link(ts(sg_, sg_, MAGIC, ALU.max, MAGIC + QMAX, ALU.min))
                stt(gt_, sg_, MAGIC, gt_, ALU.subtract, ALU.mult).then_inc(gs_done, 1)
                v.wait_ge(gs_done, i)
                extrema(gt_, i - 1)

            gate_front(0)
            own.loop(1, FT, 4, gate_turn)
            v.wait_ge(s_y, FT)
            sg_, gt_ = sig[:, (FT - 1) % 2], gate[:, FT - 1]
            own.link(ts(sg_, sg_, MAGIC, ALU.max, MAGIC + QMAX, ALU.min))
            stt(gt_, sg_, MAGIC, gt_, ALU.subtract, ALU.mult).then_inc(gs_done, 1)
            v.wait_ge(gs_done, FT)
            extrema(gt_, FT - 1)
            own.wait(own.n)
            parameters(3, FT, 2.0 ** -16)

            def times_up(i):
                v.wait_ge(p_y, i + 1)
                own.link(clip(one(gate, i), 3))
                own.link(stt(one(gate, i), one(gate, i), MAGIC, one(up, i), ALU.subtract, ALU.mult))
                extrema(one(gate, i), i)
            own.loop(0, FT, 4, times_up)
            own.wait(own.n)
            parameters(4, FT, aqp[:, 3, 3:4])

            def out_int(i):
                v.wait_ge(o_y, i + 1)
                own.link(clip(one(gate, i), 4))
                ts(one(gate, i), one(gate, i), MAGIC, ALU.subtract, SINT, ALU.mult).then_inc(o_int, 1)

            def out_low(i):
                v.wait_ge(o_hi, i + 1)
                tt(one(og[1], i), one(gate, i), one(og[0], i), ALU.subtract).then_inc(o_lo, 1)

            out_int(0)

            def out_turn(i):
                out_int(i + 1)
                out_low(i)
            own.loop(0, FT - 1, 1, out_turn)
            out_low(FT - 1)

            for t in range(NT):
                v.wait_ge(d_ps, t + 1)
                own.link(stt(xres[:, t], bank(t), aqp[:, 4, 4:5], xres[:, t], ALU.mult, ALU.add))
                own.link(v.bn_stats(st6[:, t], xres[:, t]))
                own.link(v.bn_aggr(mv[:, t], st6[:, t]))
            norm_var()
            normalise(2)
            hidden_low(1, SX)

            v.wait_ge(in_mask, 16)
            own.link(ts(flat(mk), flat(mk), SXW, ALU.mult))

            def q_mean(u):
                v.wait_ge(a_sq, u + 1)
                own.link(v.tensor_reduce(ss[:, 0], quarters(sqa[:, 0]), AX.X, ALU.add))
                ts(ss[:, 0], ss[:, 0], 1.0 / DH, ALU.mult, EPS * SXW * SXW, ALU.add).then_inc(a_ms, 1)

            def q_norm(u):
                v.wait_ge(a_rs, u + 1)
                if not isinstance(u, int) or u >= 1:
                    v.wait_ge(a_qt, u)
                tt(quarters(qn[:, 0]), quarters(bank(4)), rk[:, 0].unsqueeze(2).broadcast_to([P, R, DH]),
                   ALU.mult).then_inc(a_qn, 1)

            def q_low(u):
                v.wait_ge(a_qh, u + 1)
                stt(qt[1], quarters(bank(5)), nws[:, 0:1], qt[0], ALU.mult, ALU.subtract).then_inc(a_ql, 1)

            def o_low(u):
                v.wait_ge(a_oh, u + 1)
                stt(ot[1], quarters(bank(6)), 1.0 / SP, ot[0], ALU.mult, ALU.subtract).then_inc(a_ol, 1)

            def add_out(j, s):
                t = s % 4
                v.wait_ge(a_y, 4 * j + s + 1)
                stt(xres[:, t], bank(7), 1.0 / SXW, xres[:, t], ALU.mult, ALU.add).then_inc(a_x, 1)

            def attention_step(j, s):
                u, t = 4 * j + s, s % 4
                more = not isinstance(j, int) or u + 1 < HK * NT
                for h in range(R):
                    if not isinstance(j, int) or u >= 1:
                        v.wait_ge(a_e, 4 * u - 3 + h)
                    wait_apart(v, a_s, 4 * u + h + 1, (in_mask, 16))
                    v.tensor_tensor_reduce(sc[:, h], bank(h), mk[:, t % 2], -1.0 / SXW, 3.0e38, ALU.add, ALU.min,
                                           mneg[:, h:h + 1]).then_inc(a_sm, 1)
                for h in range(R):
                    v.wait_ge(a_e, 4 * u + h + 1)
                    if h == 0 and (not isinstance(j, int) or u >= 1):
                        v.wait_ge(a_p, 4 * u)
                    v.reciprocal(rden[:, h:h + 1], den[:, h:h + 1]).then_inc(a_rd, 1)
                if more:
                    q_mean(u + 1)
                if not isinstance(j, int) or u >= 1:
                    o_low(u - 1)
                if more:
                    q_norm(u + 1)
                for h in range(R):
                    if more and h == R - 1:
                        q_low(u + 1)
                    v.wait_ge(a_ph, 4 * u + h + 1)
                    tt(pt[1][:, :, h * P:(h + 1) * P], quarters(bank(h)), pt[0][:, :, h * P:(h + 1) * P],
                       ALU.subtract).then_inc(a_pl, 1)
                if not isinstance(j, int) or u >= 1:
                    add_out(j, s - 1)

            q_mean(0)
            q_norm(0)
            q_low(0)
            attention_step(0, 0)

            def four_steps(j):
                for s in range(1, 5):
                    attention_step(j, s)
            own.loop(0, HK - 1, 4, four_steps)
            for s in range(1, 4):
                attention_step(HK - 1, s)
            o_low(HK * NT - 1)
            add_out(HK - 1, 3)
            v.wait_ge(a_x, HK * NT)

            for t in range(NT):
                own.mark(v.bn_stats(st6[:, t], xres[:, t]))
            own.wait(own.n)
            for t in range(NT):
                own.mark(v.bn_aggr(mv[:, t], st6[:, t]))
            own.wait(own.n)
            norm_var()
            v.wait_ge(in_mp, 16 * 5)
            own.mark(ts(flat(mbs[:, :, :]), flat(mb[:, :, :]), SXW, ALU.mult))
            own.link(ts(flat(rw_raw), flat(rw_raw), SW, ALU.mult))
            v.tensor_copy(flat(rw[0]), flat(rw_raw)).then_inc(r_ws, 1)
            v.wait_ge(r_ws, 1)
            tt(flat(rw[1]), flat(rw_raw), flat(rw[0]), ALU.subtract).then_inc(r_ws, 1)
            normalise(3)
            hidden_low(2, SX)

            def over(w, n):
                return w.unsqueeze(2).broadcast_to([P, NT, n])

            rb, rbias = (rbb[:, i].unsqueeze(1).broadcast_to([P, NT, NE]) for i in range(2))
            v.wait_ge(r_ps, 1)
            own.link(stt(lg, bank(4)[:, 0:NT * NE].rearrange("p (a b) -> p a b", a=NT), 1.0 / SXW, rb, ALU.mult, ALU.add))
            own.link(v.tensor_reduce(lmax, lg, AX.X, ALU.max))
            tt(lg, lg, over(lmax, NE), ALU.subtract).then_inc(r_sub, 1)
            v.wait_ge(r_exp, 1)
            own.link(v.tensor_reduce(lsum, lg, AX.X, ALU.add))
            own.link(v.reciprocal(linv, lsum))
            own.link(tt(score, lg, over(linv, NE), ALU.mult))
            own.link(tt(score, score, rbias, ALU.add))

            def ranks(dst, src, n):
                ra, rb_ = (w[:, :, 0:n * n].rearrange("p t (a b) -> p t a b", a=n) for w in (rt_a, rt_b))
                mine = src.unsqueeze(3).broadcast_to([P, NT, n, n])
                other = src.unsqueeze(2).broadcast_to([P, NT, n, n])
                low = tri[:, 0:n, 0:n].unsqueeze(1).broadcast_to([P, NT, n, n])
                own.mark(tt(ra, other, mine, ALU.is_gt))
                own.link(tt(rb_, other, mine, ALU.is_equal))
                own.link(tt(rb_, rb_, low, ALU.mult))
                own.link(tt(ra, ra, rb_, ALU.add))
                own.link(v.tensor_reduce(dst, ra, AX.X, ALU.add))

            own.link(v.tensor_reduce(flat(gmax), flat(score).rearrange("p (a b) -> p a b", b=4), AX.X, ALU.max))
            ranks(keep, gmax, 4)
            own.link(ts(keep, keep, 2.0, ALU.is_lt))
            own.link(ts(kbig, keep, -1.0, ALU.add, 1.0e30, ALU.mult))

            def groups(w):
                return flat(w).rearrange("p (a b) -> p a b", b=4)

            def spread4(w):
                return flat(w).unsqueeze(2).broadcast_to([P, NT * 4, 4])

            own.link(tt(groups(masked), groups(score), spread4(keep), ALU.mult))
            own.link(tt(groups(masked), groups(masked), spread4(kbig), ALU.add))
            ranks(rank, masked, NE)
            own.link(ts(rank, rank, 2.0, ALU.is_lt))
            own.mark(v.memset(gts[:, :, 0:NS], 1.0))
            own.link(tt(gts[:, :, NS:EX], score, rank, ALU.mult))
            ts(gsc, gts, 1.0 / SXW, ALU.mult).then_inc(gates_ready, 1)
            for t in range(NT):
                v.wait_ge(b3_ps, t + 1)
                stt(xres[:, t], bank(4 + t), 1.0, xres[:, t], ALU.mult, ALU.add).then_inc(b3_x, 1)

            def expert_step(j, s):
                e, q = 2 * j + s, s % 2
                v.wait_ge(m_sg, e + 1)
                stt(hu[:, q], bank(2 * q), mbs[:, 0, bass.ds(e, 1)], sg[:, q], ALU.add, ALU.mult).then_inc(m_u, 1)
                v.wait_ge(m_u, e + 1)
                v.wait_ge(m_h, 2 * e + 2)
                stt(hv[:, q], bank(2 * q + 1), mbs[:, 1, bass.ds(e, 1)], hu[:, q], ALU.add, ALU.mult).then_inc(m_v, 1)
                v.wait_ge(m_hh, e + 1)
                stt(ht[1][:, q], hv[:, q], 2.0 ** -16, ht[0][:, q], ALU.mult, ALU.subtract).then_inc(m_hl, 1)

            def expert_add(j, s):
                e = 2 * j + s
                for t in range(NT):
                    v.wait_ge(m_y, e * NT + t + 1)
                    stt(xres[:, t], bank(4 + t), gsc[:, t, bass.ds(e, 1)], xres[:, t], ALU.mult, ALU.add)\
                        .then_inc(m_x, 1)

            v.wait_ge(b3_x, NT)
            expert_step(0, 0)
            with v.Fori(0, EX // 2 - 1) as j:
                for s in range(1, 3):
                    expert_step(j, s)
                    expert_add(j, s - 1)
            expert_step(EX // 2 - 1, 1)
            expert_add(EX // 2 - 1, 0)
            expert_add(EX // 2 - 1, 1)


def kernel(**inputs):
    import numpy as np
    import concourse.bacc as bacc
    from concourse.bass_utils import run_bass_kernel_spmd

    get = {k: np.asarray(a) for k, a in inputs.items()}

    def rows(a, n):
        return a.reshape(n, P, -1).transpose(1, 0, 2)

    def every(a):
        return np.broadcast_to(a, (P,) + a.shape)

    x = rows(get["x"].reshape(TOK, D), NT)
    ctx = rows(get["ctx_4096"].reshape(KV, D), MT)
    ctx_t = rows(get["ctx_4096"].reshape(KV, D).T, KD)
    quant_par = every(np.concatenate([get["L0_xattn_x1_scale"], get["L0_xattn_x2_scale"],
                                      get["L0_xattn_x1_zp"], get["L0_xattn_x2_zp"]]))
    ident = np.eye(P, dtype=np.float32)
    ffn = np.zeros((NCH * P, D), np.float32)
    ffn[0:F] = get["L0_ffn_w_up"]
    ffn[FT * P:FT * P + F] = get["L0_ffn_w_gate"]
    down = np.zeros((D, FT * P), np.float32)
    down[:, 0:F] = get["L0_ffn_w_down"]
    ffn[2 * FT * P:] = down.reshape(KD, P, FT, P).transpose(2, 1, 0, 3).reshape(FT * P, D)
    ffn_w = ffn.reshape(NCH, P, D).transpose(1, 0, 2)
    kv = np.concatenate([get["L1_xattn_k_proj_w"], get["L1_xattn_v_proj_w"]]).T
    kv_w = kv.reshape(KD, P, 4, D).transpose(2, 1, 0, 3)
    mask = rows(get["mask_1x1xSxS2_ff0"].reshape(SQ, SKV), 2)
    norm_w = np.stack([get["L1_xattn_q_norm_w"], get["L1_xattn_k_norm_w"]], 1)
    wq = get["L1_xattn_q_proj_w"].T.reshape(KD, P, HK, R * DH).transpose(2, 1, 0, 3).reshape(HK, P, KD * D)
    wo = get["L1_xattn_o_proj_w"].T.reshape(HK, R, P, D).transpose(0, 2, 1, 3).reshape(HK, P, R * D)
    router_w = rows(get["L1_ffn_router_w"], KD)
    router_b = every(np.stack([get["L1_ffn_router_b"], get["L1_ffn_router_bias"]]))

    def first(shared, experts):
        return np.concatenate([shared.reshape(D, NS, INTER).transpose(1, 0, 2), experts])

    w1 = first(get["L1_ffn_sw1"], get["L1_ffn_ew1"]).reshape(EX, KD, P, INTER).transpose(0, 2, 1, 3)
    w2 = first(get["L1_ffn_sw2"], get["L1_ffn_ew2"]).reshape(EX, KD, P, INTER).transpose(0, 2, 1, 3)
    w3 = np.concatenate([get["L1_ffn_sw3"].reshape(NS, INTER, D), get["L1_ffn_ew3"]])
    moe_w = np.concatenate([w1.reshape(EX, P, D), w2.reshape(EX, P, D), w3], 2)
    moe_b = np.stack([np.concatenate([get["L1_ffn_sb1"].reshape(NS, INTER), get["L1_ffn_eb1"]]).T,
                      np.concatenate([get["L1_ffn_sb2"].reshape(NS, INTER), get["L1_ffn_eb2"]]).T], 1)
    moe_b3 = np.concatenate([get["L1_ffn_sb3"][None], get["L1_ffn_eb3"]])
    tri = every(np.tril(np.ones((NE, NE), np.float32), -1))

    given = dict(x=x, ctx=ctx, ctx_t=ctx_t, quant_par=quant_par, ident_in=ident, ffn_w=ffn_w, kv_w=kv_w,
                 mask=mask, norm_w=norm_w, wq=wq, wo=wo, router_w=router_w, router_b=router_b, moe_w=moe_w,
                 moe_b=moe_b, moe_b3=moe_b3, tri_in=tri)
    nc = bacc.Bacc("TRN2", target_bir_lowering=False, num_devices=1)
    arrays, args = {}, {}
    for name, a in given.items():
        a = np.ascontiguousarray(a)
        arrays[f"in_{name}"] = a
        args[name] = nc.dram_tensor(f"in_{name}", a.shape, mybir.dt.from_np(a.dtype), kind="ExternalInput").ap()
    out = nc.dram_tensor("out_x", (P, NT, D), F32, kind="ExternalOutput").ap()
    block_kernel(nc, out=out, **args)
    r = run_bass_kernel_spmd(nc, [arrays], core_ids=[0])
    return r.results[0]["out_x"].transpose(1, 0, 2).reshape(B, SQ, D)
```

```python
import concourse.bass as bass
from concourse import mybir
from contextlib import ExitStack

F32 = mybir.dt.float32
F16 = mybir.dt.float16
BF16 = mybir.dt.bfloat16
ALU = mybir.AluOpType
ACT = mybir.ActivationFunctionType
AX = mybir.AxisListType

P = 128
B, SQ, D = 2, 256, 512
SKV = 512
TOK, KV = B * SQ, B * SKV
NT = TOK // P
KD = D // P
MT = KV // P
F = 1376
FT = (F + P - 1) // P
QB = 32
NCH = 3 * FT
H, HK, DH = 32, 8, 128
R = H // HK
NE, NS, INTER = 16, 2, 128
EX = NE + NS
EPS = 1e-5
MAGIC = 12582912.0
QMAX = 65535.0
TINY = 1e-12

SX = 16.0
SW = 64.0
SXW = SX * SW
SINT = 2.0 ** -8
SP = 1024.0

RAW = 3
K_AHEAD = 3
KB = 4
KW = 4
WS = FT
ER = 3
SC = 4


class Chain:

    def __init__(self, eng, sem):
        self.eng, self.sem, self.n, self.k = eng, sem, 0, 0

    def mark(self, ins):
        ins.then_inc(self.sem, 1)
        self.n, self.k = self.n + 1, self.k + 1
        return self.n

    def link(self, ins):
        self.eng.wait_ge(self.sem, self.mark(ins))

    def wait(self, value):
        self.eng.wait_ge(self.sem, value)

    def loop(self, lo, hi, per, body):
        base, k = self.n, self.k
        with self.eng.Fori(lo, hi) as i:
            self.n = base + (i - lo) * per
            body(i)
            assert self.k - k == per, (self.k - k, per)
        self.n = base + (hi - lo) * per


def plain_loop(eng, lo, hi, body):
    with eng.Fori(lo, hi) as i:
        body(i)


def held(eng, value):
    return value if isinstance(value, int) else eng.snap(value)


def wait_apart(eng, sem, value, there):
    if not isinstance(value, int):
        eng.compute_val(value)
        eng.wait_ge(*there)
    eng.wait_ge(sem, value)


def block_kernel(nc, x, ctx, ctx_t, quant_par, ident_in, ffn_w, kv_w, mask, norm_w, wq, wo,
                 router_w, router_b, moe_w, moe_b, moe_b3, tri_in, out):
    es = ExitStack()
    with es:
        arena = es.enter_context(nc.sbuf_tensor("arena", [P, 202 * 256], F32))

        def carve(kib, shape, dtype=F32):
            n = 1
            for s in shape:
                n *= s
            words = n if dtype == F32 else n // 2
            start = int(kib * 256)
            v = arena[:, start:start + words]
            if dtype != F32:
                v = v.bitcast(dtype)
            if len(shape) == 2:
                v = v.rearrange("p (a b) -> p a b", a=shape[0])
            if len(shape) == 3:
                v = v.rearrange("p (a b c) -> p a b c", a=shape[0], b=shape[1])
            return v

        xres = carve(0, (NT, D))
        xn = carve(8, (NT, D))
        xt = [carve(16, (KD, TOK), F16), carve(20, (KD, TOK), F16)]
        ct = [carve(24, (KD, KV), F16), carve(32, (KD, KV), F16)]
        kt = [carve(40, (HK, KV), F16), carve(56, (HK, KV), F16)]
        vv = [carve(72, (MT, HK * DH), F16), carve(88, (MT, HK * DH), F16)]
        ctx_t_raw = carve(88, (KD, KV))
        ctx_raw = carve(150, (MT, D))
        q2 = carve(166, (MT, D), BF16)
        q1 = carve(174, (NT, D), BF16)
        q1t = carve(178, (KD, TOK), BF16)
        wf = [carve(104, (WS, D), F16), carve(115, (WS, D), F16)]
        kw_raw = carve(126, (KD, D))
        kw = [carve(134, (2, KD * D), F16), carve(142, (2, KD * D), F16)]
        up = carve(150, (FT, TOK))
        gate = carve(172, (FT, TOK))
        og = [carve(150, (FT, TOK), F16), carve(161, (FT, TOK), F16)]
        raw = carve(194, (RAW, D))
        deq = carve(200, (1, D))
        sq0 = carve(182, (2, D))
        kn0 = carve(186, (1, D))
        vf = carve(24 - 16, (2, D))
        sig = carve(12, (2, TOK))
        aq_raw = carve(24, (1, KD * D))
        ao_raw = carve(32, (1, R * D))
        aq = [carve(134, (2, KD * D), F16), carve(142, (2, KD * D), F16)]
        ao = [carve(126, (2, R * D), F16), carve(194, (2, R * D), F16)]
        sc = carve(150, (R, SKV))
        pr = carve(158, (R, SKV))
        pt = [carve(108, (KD, R * P), F16), carve(112, (KD, R * P), F16)]
        sqa = carve(166, (1, D))
        qn = carve(168, (1, D))
        qt = [carve(116, (R, P), F16), carve(117, (R, P), F16)]
        ot = [carve(118, (R, P), F16), carve(119, (R, P), F16)]
        mk = carve(104, (2, SKV))
        me_raw = carve(172, (ER, 3 * D))
        me = [carve(134, (2, 3 * D), F16), carve(140, (2, 3 * D), F16)]
        sg = carve(104, (2, TOK))
        hu = carve(108, (2, TOK))
        hv = carve(112, (2, TOK))
        ht = [carve(116, (2, TOK), F16), carve(118, (2, TOK), F16)]
        b3 = carve(152, (1, D))
        gt = carve(154, (1, TOK))
        rw_raw = carve(156, (KD, NE))
        rw = [carve(156.25, (KD, NE), F16), carve(156.375, (KD, NE), F16)]
        lg, score, masked = carve(156.5, (NT, NE)), carve(156.75, (NT, NE)), carve(157, (NT, NE))
        gmax, keep, kbig = carve(157.25, (NT, 4)), carve(157.5, (NT, 4)), carve(157.75, (NT, 4))
        lmax, lsum, linv = carve(158, (NT,)), carve(158.125, (NT,)), carve(158.25, (NT,))
        rank = carve(158.5, (NT, NE))
        gts, gsc = carve(158.75, (NT, EX)), carve(159.25, (NT, EX))
        tri = carve(168, (NE, NE))
        rbb = carve(169, (2, NE))
        rt_a = carve(160, (NT, NE * NE))
        rt_b = carve(164, (NT, NE * NE))

        def small(name, shape, dtype=F32):
            return es.enter_context(nc.sbuf_tensor(name, [P] + list(shape), dtype))

        ident = small("ident", [P])
        identb = small("identb", [P], BF16)
        onesf = small("onesf", [P])
        ones = small("ones", [P], BF16)
        nh = small("nh", [16])
        par = small("par", [4])
        pc = small("pc", [8])
        st6 = small("st6", [NT, 6])
        mv = small("mv", [NT, 2])
        ve = small("ve", [NT])
        rs = small("rs", [NT])
        rq = small("rq", [NT])
        rsum = small("rsum", [NT])
        mm2 = small("mm2", [2, FT])
        ext = small("ext", [2])
        row2 = small("row2", [4])
        aqp = small("aqp", [5, 8])
        dsc = small("dsc", [SC, 16])
        dsi = small("dsi", [SC, 16])
        ss = small("ss", [2, R])
        rk = small("rk", [2, R])
        nw = small("nw", [2])
        nws = small("nws", [2])
        mneg = small("mneg", [R])
        den = small("den", [R])
        rden = small("rden", [R])
        mb = small("mb", [2, EX])
        mbs = small("mbs", [2, EX])

        def one(v, i):
            return v[:, bass.ds(i, 1)].squeeze(1) if not isinstance(i, int) else v[:, i]

        def cols(v, a, n):
            return v[:, bass.ds(a, n)]

        ps = es.enter_context(nc.psum_tensor("ps", [P, 8, 512], F32))

        def bank(i):
            return one(ps, i)

        def quarters(v):
            return v.rearrange("p (a b) -> p a b", a=4)

        names = set()

        def sem(name):
            assert name not in names
            names.add(name)
            return es.enter_context(nc.semaphore(name))

        in_x, in_par, in_ctx, in_ctt = sem("in_x"), sem("in_par"), sem("in_ctx"), sem("in_ctt")
        in_raw, in_kw, in_mask, in_aq, in_ao = sem("in_raw"), sem("in_kw"), sem("in_mask"), sem("in_aq"), sem("in_ao")
        in_me, in_mp, stored = sem("in_me"), sem("in_mp"), sem("stored")
        own_v, own_a, own_g = sem("own_v"), sem("own_a"), sem("own_g")
        const_g, const_v = sem("const_g"), sem("const_v")
        var_ready, rstd_ready = sem("var_ready"), sem("rstd_ready")
        q1_ready, q1t_ps, q1t_ready = sem("q1_ready"), sem("q1t_ps"), sem("q1t_ready")
        q2_ready, col_ps, x1_ps, x1_done = sem("q2_ready"), sem("col_ps"), sem("x1_ps"), sem("x1_done")
        ext_ready, ext_t, row_ready, ext_b, ext_used = (sem("ext_ready"), sem("ext_t"), sem("row_ready"),
                                                        sem("ext_b"), sem("ext_used"))
        par_ready = sem("par_ready")
        xn_ready, xt_ps, xt_hi, xt_lo = sem("xn_ready"), sem("xt_ps"), sem("xt_hi"), sem("xt_lo")
        ct_hi, ct_lo, kw_sc, kw_hi, kw_lo = sem("ct_hi"), sem("ct_lo"), sem("kw_sc"), sem("kw_hi"), sem("kw_lo")
        k_ps, k_sq, k_ms, k_rs, k_nm, k_t, k_hi, k_lo = (sem("k_ps"), sem("k_sq"), sem("k_ms"), sem("k_rs"),
                                                         sem("k_nm"), sem("k_t"), sem("k_hi"), sem("k_lo"))
        v_ps, v_cp, v_lo = sem("v_ps"), sem("v_cp"), sem("v_lo")
        w_inv, w_div, w_mag, w_rnd, w_deq, w_t, w_hi, w_lo = (sem("w_inv"), sem("w_div"), sem("w_mag"), sem("w_rnd"), sem("w_deq"),
                                                       sem("w_t"), sem("w_hi"), sem("w_lo"))
        f_ps, f_cp, f_mm = sem("f_ps"), sem("f_cp"), sem("f_mm")
        u_y, u_dq = sem("u_y"), sem("u_dq")
        g_y, g_dq, s_y, s_cl, gs_done = sem("g_y"), sem("g_dq"), sem("s_y"), sem("s_cl"), sem("gs_done")
        p_y, p_done = sem("p_y"), sem("p_done")
        o_y, o_int, o_hi, o_lo, d_ps, x2_done = (sem("o_y"), sem("o_int"), sem("o_hi"), sem("o_lo"), sem("d_ps"),
                                                 sem("x2_done"))
        aw_sc, aw_hi, aw_lo = sem("aw_sc"), sem("aw_hi"), sem("aw_lo")
        a_q, a_sq, a_ms, a_rs, a_qn, a_qt, a_qh, a_ql = (sem("a_q"), sem("a_sq"), sem("a_ms"), sem("a_rs"),
                                                         sem("a_qn"), sem("a_qt"), sem("a_qh"), sem("a_ql"))
        a_s, a_sm, a_e, a_rd, a_p, a_pt, a_ph, a_pl = (sem("a_s"), sem("a_sm"), sem("a_e"), sem("a_rd"),
                                                       sem("a_p"), sem("a_pt"), sem("a_ph"), sem("a_pl"))
        a_o, a_oh, a_ol, a_y, a_x = sem("a_o"), sem("a_oh"), sem("a_ol"), sem("a_y"), sem("a_x")
        r_ws, r_ps, r_sub, r_exp, gates_ready, g_t, g_c = (sem("r_ws"), sem("r_ps"), sem("r_sub"), sem("r_exp"),
                                                           sem("gates_ready"), sem("g_t"), sem("g_c"))
        b3_ps, b3_x = sem("b3_ps"), sem("b3_x")
        m_sc, m_hi_in, m_lo_in, m_hi_out, m_lo_out, m_h, m_sg, m_u, m_v, m_hh, m_hl, m_y, m_x = (
            sem("m_sc"), sem("m_hi_in"), sem("m_lo_in"), sem("m_hi_out"), sem("m_lo_out"), sem("m_h"), sem("m_sg"), sem("m_u"), sem("m_v"), sem("m_hh"),
            sem("m_hl"), sem("m_y"), sem("m_x"))

        block = es.enter_context(nc.Block())

        @block.sync
        def _(sp):
            sp.dma_start(xres, x).then_inc(in_x, 16)
            for t, s in ((par, quant_par), (ident, ident_in), (nw, norm_w)):
                sp.dma_start(t[:, :], s).then_inc(in_par, 16)
            sp.dma_start(ctx_raw, ctx).then_inc(in_ctx, 16)
            sp.dma_start(ctx_t_raw, ctx_t).then_inc(in_ctt, 16)

            def sp_wait(s, value):
                wait_apart(sp, s, value, (in_x, 16))

            def ring(n):
                if not isinstance(n, int) or n >= 1:
                    sp_wait(in_raw, n * 16)
                if not isinstance(n, int) or n >= RAW:
                    sp_wait(w_deq, n - RAW + 1)
                sp.dma_start(one(raw, n % RAW), one(ffn_w, n)).then_inc(in_raw, 16)

            def kw_load(c):
                if c >= 1:
                    sp.wait_ge(kw_lo, c)
                sp.dma_start(kw_raw, kv_w[c]).then_inc(in_kw, 16)

            kw_load(0)
            for n in range(RAW):
                ring(n)
            kw_load(1)
            kw_load(2)
            plain_loop(sp, RAW, FT, ring)
            kw_load(3)
            plain_loop(sp, FT, NCH, ring)
            sp.wait_ge(v_ps, 2 * MT)
            sp.dma_start(aq_raw[:, 0], wq[0]).then_inc(in_aq, 16)
            sp.dma_start(ao_raw[:, 0], wo[0]).then_inc(in_ao, 16)
            sp.wait_ge(d_ps, NT)
            sp.dma_start(mk, mask).then_inc(in_mask, 16)
            sp.dma_start(mb[:, :, :], moe_b).then_inc(in_mp, 16)

            def attention_weights(g):
                sp_wait(aw_lo, g * 8 - 4)
                sp.dma_start(aq_raw[:, 0], wq[bass.ds(g, 1)].squeeze(0)).then_inc(in_aq, 16)
                sp_wait(aw_lo, g * 8)
                sp.dma_start(ao_raw[:, 0], wo[bass.ds(g, 1)].squeeze(0)).then_inc(in_ao, 16)

            plain_loop(sp, 1, HK, attention_weights)
            for e in range(ER):
                if e >= 1:
                    sp.wait_ge(in_me, 16 * e)
                sp.dma_start(me_raw[:, e], moe_w[e]).then_inc(in_me, 16)
            sp.wait_ge(a_x, H // R * NT)
            sp.dma_start(b3[0:NE + 1, 0], moe_b3).then_inc(in_mp, 16)
            sp.dma_start(rw_raw, router_w).then_inc(in_mp, 16)
            sp.dma_start(rbb, router_b).then_inc(in_mp, 16)
            sp.dma_start(tri, tri_in).then_inc(in_mp, 16)

            def expert_weights(e):
                sp_wait(in_me, e * 16)
                sp_wait(m_lo_out, e - ER + 1)
                sp.dma_start(one(me_raw, e % ER), moe_w[bass.ds(e, 1)].squeeze(0)).then_inc(in_me, 16)

            plain_loop(sp, ER, EX, expert_weights)
            for t in range(NT):
                sp.wait_ge(m_x, (EX - 1) * NT + t + 1)
                sp.dma_start(out[:, t], xres[:, t]).then_inc(stored, 16)
            sp.wait_ge(stored, 16 * NT)

        @block.gpsimd
        def _(g):
            own = Chain(g, own_g)
            g.memset(nh[:, :], -0.5).then_inc(const_g, 1)
            g.memset(ones[:, :], 1.0).then_inc(const_g, 1)
            g.wait_ge(const_g, 1)

            def rstd(k):
                g.wait_ge(var_ready, k + 1)
                g.tensor_tensor(rs[:, :], ve[:, :], nh[:, 0:NT], ALU.pow).then_inc(rstd_ready, 1)

            rstd(0)

            def kw_split(c):
                g.wait_ge(in_kw, 16 * (c + 1))
                v = kw_raw.rearrange("p a b -> p (a b)")
                if c >= 2:
                    g.wait_ge(k_ps, (c - 1) * MT)
                g.tensor_scalar(v, v, SW, 1.0, ALU.mult, ALU.mult).then_inc(kw_sc, 1)
                g.wait_ge(kw_hi, c + 1)
                g.tensor_tensor(kw[1][:, c % 2], v, kw[0][:, c % 2], ALU.subtract).then_inc(kw_lo, 1)

            kw_split(0)
            rstd(1)
            kw_split(1)

            def divide(n):
                g.wait_ge(w_inv, n + 1)
                v = one(raw, n % RAW).rearrange("p (a b) -> p a b", b=QB)
                s = one(dsi, n % SC).unsqueeze(2).broadcast_to([P, D // QB, QB])
                g.tensor_tensor(v, v, s, ALU.mult).then_inc(w_div, 1)

            def scale_back(n):
                g.wait_ge(w_rnd, n + 1)
                v = one(raw, n % RAW).rearrange("p (a b) -> p a b", b=QB)
                s = one(dsc, n % SC).unsqueeze(2).broadcast_to([P, D // QB, QB])
                if not isinstance(n, int) or n >= 1:
                    g.wait_ge(w_t, n)
                g.tensor_tensor(deq[:, 0].rearrange("p (a b) -> p a b", b=QB), v, s, ALU.mult).then_inc(w_deq, 1)

            divide(0)
            scale_back(0)
            divide(1)

            def k_pow(u):
                g.wait_ge(k_ms, u + 1)
                if not isinstance(u, int) or u >= 2:
                    g.wait_ge(k_nm, u - 1)
                g.tensor_tensor(one(rk, u % 2), one(ss, u % 2), nh[:, 0:R], ALU.pow).then_inc(k_rs, 1)

            k_pow(0)
            k_pow(1)
            plain_loop(g, 2, 2 * MT, k_pow)

            def divide(n):
                g.wait_ge(w_inv, n + 1)
                v = one(raw, n % RAW).rearrange("p (a b) -> p a b", b=QB)
                s = one(dsi, n % SC).unsqueeze(2).broadcast_to([P, D // QB, QB])
                g.tensor_tensor(v, v, s, ALU.mult).then_inc(w_div, 1)

            def scale_back(n):
                g.wait_ge(w_rnd, n + 1)
                v = one(raw, n % RAW).rearrange("p (a b) -> p a b", b=QB)
                s = one(dsc, n % SC).unsqueeze(2).broadcast_to([P, D // QB, QB])
                if not isinstance(n, int) or n >= 1:
                    g.wait_ge(w_t, n)
                g.tensor_tensor(deq[:, 0].rearrange("p (a b) -> p a b", b=QB), v, s, ALU.mult).then_inc(w_deq, 1)

            kw_split(2)

            def weights(n, more=True):
                scale_back(n)
                if more:
                    divide(n + 1)

            weights(1)
            plain_loop(g, 2, FT + 1, weights)
            kw_split(3)
            plain_loop(g, FT + 1, 2 * FT + 1, weights)

            def v_low(u):
                g.wait_ge(v_cp, u + 1)
                c, m = u // MT, u % MT
                g.tensor_tensor(cols(one(vv[1], m), c * D, D), one(vf, u % 2), cols(one(vv[0], m), c * D, D),
                                ALU.subtract).then_inc(v_lo, 1)

            def down_turn(i, more=True):
                weights(2 * FT + 1 + i, more)
                v_low(i - 1)

            weights(2 * FT + 1)
            weights(2 * FT + 2)
            v_low(0)
            down_turn(2)
            plain_loop(g, 3, FT - 2, down_turn)
            down_turn(FT - 2, False)
            plain_loop(g, FT - 2, 2 * MT, v_low)

            def attention_split(g_, part, k):
                src = (aq_raw, ao_raw)[part][:, 0, k * D:(k + 1) * D]
                lo, hi = (cols(one(w, g_ % 2), k * D, D) for w in ((aq, ao)[part][1], (aq, ao)[part][0]))
                if k == 0:
                    wait_apart(g, (in_aq, in_ao)[part], (g_ + 1) * 16, (const_g, 2))
                g.tensor_scalar(src, src, SW, 1.0, ALU.mult, ALU.mult).then_inc(aw_sc, 1)
                g.wait_ge(aw_hi, g_ * 8 + part * 4 + k + 1)
                g.tensor_tensor(lo, src, hi, ALU.subtract).then_inc(aw_lo, 1)

            for part in range(2):
                for k in range(4):
                    attention_split(0, part, k)
            rstd(2)

            def q_pow(u):
                g.wait_ge(a_ms, u + 1)
                g.tensor_tensor(rk[:, 0], ss[:, 0], nh[:, 0:R], ALU.pow).then_inc(a_rs, 1)

            def attention_step(j, s):
                u = 4 * j + s
                for h in range(R):
                    wait_apart(g, a_rd, 4 * u + h + 1, (const_g, 2))
                    g.tensor_scalar(pr[:, h], pr[:, h], rden[:, h:h + 1], SP, ALU.mult, ALU.mult)\
                     .then_inc(a_p, 1)
                if not isinstance(j, int) or u + 1 < HK * NT:
                    q_pow(u + 1)
                if not isinstance(j, int):
                    for i in range(2):
                        attention_split(j + 1, (s - 1) // 2, 2 * ((s - 1) % 2) + i)

            q_pow(0)
            attention_step(0, 0)
            with g.Fori(0, HK - 1) as j:
                for s in range(1, 5):
                    attention_step(j, s)
            for s in range(1, 4):
                attention_step(HK - 1, s)

            def low_in(e, q):
                g.wait_ge(m_hi_in, e + 1)
                g.tensor_tensor(me[1][:, q, 0:2 * D], one(me_raw, e % ER)[:, 0:2 * D], me[0][:, q, 0:2 * D],
                                ALU.subtract).then_inc(m_lo_in, 1)

            def low_out(e, q):
                g.wait_ge(m_hi_out, e + 1)
                g.tensor_tensor(me[1][:, q, 2 * D:3 * D], one(me_raw, e % ER)[:, 2 * D:3 * D],
                                me[0][:, q, 2 * D:3 * D], ALU.subtract).then_inc(m_lo_out, 1)

            low_in(0, 0)
            low_out(0, 0)
            low_in(1, 1)
            rstd(3)

            def expert_turn(j):
                for s in range(2):
                    low_in(2 * j + s, s)
                    low_out(2 * j + s - 1, 1 - s)
            plain_loop(g, 1, EX // 2, expert_turn)
            low_out(EX - 1, 1)

        @block.scalar
        def _(a):
            def copy(out_, in_, scale=1.0, bias=0.0):
                return a.activation(out_, in_, ACT.Copy, scale=scale, bias=bias)

            a.wait_ge(in_ctt, 16)
            for k in range(KD):
                copy(ct[0][:, k], ctx_t_raw[:, k], SX).then_inc(ct_hi, 1)

            def kw_high(c):
                a.wait_ge(kw_sc, c + 1)
                copy(kw[0][:, c % 2], kw_raw.rearrange("p a b -> p (a b)")).then_inc(kw_hi, 1)

            kw_high(0)
            for k in range(KD):
                a.wait_ge(q1t_ps, k + 1)
                copy(q1t[:, k], bank(k).bitcast(BF16)[:, 0:TOK]).then_inc(q1t_ready, 1)
            kw_high(1)

            def hidden_high(n, scale):
                for k in range(KD):
                    a.wait_ge(xt_ps, KD * n + k + 1)
                    copy(xt[0][:, k], bank(k), scale).then_inc(xt_hi, 1)

            hidden_high(0, 1.0)

            def round_weights(n):
                w = one(raw, n % RAW)
                wait_apart(a, w_div, n + 1, (in_ctt, 16))
                copy(w, w, 1.0, MAGIC).then_inc(w_mag, 1)
                wait_apart(a, w_mag, n + 1, (in_ctt, 16))
                copy(w, w, 1.0, -MAGIC).then_inc(w_rnd, 1)

            round_weights(0)

            def k_square(u):
                a.wait_ge(k_ps, u + 1)
                if not isinstance(u, int) or u >= 2:
                    a.wait_ge(k_ms, u - 1)
                a.activation(one(sq0, u % 2), bank(u % KB), ACT.Square).then_inc(k_sq, 1)

            def k_high(u):
                a.wait_ge(k_t, u + 1)
                c, m = u // MT, u % MT
                copy(kt[0][:, bass.ds(4 * c, 4), bass.ds(m * P, P)], quarters(bank(6)), nws[:, 1:2]).then_inc(k_hi, 1)

            a.wait_ge(const_v, 3)
            k_square(0)
            k_square(1)

            def k_turn(u):
                k_square(u + 2)
                k_high(u)
            k_turn(0)
            plain_loop(a, 1, 2 * MT - 2, k_turn)
            k_high(2 * MT - 2)
            k_high(2 * MT - 1)

            kw_high(2)

            def weight_high(n, reused=True):
                a.wait_ge(w_t, n + 1)
                if reused:
                    a.wait_ge(f_ps, n - WS + 1)
                copy(one(wf[0], n % WS), bank(2), SW).then_inc(w_hi, 1)

            def tile_out(n, dst, scale):
                a.wait_ge(f_ps, n + 1)
                copy(one(dst, n % FT), bank(n % 2), scale).then_inc(f_cp, 1)

            sx4 = aqp[:, 0, 4:5]

            def up_turn(n):
                weight_high(n + 1, reused=False)
                round_weights(n + 2)
                tile_out(n, up, sx4)

            round_weights(1)
            weight_high(0, reused=False)
            plain_loop(a, 0, FT - 1, up_turn)
            weight_high(FT)
            round_weights(FT + 1)
            tile_out(FT - 1, up, sx4)
            kw_high(3)

            def quantise(src, j, i, done):
                copy(one(src, i), one(src, i), aqp[:, j, 0:1], MAGIC).then_inc(done, 1)

            def gate_turn(n):
                weight_high(n + 1)
                round_weights(n + 2)
                tile_out(n, gate, sx4)
                if isinstance(n, int):
                    a.wait_ge(par_ready, 2)
                quantise(up, 1, n - FT, u_y)
            gate_turn(FT)
            plain_loop(a, FT + 1, 2 * FT, gate_turn)

            def v_out(u):
                c, m = u // MT, u % MT
                a.wait_ge(v_ps, u + 1)
                copy(cols(one(vv[0], m), c * D, D), bank(4 + u % 2), 1.0 / SW)
                if not isinstance(u, int) or u >= 2:
                    a.wait_ge(v_lo, u - 1)
                copy(one(vf, u % 2), bank(4 + u % 2), 1.0 / SW).then_inc(v_cp, 1)

            def gate_front(i):
                quantise(gate, 2, i, g_y)

            def gate_sigmoid(i):
                wait_apart(a, g_dq, i + 1, (in_ctt, 16))
                a.activation(one(sig, i % 2), one(gate, i), ACT.Sigmoid).then_inc(own_a, 1)
                wait_apart(a, own_a, i + 1, (in_ctt, 16))
                copy(one(sig, i % 2), one(sig, i % 2), 65536.0, MAGIC).then_inc(s_y, 1)

            v_out(0)
            a.wait_ge(par_ready, 3)
            gate_front(0)

            def down_turn(i, more=True, rounds=True):
                if more:
                    gate_front(i + 1)
                if not isinstance(i, int) or i >= 1:
                    if not isinstance(i, int) or i >= 3:
                        a.wait_ge(gs_done, i - 2)
                    gate_sigmoid(i - 1)
                if more:
                    weight_high(2 * FT + i + 1)
                    if rounds:
                        round_weights(2 * FT + i + 2)
                v_out(i + 1)

            for i in range(3):
                down_turn(i)
            plain_loop(a, 3, FT - 2, down_turn)
            down_turn(FT - 2, rounds=False)
            down_turn(FT - 1, False)
            a.wait_ge(gs_done, FT - 2)
            gate_sigmoid(FT - 1)

            a.wait_ge(par_ready, 4)

            def product_quant(i):
                quantise(gate, 3, i, p_y)

            def product_turn(i):
                product_quant(i)
                v_out(FT + 1 + i)
            plain_loop(a, 0, 2 * MT - FT - 1, product_turn)
            plain_loop(a, 2 * MT - FT - 1, FT, product_quant)

            def attention_high(g_, part, k):
                n = g_ * 8 + part * 4 + k
                a.wait_ge(aw_sc, n + 1)
                copy(cols(one((aq, ao)[part][0], g_ % 2), k * D, D),
                     (aq_raw, ao_raw)[part][:, 0, k * D:(k + 1) * D]).then_inc(aw_hi, 1)

            for part in range(2):
                for k in range(4):
                    attention_high(0, part, k)
            a.wait_ge(par_ready, 5)

            def out_quant(i):
                quantise(gate, 4, i, o_y)

            def out_high(i):
                a.wait_ge(o_int, i + 1)
                copy(one(og[0], i), one(gate, i)).then_inc(o_hi, 1)
            out_quant(0)

            def out_turn(i):
                out_quant(i + 1)
                out_high(i)
            plain_loop(a, 0, FT - 1, out_turn)
            out_high(FT - 1)

            hidden_high(1, SX)

            def q_square(u):
                a.wait_ge(a_q, u + 1)
                a.activation(sqa[:, 0], bank(4), ACT.Square).then_inc(a_sq, 1)

            def q_high(u):
                a.wait_ge(a_qt, u + 1)
                copy(qt[0], quarters(bank(5)), nws[:, 0:1]).then_inc(a_qh, 1)

            def o_high(u):
                a.wait_ge(a_o, u + 1)
                copy(ot[0], quarters(bank(6)), 1.0 / SP).then_inc(a_oh, 1)

            def attention_step(j, s):
                u = 4 * j + s
                for h in range(R):
                    a.wait_ge(a_sm, 4 * u + h + 1)
                    if h == 0 and not (isinstance(j, int) and u == 0):
                        a.wait_ge(a_pt, 4 * u)
                    a.activation(pr[:, h], sc[:, h], ACT.Exp, bias=mneg[:, h:h + 1], scale=-1.0,
                                 accum_out=den[:, h:h + 1]).then_inc(a_e, 1)
                more = not isinstance(j, int) or u + 1 < HK * NT
                if more:
                    q_square(u + 1)
                if not isinstance(j, int) or u >= 1:
                    o_high(u - 1)
                for h in range(R):
                    if more and h == R - 1:
                        q_high(u + 1)
                    a.wait_ge(a_pt, 4 * u + h + 1)
                    if h == 0 and (not isinstance(j, int) or u >= 1):
                        a.wait_ge(a_o, u)
                    copy(pt[0][:, :, h * P:(h + 1) * P], quarters(bank(h))).then_inc(a_ph, 1)
                if not isinstance(j, int):
                    for i in range(2):
                        attention_high(j + 1, (s - 1) // 2, 2 * ((s - 1) % 2) + i)

            q_square(0)
            q_high(0)
            attention_step(0, 0)
            with a.Fori(0, HK - 1) as j:
                for s in range(1, 5):
                    attention_step(j, s)
            for s in range(1, 4):
                attention_step(HK - 1, s)
            o_high(HK * NT - 1)

            def scale(e):
                wait_apart(a, in_me, (e + 1) * 16, (in_ctt, 16))
                copy(one(me_raw, e % ER), one(me_raw, e % ER), SW).then_inc(m_sc, 1)

            def high_in(e, q):
                if not isinstance(e, int) or e >= 2:
                    wait_apart(a, m_h, (e - 1) * 2, (in_ctt, 16))
                wait_apart(a, m_sc, e + 1, (in_ctt, 16))
                copy(me[0][:, q, 0:2 * D], one(me_raw, e % ER)[:, 0:2 * D]).then_inc(m_hi_in, 1)

            def high_out(e, q):
                if not isinstance(e, int) or e >= 2:
                    wait_apart(a, m_y, (e - 1) * NT, (in_ctt, 16))
                wait_apart(a, m_sc, e + 1, (in_ctt, 16))
                copy(me[0][:, q, 2 * D:3 * D], one(me_raw, e % ER)[:, 2 * D:3 * D]).then_inc(m_hi_out, 1)

            scale(0)
            high_in(0, 0)
            high_out(0, 0)
            scale(1)
            high_in(1, 1)
            hidden_high(2, SX)
            a.wait_ge(r_sub, 1)
            a.activation(lg, lg, ACT.Exp).then_inc(r_exp, 1)
            a.wait_ge(g_t, 1)
            copy(gt[0:NE + 1, 0], bank(5)[0:NE + 1, :]).then_inc(g_c, 1)

            def expert_step(j, s):
                e, q = 2 * j + s, s % 2
                a.wait_ge(m_h, 2 * e + 1)
                if not isinstance(j, int) or e >= 2:
                    a.wait_ge(m_u, e - 1)
                a.activation(sg[:, q], bank(2 * q), ACT.Sigmoid, bias=mb[:, 0, bass.ds(e, 1)], scale=1.0 / SXW).then_inc(m_sg, 1)
                if not isinstance(j, int) or e + 2 < EX:
                    scale(e + 2)
                a.wait_ge(m_v, e + 1)
                if not isinstance(j, int) or e >= 2:
                    a.wait_ge(m_y, (e - 1) * NT)
                copy(ht[0][:, q], hv[:, q], 2.0 ** -16).then_inc(m_hh, 1)
                if not isinstance(j, int) or e + 2 < EX:
                    high_in(e + 2, q)
                if not isinstance(j, int) or e + 1 < EX:
                    high_out(e + 1, 1 - q)

            expert_step(0, 0)
            expert_step(0, 1)
            with a.Fori(1, EX // 2 - 1) as j:
                for s in range(2):
                    expert_step(j, s)
            expert_step(EX // 2 - 1, 0)
            expert_step(EX // 2 - 1, 1)

        @block.tensor
        def _(pe):
            def product(out_, lhs, rhs, first, last):
                pe.matmul(out_, lhs[0], rhs[0], start=first, stop=False)
                pe.matmul(out_, lhs[0], rhs[1], start=False, stop=False)
                return pe.matmul(out_, lhs[1], rhs[0], start=False, stop=last)

            pe.wait_ge(const_v, 1)
            pe.wait_ge(q1_ready, 1)
            for k in range(KD):
                for t in range(NT):
                    mm = pe.transpose(bank(k).bitcast(BF16)[:, t * P:(t + 1) * P], q1[:, t, k * P:(k + 1) * P],
                                      identb[:, :])
                mm.then_inc(q1t_ps, 1)
            pe.wait_ge(const_g, 2)
            pe.wait_ge(q2_ready, 1)
            for b in range(B):
                for k in range(KD):
                    mm = pe.matmul(bank(6 + b), ones[:, :], q2[:, b * KD + k], start=k == 0, stop=k == KD - 1)
                mm.then_inc(col_ps, 1)
            pe.wait_ge(q1t_ready, KD)
            for t in range(NT):
                for k in range(KD):
                    mm = pe.matmul(bank((4, 5, 0, 1)[t]), q1t[:, k, t * P:(t + 1) * P], q2[:, t // 2 * KD + k],
                                   start=k == 0, stop=k == KD - 1)
                mm.then_inc(x1_ps, 1)

            def spread(k):
                pe.wait_ge(ext_ready, k + 1)
                pe.transpose(bank(7)[0:2, 0:P], ext[:, :], ident[:, :]).then_inc(ext_t, 1)
                pe.wait_ge(row_ready, k + 1)
                pe.matmul(bank(7)[:, P:P + 2], onesf[0:2, :], row2[0:2, 2:4], start=True, stop=True).then_inc(ext_b, 1)

            spread(0)

            def hidden_transposes(n):
                pe.wait_ge(xn_ready, n + 1)
                for k in range(KD):
                    for t in range(NT):
                        mm = pe.transpose(bank(k)[:, t * P:(t + 1) * P], xn[:, t, k * P:(k + 1) * P], ident[:, :])
                    mm.then_inc(xt_ps, 1)

            hidden_transposes(0)

            def kv_product(c, m, dst):
                for k in range(KD):
                    lhs = [cols(h[:, k], m * P, P) for h in ct]
                    rhs = [cols(one(h, c), k * D, D) for h in kw]
                    mm = product(dst, lhs, rhs, k == 0, k == KD - 1)
                return mm

            def k_unit(c, m):
                u = c * MT + m
                if m == 0:
                    pe.wait_ge(kw_lo, c + 1)
                if not isinstance(c, int) or u >= KB:
                    pe.wait_ge(k_nm, u - KB + 1)
                elif c == 0:
                    pe.wait_ge(xt_lo, m + 1)
                kv_product(c, m, bank(m % KB)).then_inc(k_ps, 1)

            def k_transposes(u):
                pe.wait_ge(k_nm, u + 1)
                if not isinstance(u, int) or u >= 1:
                    pe.wait_ge(k_lo, u)
                for h in range(4):
                    mm = pe.transpose(bank(6)[:, h * P:(h + 1) * P], kn0[:, 0, h * P:(h + 1) * P], ident[:, :])
                mm.then_inc(k_t, 1)

            units = [(c, m) for c in range(KW // 2) for m in range(MT)]
            for u, (c, m) in enumerate(units):
                k_unit(c, m)
                if u >= K_AHEAD:
                    k_transposes(u - K_AHEAD)
            for u in range(len(units) - K_AHEAD, len(units)):
                k_transposes(u)

            def weight_transposes(n):
                pe.wait_ge(w_deq, n + 1)
                if not isinstance(n, int) or n >= 1:
                    pe.wait_ge(w_lo, n)
                for k in range(4):
                    mm = pe.transpose(bank(2)[:, k * P:(k + 1) * P], deq[:, 0, k * P:(k + 1) * P],
                                      ident[:, :])
                mm.then_inc(w_t, 1)

            def tile(base, i, odd):
                n = base + i
                pe.wait_ge(w_lo, n + 1)
                if not isinstance(n, int) or n >= 2:
                    pe.wait_ge(f_cp, n - 1)
                for k in range(KD):
                    lhs = [cols(one(h, i), k * P, P) for h in wf]
                    mm = product(bank(odd), lhs, [h[:, k] for h in xt], k == 0, k == KD - 1)
                mm.then_inc(f_ps, 1)

            pe.wait_ge(xt_lo, KD)
            weight_transposes(0)

            def tiles(base):
                def step(i, odd):
                    weight_transposes(base + i + 1)
                    tile(base, i, odd)
                for i in range(3):
                    step(i, (base + i) % 2)
                with pe.Fori(1, FT // 2) as j:
                    for s in range(2):
                        step(2 * j + 1 + s, (base + 1 + s) % 2)

            assert FT % 2 == 1
            tiles(0)
            spread(1)
            tiles(FT)

            def v_unit(c, m, odd):
                u = c * MT + m
                pe.wait_ge(kw_lo, KW // 2 + c + 1)
                if not isinstance(u, int) or u >= 2:
                    pe.wait_ge(v_cp, u - 1)
                kv_product(c, m, bank(4 + odd)).then_inc(v_ps, 1)

            def v_turn(c, m, odd):
                weight_transposes(2 * FT + c * MT + m - 1)
                v_unit(c, m, odd)

            def by_two(c, lo, hi, turn):
                with pe.Fori(lo // 2, hi // 2) as j:
                    for s in range(2):
                        turn(c, 2 * j + s, s)

            last = FT + 1 - MT
            v_unit(0, 0, 0)
            v_unit(0, 1, 1)
            spread(2)
            by_two(0, 2, MT, v_turn)
            by_two(1, 0, last, v_turn)
            spread(3)
            by_two(1, last, MT, v_unit)
            spread(4)

            def down(i, first=False, last=False):
                pe.wait_ge(o_lo, i + 1)
                for t in range(NT):
                    lhs = [cols(one(h, i), t * P, P) for h in og]
                    mm = product(bank(t), lhs, [one(h, i) for h in wf], first, last)
                    if last:
                        mm.then_inc(d_ps, 1)
            pe.wait_ge(w_lo, NCH)
            down(0, first=True)
            plain_loop(pe, 1, FT - 1, down)
            down(FT - 1, last=True)

            hidden_transposes(1)

            def q_unit(j, s):
                u, par_ = 4 * j + s, (j + s // 4) % 2
                if s % 4 == 0:
                    pe.wait_ge(aw_lo, (j + s // 4) * 8 + 4)
                if not isinstance(j, int) or u >= 1:
                    pe.wait_ge(a_qn, u)
                t = s % 4
                for k in range(KD):
                    rhs = [cols(one(h, par_), k * D, D) for h in aq]
                    mm = product(bank(4), [h[:, k, t * P:(t + 1) * P] for h in xt], rhs, k == 0, k == KD - 1)
                mm.then_inc(a_q, 1)

            def q_transposes(u):
                pe.wait_ge(a_qn, u + 1)
                if not isinstance(u, int) or u >= 1:
                    pe.wait_ge(a_ql, u)
                for h in range(R):
                    mm = pe.transpose(bank(5)[:, h * P:(h + 1) * P], qn[:, 0, h * P:(h + 1) * P], ident[:, :])
                mm.then_inc(a_qt, 1)

            def scores(j, s):
                u, grp, b = 4 * j + s, j + s // 4, s % 4 // 2
                pe.wait_ge(a_ql, u + 1)
                for h in range(R):
                    if not isinstance(j, int) or u >= 1:
                        pe.wait_ge(a_pl, 4 * u - 3 + h)
                    rhs = [cols(one(w, grp), b * SKV, SKV) for w in kt]
                    product(bank(h), [w[:, h] for w in qt], rhs, True, True).then_inc(a_s, 1)

            def values(j, s):
                u, grp, b = 4 * j + s, j + s // 4, s % 4 // 2
                pe.wait_ge(a_pl, 4 * u + 4)
                if not isinstance(j, int) or u >= 1:
                    pe.wait_ge(a_ol, u)
                for k in range(KD):
                    lhs = [cols(w[:, b * KD + k], grp * DH, DH) for w in vv]
                    mm = product(bank(6), lhs, [w[:, k] for w in pt], k == 0, k == KD - 1)
                mm.then_inc(a_o, 1)

            def p_transposes(u):
                for h in range(R):
                    pe.wait_ge(a_p, 4 * u + h + 1)
                    for k in range(KD):
                        mm = pe.transpose(bank(h)[:, k * P:(k + 1) * P], pr[:, h, k * P:(k + 1) * P], ident[:, :])
                    mm.then_inc(a_pt, 1)

            def project(j, s):
                u, par_ = 4 * j + s, (j + s // 4) % 2
                if s % 4 == 0:
                    pe.wait_ge(aw_lo, (j + s // 4) * 8 + 8)
                pe.wait_ge(a_ol, u + 1)
                if not isinstance(j, int) or u >= 1:
                    pe.wait_ge(a_x, u)
                for h in range(R):
                    rhs = [cols(one(w, par_), h * D, D) for w in ao]
                    mm = product(bank(7), [w[:, h] for w in ot], rhs, h == 0, h == R - 1)
                mm.then_inc(a_y, 1)

            def attention_step(j, s):
                u = 4 * j + s
                more = not isinstance(j, int) or u + 1 < HK * NT
                scores(j, s)
                if more:
                    q_unit(j, s + 1)
                if not isinstance(j, int) or u >= 1:
                    values(j, s - 1)
                p_transposes(u)
                if more:
                    q_transposes(u + 1)
                if not isinstance(j, int) or u >= 1:
                    project(j, s - 1)

            pe.wait_ge(xt_lo, 2 * KD)
            q_unit(0, 0)
            q_transposes(0)
            attention_step(0, 0)
            with pe.Fori(0, HK - 1) as j:
                for s in range(1, 5):
                    attention_step(j, s)
            for s in range(1, 4):
                attention_step(HK - 1, s)
            values(HK - 1, 3)
            project(HK - 1, 3)

            hidden_transposes(2)
            pe.wait_ge(xt_lo, 3 * KD)
            pe.wait_ge(r_ws, 2)
            for t in range(NT):
                for k in range(KD):
                    for i in range(2):
                        for w in range(2):
                            mm = pe.matmul(bank(4)[:, t * NE:(t + 1) * NE], xt[i][:, k, t * P:(t + 1) * P], rw[w][:, k],
                                           start=k + i + w == 0, stop=k == KD - 1 and i + w == 2)
            mm.then_inc(r_ps, 1)

            def hidden(e, q):
                pe.wait_ge(m_lo_in, e + 1)
                if not isinstance(e, int) or e >= 2:
                    pe.wait_ge(m_v, e - 1)
                for i in range(2):
                    for k in range(KD):
                        lhs = [w[:, q, i * D + k * P:i * D + (k + 1) * P] for w in me]
                        mm = product(bank(2 * q + i), lhs, [h[:, k] for h in xt], k == 0, k == KD - 1)
                    mm.then_inc(m_h, 1)

            def experts_out(e, q):
                pe.wait_ge(m_hl, e + 1)
                pe.wait_ge(m_lo_out, e + 1)
                for t in range(NT):
                    if not isinstance(e, int) or e >= 1:
                        pe.wait_ge(m_x, (e - 1) * NT + t + 1)
                    product(bank(4 + t), [h[:, q, t * P:(t + 1) * P] for h in ht],
                            [w[:, q, 2 * D:3 * D] for w in me], True, True).then_inc(m_y, 1)

            hidden(0, 0)
            hidden(1, 1)
            pe.wait_ge(gates_ready, 1)
            for t in range(NT):
                mm = pe.transpose(bank(5)[0:NE + 1, t * P:(t + 1) * P], gts[:, t, 1:EX], ident[:, :])
            mm.then_inc(g_t, 1)
            pe.wait_ge(g_c, 1)
            for t in range(NT):
                pe.matmul(bank(4 + t), gt[0:NE + 1, 0, t * P:(t + 1) * P], b3[0:NE + 1, 0], start=True,
                          stop=True).then_inc(b3_ps, 1)
            pe.wait_ge(b3_x, NT)
            experts_out(0, 0)
            with pe.Fori(0, EX // 2 - 1) as j:
                for s in range(1, 3):
                    hidden(2 * j + s + 1, (s + 1) % 2)
                    experts_out(2 * j + s, s % 2)
            experts_out(EX - 1, 1)

        @block.vector
        def _(v):
            own = Chain(v, own_v)

            def tt(out_, x_, y_, op):
                return v.tensor_tensor(out_, x_, y_, op)

            def ts(out_, x_, s1, o1, s2=None, o2=ALU.bypass):
                return v.tensor_scalar(out_, x_, s1, s2, o1, o2)

            def stt(out_, x_, s_, y_, o1, o2):
                return v.scalar_tensor_tensor(out_, x_, s_, y_, o1, o2)

            def flat(w):
                return w.rearrange("p a b -> p (a b)")

            v.memset(onesf[:, :], 1.0).then_inc(const_v, 1)
            v.wait_ge(in_par, 48)
            v.tensor_copy(identb[:, :], ident[:, :]).then_inc(const_v, 1)
            own.mark(ts(nws[:, 0:1], nw[:, 0:1], SW / DH ** 0.5, ALU.mult))
            ts(nws[:, 1:2], nw[:, 1:2], SX, ALU.mult).then_inc(const_v, 1)
            inv1, inv2, w1, w2, s12, c1, c2, k1 = (pc[:, i:i + 1] for i in range(8))
            own.mark(v.reciprocal(pc[:, 0:2], par[:, 0:2]))
            own.mark(ts(pc[:, 2:4], par[:, 2:4], -1.0, ALU.mult, 128.0, ALU.add))
            own.link(tt(s12, par[:, 0:1], par[:, 1:2], ALU.mult))
            own.mark(tt(c1, s12, w1, ALU.mult))
            own.mark(tt(c2, s12, w2, ALU.mult))
            own.link(ts(k1, w1, float(D), ALU.mult))

            def norm_stats(k, t):
                own.link(v.bn_stats(st6[:, t], xres[:, t]))
                own.link(v.bn_aggr(mv[:, t], st6[:, t]))

            def norm_var():
                ts(ve[:, :], mv[:, :, 1], EPS, ALU.add).then_inc(var_ready, 1)

            v.wait_ge(in_x, 16)
            for t in range(NT):
                own.mark(v.bn_stats(st6[:, t], xres[:, t]))
            own.wait(own.n)
            for t in range(NT):
                own.mark(v.bn_aggr(mv[:, t], st6[:, t]))
            own.wait(own.n)
            norm_var()
            v.wait_ge(in_ctx, 16)
            own.link(ts(flat(ctx_raw), flat(ctx_raw), inv2, ALU.mult, par[:, 3:4], ALU.add))
            v.wait_ge(rstd_ready, 1)
            own.link(ts(rq[:, :], rs[:, :], inv1, ALU.mult))
            for t in range(NT):
                own.mark(ts(xn[:, t], xres[:, t], mv[:, t, 0:1], ALU.subtract, rq[:, t:t + 1], ALU.mult))
            own.wait(own.n)
            own.link(ts(flat(xn), flat(xn), par[:, 2:3], ALU.add, MAGIC, ALU.add))
            own.link(ts(flat(xn), flat(xn), MAGIC, ALU.max, MAGIC + 255.0, ALU.min))
            ts(flat(q1), flat(xn), MAGIC + 128.0, ALU.subtract).then_inc(q1_ready, 1)
            own.link(ts(flat(ctx_raw), flat(ctx_raw), MAGIC, ALU.add, MAGIC, ALU.max))
            ts(flat(q2), flat(ctx_raw), MAGIC + 255.0, ALU.min, MAGIC + 128.0, ALU.subtract).then_inc(q2_ready, 1)
            v.wait_ge(q1_ready, 1)
            own.link(v.tensor_reduce(rsum[:, :], q1, AX.X, ALU.add))
            own.link(ts(rsum[:, :], rsum[:, :], k1, ALU.add, c2, ALU.mult))
            for t in range(NT):
                v.wait_ge(col_ps, t // 2 + 1)
                own.link(stt(xres[:, t], bank(6 + t // 2), c1, xres[:, t], ALU.mult, ALU.add))
                own.link(ts(xres[:, t], xres[:, t], rsum[:, t:t + 1], ALU.add))

            for k in range(KD):
                v.wait_ge(ct_hi, k + 1)
                stt(ct[1][:, k], ctx_t_raw[:, k], SX, ct[0][:, k], ALU.mult, ALU.subtract).then_inc(ct_lo, 1)

            for t in range(NT):
                v.wait_ge(x1_ps, t + 1)
                own.link(stt(xres[:, t], bank((4, 5, 0, 1)[t]), s12, xres[:, t], ALU.mult, ALU.add))
                own.link(v.bn_stats(st6[:, t], xres[:, t]))
                own.link(v.bn_aggr(mv[:, t], st6[:, t]))
            norm_var()

            def normalise(k):
                v.wait_ge(rstd_ready, k + 1)
                for t in range(NT):
                    i = ts(xn[:, t], xres[:, t], mv[:, t, 0:1], ALU.subtract, rs[:, t:t + 1], ALU.mult)
                    if k != 1 and t == NT - 1:
                        i.then_inc(xn_ready, 1)
                    else:
                        own.mark(i)

            normalise(1)
            own.wait(own.n)

            def extrema(src, col):
                own.mark(v.tensor_reduce(mm2[:, 0, bass.ds(col, 1)], src, AX.X, ALU.max))
                own.mark(v.tensor_reduce(mm2[:, 1, bass.ds(col, 1)], src, AX.X, ALU.min, negate=True))

            for t in range(NT):
                extrema(xn[:, t], t)
            own.wait(own.n)

            def parameters(k, n, factor):
                v.tensor_reduce(ext[:, :], mm2[:, :, 0:n], AX.X, ALU.max).then_inc(ext_ready, 1)
                v.wait_ge(ext_t, k + 1)
                own.link(v.tensor_reduce(row2[0:2, 0:1], bank(7)[0:2, 0:P], AX.X, ALU.max))
                ts(row2[0:2, 2:4], ident[0:2, 0:2], row2[0:2, 0:1], ALU.mult).then_inc(row_ready, 1)
                v.wait_ge(ext_b, k + 1)
                yinv, lo, hi, s, s4, inv, z = (aqp[:, k, i:i + 1] for i in range(7))
                own.link(ts(ext[:, :], bank(7)[:, P:P + 2], 0.0, ALU.max, factor, ALU.mult))
                own.link(tt(s, ext[:, 0:1], ext[:, 1:2], ALU.add))
                own.link(ts(s, s, 1.0 / QMAX, ALU.mult, TINY, ALU.max))
                own.link(v.reciprocal(inv, s))
                own.mark(ts(s4, s, 4.0, ALU.mult))
                own.mark(ts(yinv, inv, factor, ALU.mult))
                own.link(ts(z, ext[:, 1:2], inv, ALU.mult, MAGIC, ALU.add))
                own.link(ts(z, z, MAGIC + QMAX, ALU.min, MAGIC, ALU.subtract))
                own.link(ts(lo, z, -1.0, ALU.mult, MAGIC, ALU.add))
                ts(hi, lo, QMAX, ALU.add).then_inc(par_ready, 1)
                v.wait_ge(par_ready, k + 1)

            def clip(dst, k):
                return ts(dst, dst, aqp[:, k, 1:2], ALU.max, aqp[:, k, 2:3], ALU.min)

            parameters(0, NT, 1.0)
            own.link(ts(flat(xn), flat(xn), aqp[:, 0, 0:1], ALU.mult, MAGIC, ALU.add))
            own.link(clip(flat(xn), 0))
            ts(flat(xn), flat(xn), MAGIC, ALU.subtract, SINT, ALU.mult).then_inc(xn_ready, 1)

            def hidden_low(n, scale):
                for k in range(KD):
                    v.wait_ge(xt_hi, KD * n + k + 1)
                    stt(xt[1][:, k], bank(k), scale, xt[0][:, k], ALU.mult, ALU.subtract).then_inc(xt_lo, 1)

            hidden_low(0, 1.0)

            def block_scales(n):
                v.wait_ge(in_raw, 16 * (n + 1))
                s, i = one(dsc, n % SC), one(dsi, n % SC)
                src = one(raw, n % RAW).rearrange("p (a b) -> p a b", b=QB)
                own.link(v.tensor_reduce(s, src, AX.X, ALU.max, apply_absolute_value=True))
                own.link(ts(s, s, 1.0 / 7.0, ALU.mult, TINY, ALU.max))
                v.reciprocal(i, s).then_inc(w_inv, 1)

            def weight_low(n):
                v.wait_ge(w_hi, n + 1)
                stt(one(wf[1], n % WS), bank(2), SW, one(wf[0], n % WS), ALU.mult, ALU.subtract).then_inc(w_lo, 1)

            block_scales(0)
            block_scales(1)

            def k_mean(u):
                v.wait_ge(k_sq, u + 1)
                ms = one(ss, u % 2)
                own.link(v.tensor_reduce(ms, quarters(one(sq0, u % 2)), AX.X, ALU.add))
                ts(ms, ms, 1.0 / DH, ALU.mult, EPS * SXW * SXW, ALU.add).then_inc(k_ms, 1)

            def k_norm(u):
                v.wait_ge(k_rs, u + 1)
                if not isinstance(u, int) or u >= 1:
                    v.wait_ge(k_t, u)
                tt(quarters(kn0[:, 0]), quarters(bank(u % KB)), one(rk, u % 2).unsqueeze(2).broadcast_to([P, R, DH]),
                   ALU.mult).then_inc(k_nm, 1)

            def k_low(u):
                c, m = u // MT, u % MT
                v.wait_ge(k_hi, u + 1)
                dst = [w[:, bass.ds(4 * c, 4), bass.ds(m * P, P)] for w in kt]
                stt(dst[1], quarters(bank(6)), nws[:, 1:2], dst[0], ALU.mult, ALU.subtract).then_inc(k_lo, 1)

            def k_turn(u):
                k_mean(u + 2)
                k_norm(u + 1)
                k_low(u)
            k_mean(0)
            k_mean(1)
            k_norm(0)
            k_turn(0)
            own.loop(1, 2 * MT - 2, 1, k_turn)
            k_norm(2 * MT - 1)
            k_low(2 * MT - 2)
            k_low(2 * MT - 1)

            def weights(n):
                block_scales(n + 2)
                weight_low(n)

            def dequantise(dst, k, i, ready, done):
                v.wait_ge(ready, i + 1)
                own.link(clip(one(dst, i), k))
                ts(one(dst, i), one(dst, i), MAGIC, ALU.subtract, aqp[:, k, 3:4], ALU.mult).then_inc(done, 1)

            def with_tiles(base, after, per):
                def turn(i):
                    weights(base + i)
                    after(i - 2)
                weights(base)
                weights(base + 1)
                own.loop(2, FT, 2 + per, turn)
                after(FT - 2)
                after(FT - 1)
                own.wait(own.n)

            def up_after(i):
                v.wait_ge(f_cp, i + 1)
                extrema(one(up, i), i)

            def gate_after(i):
                v.wait_ge(f_cp, FT + i + 1)
                extrema(one(gate, i), i)
                dequantise(up, 1, i, u_y, u_dq)

            with_tiles(0, up_after, 2)
            parameters(1, FT, 1.0)
            with_tiles(FT, gate_after, 3)
            parameters(2, FT, 1.0)

            def gate_front(i):
                dequantise(gate, 2, i, g_y, g_dq)

            def gate_back(i):
                v.wait_ge(s_y, i + 1)
                sg_, gt_ = one(sig, i % 2), one(gate, i)
                own.link(ts(sg_, sg_, MAGIC, ALU.max, MAGIC + QMAX, ALU.min))
                stt(gt_, sg_, MAGIC, gt_, ALU.subtract, ALU.mult).then_inc(gs_done, 1)
                v.wait_ge(gs_done, i + 1)
                extrema(one(gate, i), i)

            def down_turn(i):
                gate_front(i)
                weights(2 * FT + i)
                gate_back(i - 1)

            gate_front(0)
            weights(2 * FT)
            own.loop(1, FT - 2, 6, down_turn)
            gate_front(FT - 2)
            weight_low(NCH - 2)
            gate_back(FT - 3)
            gate_front(FT - 1)
            weight_low(NCH - 1)
            gate_back(FT - 2)
            gate_back(FT - 1)
            own.wait(own.n)
            parameters(3, FT, 2.0 ** -16)

            def times_up(i):
                v.wait_ge(p_y, i + 1)
                own.link(clip(one(gate, i), 3))
                stt(one(gate, i), one(gate, i), MAGIC, one(up, i), ALU.subtract, ALU.mult).then_inc(p_done, 1)
                v.wait_ge(p_done, i + 1)
                extrema(one(gate, i), i)
            own.loop(0, FT, 3, times_up)
            own.wait(own.n)
            parameters(4, FT, aqp[:, 3, 3:4])

            def out_int(i):
                v.wait_ge(o_y, i + 1)
                own.link(clip(one(gate, i), 4))
                ts(one(gate, i), one(gate, i), MAGIC, ALU.subtract, SINT, ALU.mult).then_inc(o_int, 1)

            def out_low(i):
                v.wait_ge(o_hi, i + 1)
                tt(one(og[1], i), one(gate, i), one(og[0], i), ALU.subtract).then_inc(o_lo, 1)

            out_int(0)

            def out_turn(i):
                out_int(i + 1)
                out_low(i)
            own.loop(0, FT - 1, 1, out_turn)
            out_low(FT - 1)

            for t in range(NT):
                v.wait_ge(d_ps, t + 1)
                own.link(stt(xres[:, t], bank(t), aqp[:, 4, 4:5], xres[:, t], ALU.mult, ALU.add))
                own.link(v.bn_stats(st6[:, t], xres[:, t]))
                own.link(v.bn_aggr(mv[:, t], st6[:, t]))
            norm_var()
            normalise(2)
            hidden_low(1, SX)

            v.wait_ge(in_mask, 16)
            own.link(ts(flat(mk), flat(mk), SXW, ALU.mult))

            def q_mean(u):
                v.wait_ge(a_sq, u + 1)
                own.link(v.tensor_reduce(ss[:, 0], quarters(sqa[:, 0]), AX.X, ALU.add))
                ts(ss[:, 0], ss[:, 0], 1.0 / DH, ALU.mult, EPS * SXW * SXW, ALU.add).then_inc(a_ms, 1)

            def q_norm(u):
                v.wait_ge(a_rs, u + 1)
                if not isinstance(u, int) or u >= 1:
                    v.wait_ge(a_qt, u)
                tt(quarters(qn[:, 0]), quarters(bank(4)), rk[:, 0].unsqueeze(2).broadcast_to([P, R, DH]),
                   ALU.mult).then_inc(a_qn, 1)

            def q_low(u):
                v.wait_ge(a_qh, u + 1)
                stt(qt[1], quarters(bank(5)), nws[:, 0:1], qt[0], ALU.mult, ALU.subtract).then_inc(a_ql, 1)

            def o_low(u):
                v.wait_ge(a_oh, u + 1)
                stt(ot[1], quarters(bank(6)), 1.0 / SP, ot[0], ALU.mult, ALU.subtract).then_inc(a_ol, 1)

            def add_out(j, s):
                t = s % 4
                v.wait_ge(a_y, 4 * j + s + 1)
                stt(xres[:, t], bank(7), 1.0 / SXW, xres[:, t], ALU.mult, ALU.add).then_inc(a_x, 1)

            def attention_step(j, s):
                u, t = 4 * j + s, s % 4
                more = not isinstance(j, int) or u + 1 < HK * NT
                for h in range(R):
                    if not isinstance(j, int) or u >= 1:
                        v.wait_ge(a_e, 4 * u - 3 + h)
                    wait_apart(v, a_s, 4 * u + h + 1, (in_mask, 16))
                    v.tensor_tensor_reduce(sc[:, h], bank(h), mk[:, t % 2], -1.0 / SXW, 3.0e38, ALU.add, ALU.min,
                                           mneg[:, h:h + 1]).then_inc(a_sm, 1)
                for h in range(R):
                    v.wait_ge(a_e, 4 * u + h + 1)
                    if h == 0 and (not isinstance(j, int) or u >= 1):
                        v.wait_ge(a_p, 4 * u)
                    v.reciprocal(rden[:, h:h + 1], den[:, h:h + 1]).then_inc(a_rd, 1)
                if more:
                    q_mean(u + 1)
                if not isinstance(j, int) or u >= 1:
                    o_low(u - 1)
                if more:
                    q_norm(u + 1)
                for h in range(R):
                    if more and h == R - 1:
                        q_low(u + 1)
                    v.wait_ge(a_ph, 4 * u + h + 1)
                    tt(pt[1][:, :, h * P:(h + 1) * P], quarters(bank(h)), pt[0][:, :, h * P:(h + 1) * P],
                       ALU.subtract).then_inc(a_pl, 1)
                if not isinstance(j, int) or u >= 1:
                    add_out(j, s - 1)

            q_mean(0)
            q_norm(0)
            q_low(0)
            attention_step(0, 0)

            def four_steps(j):
                for s in range(1, 5):
                    attention_step(j, s)
            own.loop(0, HK - 1, 4, four_steps)
            for s in range(1, 4):
                attention_step(HK - 1, s)
            o_low(HK * NT - 1)
            add_out(HK - 1, 3)
            v.wait_ge(a_x, HK * NT)

            for t in range(NT):
                own.mark(v.bn_stats(st6[:, t], xres[:, t]))
            own.wait(own.n)
            for t in range(NT):
                own.mark(v.bn_aggr(mv[:, t], st6[:, t]))
            own.wait(own.n)
            norm_var()
            v.wait_ge(in_mp, 16 * 5)
            own.mark(ts(flat(mbs[:, :, :]), flat(mb[:, :, :]), SXW, ALU.mult))
            own.link(ts(flat(rw_raw), flat(rw_raw), SW, ALU.mult))
            v.tensor_copy(flat(rw[0]), flat(rw_raw)).then_inc(r_ws, 1)
            v.wait_ge(r_ws, 1)
            tt(flat(rw[1]), flat(rw_raw), flat(rw[0]), ALU.subtract).then_inc(r_ws, 1)
            normalise(3)
            hidden_low(2, SX)

            def over(w, n):
                return w.unsqueeze(2).broadcast_to([P, NT, n])

            rb, rbias = (rbb[:, i].unsqueeze(1).broadcast_to([P, NT, NE]) for i in range(2))
            v.wait_ge(r_ps, 1)
            own.link(stt(lg, bank(4)[:, 0:NT * NE].rearrange("p (a b) -> p a b", a=NT), 1.0 / SXW, rb, ALU.mult, ALU.add))
            own.link(v.tensor_reduce(lmax, lg, AX.X, ALU.max))
            tt(lg, lg, over(lmax, NE), ALU.subtract).then_inc(r_sub, 1)
            v.wait_ge(r_exp, 1)
            own.link(v.tensor_reduce(lsum, lg, AX.X, ALU.add))
            own.link(v.reciprocal(linv, lsum))
            own.link(tt(score, lg, over(linv, NE), ALU.mult))
            own.link(tt(score, score, rbias, ALU.add))

            def ranks(dst, src, n):
                ra, rb_ = (w[:, :, 0:n * n].rearrange("p t (a b) -> p t a b", a=n) for w in (rt_a, rt_b))
                mine = src.unsqueeze(3).broadcast_to([P, NT, n, n])
                other = src.unsqueeze(2).broadcast_to([P, NT, n, n])
                low = tri[:, 0:n, 0:n].unsqueeze(1).broadcast_to([P, NT, n, n])
                own.mark(tt(ra, other, mine, ALU.is_gt))
                own.link(tt(rb_, other, mine, ALU.is_equal))
                own.link(tt(rb_, rb_, low, ALU.mult))
                own.link(tt(ra, ra, rb_, ALU.add))
                own.link(v.tensor_reduce(dst, ra, AX.X, ALU.add))

            own.link(v.tensor_reduce(flat(gmax), flat(score).rearrange("p (a b) -> p a b", b=4), AX.X, ALU.max))
            ranks(keep, gmax, 4)
            own.link(ts(keep, keep, 2.0, ALU.is_lt))
            own.link(ts(kbig, keep, -1.0, ALU.add, 1.0e30, ALU.mult))

            def groups(w):
                return flat(w).rearrange("p (a b) -> p a b", b=4)

            def spread4(w):
                return flat(w).unsqueeze(2).broadcast_to([P, NT * 4, 4])

            own.link(tt(groups(masked), groups(score), spread4(keep), ALU.mult))
            own.link(tt(groups(masked), groups(masked), spread4(kbig), ALU.add))
            ranks(rank, masked, NE)
            own.link(ts(rank, rank, 2.0, ALU.is_lt))
            own.mark(v.memset(gts[:, :, 0:NS], 1.0))
            own.link(tt(gts[:, :, NS:EX], score, rank, ALU.mult))
            ts(gsc, gts, 1.0 / SXW, ALU.mult).then_inc(gates_ready, 1)
            for t in range(NT):
                v.wait_ge(b3_ps, t + 1)
                stt(xres[:, t], bank(4 + t), 1.0, xres[:, t], ALU.mult, ALU.add).then_inc(b3_x, 1)

            def expert_step(j, s):
                e, q = 2 * j + s, s % 2
                v.wait_ge(m_sg, e + 1)
                stt(hu[:, q], bank(2 * q), mbs[:, 0, bass.ds(e, 1)], sg[:, q], ALU.add, ALU.mult).then_inc(m_u, 1)
                v.wait_ge(m_u, e + 1)
                v.wait_ge(m_h, 2 * e + 2)
                stt(hv[:, q], bank(2 * q + 1), mbs[:, 1, bass.ds(e, 1)], hu[:, q], ALU.add, ALU.mult).then_inc(m_v, 1)
                v.wait_ge(m_hh, e + 1)
                stt(ht[1][:, q], hv[:, q], 2.0 ** -16, ht[0][:, q], ALU.mult, ALU.subtract).then_inc(m_hl, 1)

            def expert_add(j, s):
                e = 2 * j + s
                for t in range(NT):
                    v.wait_ge(m_y, e * NT + t + 1)
                    stt(xres[:, t], bank(4 + t), gsc[:, t, bass.ds(e, 1)], xres[:, t], ALU.mult, ALU.add)\
                        .then_inc(m_x, 1)

            v.wait_ge(b3_x, NT)
            expert_step(0, 0)
            with v.Fori(0, EX // 2 - 1) as j:
                for s in range(1, 3):
                    expert_step(j, s)
                    expert_add(j, s - 1)
            expert_step(EX // 2 - 1, 1)
            expert_add(EX // 2 - 1, 0)
            expert_add(EX // 2 - 1, 1)


def kernel(**inputs):
    import numpy as np
    import concourse.bacc as bacc
    from concourse.bass_utils import run_bass_kernel_spmd

    get = {k: np.asarray(a) for k, a in inputs.items()}

    def rows(a, n):
        return a.reshape(n, P, -1).transpose(1, 0, 2)

    def every(a):
        return np.broadcast_to(a, (P,) + a.shape)

    x = rows(get["x"].reshape(TOK, D), NT)
    ctx = rows(get["ctx_4096"].reshape(KV, D), MT)
    ctx_t = rows(get["ctx_4096"].reshape(KV, D).T, KD)
    quant_par = every(np.concatenate([get["L0_xattn_x1_scale"], get["L0_xattn_x2_scale"],
                                      get["L0_xattn_x1_zp"], get["L0_xattn_x2_zp"]]))
    ident = np.eye(P, dtype=np.float32)
    ffn = np.zeros((NCH * P, D), np.float32)
    ffn[0:F] = get["L0_ffn_w_up"]
    ffn[FT * P:FT * P + F] = get["L0_ffn_w_gate"]
    down = np.zeros((D, FT * P), np.float32)
    down[:, 0:F] = get["L0_ffn_w_down"]
    ffn[2 * FT * P:] = down.reshape(KD, P, FT, P).transpose(2, 1, 0, 3).reshape(FT * P, D)
    ffn_w = ffn.reshape(NCH, P, D).transpose(1, 0, 2)
    kv = np.concatenate([get["L1_xattn_k_proj_w"], get["L1_xattn_v_proj_w"]]).T
    kv_w = kv.reshape(KD, P, 4, D).transpose(2, 1, 0, 3)
    mask = rows(get["mask_1x1xSxS2_ff0"].reshape(SQ, SKV), 2)
    norm_w = np.stack([get["L1_xattn_q_norm_w"], get["L1_xattn_k_norm_w"]], 1)
    wq = get["L1_xattn_q_proj_w"].T.reshape(KD, P, HK, R * DH).transpose(2, 1, 0, 3).reshape(HK, P, KD * D)
    wo = get["L1_xattn_o_proj_w"].T.reshape(HK, R, P, D).transpose(0, 2, 1, 3).reshape(HK, P, R * D)
    router_w = rows(get["L1_ffn_router_w"], KD)
    router_b = every(np.stack([get["L1_ffn_router_b"], get["L1_ffn_router_bias"]]))

    def first(shared, experts):
        return np.concatenate([shared.reshape(D, NS, INTER).transpose(1, 0, 2), experts])

    w1 = first(get["L1_ffn_sw1"], get["L1_ffn_ew1"]).reshape(EX, KD, P, INTER).transpose(0, 2, 1, 3)
    w2 = first(get["L1_ffn_sw2"], get["L1_ffn_ew2"]).reshape(EX, KD, P, INTER).transpose(0, 2, 1, 3)
    w3 = np.concatenate([get["L1_ffn_sw3"].reshape(NS, INTER, D), get["L1_ffn_ew3"]])
    moe_w = np.concatenate([w1.reshape(EX, P, D), w2.reshape(EX, P, D), w3], 2)
    moe_b = np.stack([np.concatenate([get["L1_ffn_sb1"].reshape(NS, INTER), get["L1_ffn_eb1"]]).T,
                      np.concatenate([get["L1_ffn_sb2"].reshape(NS, INTER), get["L1_ffn_eb2"]]).T], 1)
    moe_b3 = np.concatenate([get["L1_ffn_sb3"][None], get["L1_ffn_eb3"]])
    tri = every(np.tril(np.ones((NE, NE), np.float32), -1))

    given = dict(x=x, ctx=ctx, ctx_t=ctx_t, quant_par=quant_par, ident_in=ident, ffn_w=ffn_w, kv_w=kv_w,
                 mask=mask, norm_w=norm_w, wq=wq, wo=wo, router_w=router_w, router_b=router_b, moe_w=moe_w,
                 moe_b=moe_b, moe_b3=moe_b3, tri_in=tri)
    nc = bacc.Bacc("TRN2", target_bir_lowering=False, num_devices=1)
    arrays, args = {}, {}
    for name, a in given.items():
        a = np.ascontiguousarray(a)
        arrays[f"in_{name}"] = a
        args[name] = nc.dram_tensor(f"in_{name}", a.shape, mybir.dt.from_np(a.dtype), kind="ExternalInput").ap()
    out = nc.dram_tensor("out_x", (P, NT, D), F32, kind="ExternalOutput").ap()
    block_kernel(nc, out=out, **args)
    r = run_bass_kernel_spmd(nc, [arrays], core_ids=[0])
    return r.results[0]["out_x"].transpose(1, 0, 2).reshape(B, SQ, D)
```

```python
import concourse.bass as bass
from concourse import mybir
from contextlib import ExitStack

F32 = mybir.dt.float32
F16 = mybir.dt.float16
BF16 = mybir.dt.bfloat16
ALU = mybir.AluOpType
ACT = mybir.ActivationFunctionType
AX = mybir.AxisListType

P = 128
B, SQ, D = 2, 256, 512
SKV = 512
TOK, KV = B * SQ, B * SKV
NT = TOK // P
KD = D // P
MT = KV // P
F = 1376
FT = (F + P - 1) // P
QB = 32
NCH = 3 * FT
H, HK, DH = 32, 8, 128
R = H // HK
NE, NS, INTER = 16, 2, 128
EX = NE + NS
EPS = 1e-5
MAGIC = 12582912.0
QMAX = 65535.0
TINY = 1e-12

SX = 16.0
SW = 64.0
SXW = SX * SW
SINT = 2.0 ** -8
SP = 1024.0

RAW = 4
K_AHEAD = 3
KB = 4
KW = 4
WS = FT
ER = 3
SC = 6


class Chain:

    def __init__(self, eng, sem):
        self.eng, self.sem, self.n, self.k = eng, sem, 0, 0

    def mark(self, ins):
        ins.then_inc(self.sem, 1)
        self.n, self.k = self.n + 1, self.k + 1
        return self.n

    def link(self, ins):
        self.eng.wait_ge(self.sem, self.mark(ins))

    def wait(self, value):
        self.eng.wait_ge(self.sem, value)

    def loop(self, lo, hi, per, body):
        base, k = self.n, self.k
        with self.eng.Fori(lo, hi) as i:
            self.n = base + (i - lo) * per
            body(i)
            assert self.k - k == per, (self.k - k, per)
        self.n = base + (hi - lo) * per


def plain_loop(eng, lo, hi, body):
    with eng.Fori(lo, hi) as i:
        body(i)


def wait_apart(eng, sem, value, there):
    if not isinstance(value, int):
        eng.compute_val(value)
        eng.wait_ge(*there)
    eng.wait_ge(sem, value)


def block_kernel(nc, x, ctx, ctx_t, quant_par, ident_in, ffn_w, kv_w, mask, norm_w, wq, wo,
                 router_w, router_b, moe_w, moe_b, moe_b3, tri_in, out):
    es = ExitStack()
    with es:
        arena = es.enter_context(nc.sbuf_tensor("arena", [P, 204 * 256], F32))

        def carve(kib, shape, dtype=F32):
            n = 1
            for s in shape:
                n *= s
            words = n if dtype == F32 else n // 2
            start = int(kib * 256)
            v = arena[:, start:start + words]
            if dtype != F32:
                v = v.bitcast(dtype)
            if len(shape) == 2:
                v = v.rearrange("p (a b) -> p a b", a=shape[0])
            if len(shape) == 3:
                v = v.rearrange("p (a b c) -> p a b c", a=shape[0], b=shape[1])
            return v

        xres = carve(0, (NT, D))
        xn = carve(8, (NT, D))
        xt = [carve(16, (KD, TOK), F16), carve(20, (KD, TOK), F16)]
        ct = [carve(24, (KD, KV), F16), carve(32, (KD, KV), F16)]
        kt = [carve(40, (HK, KV), F16), carve(56, (HK, KV), F16)]
        vv = [carve(72, (MT, HK * DH), F16), carve(88, (MT, HK * DH), F16)]
        ctx_t_raw = carve(88, (KD, KV))
        ctx_raw = carve(150, (MT, D))
        q2 = carve(166, (MT, D), BF16)
        q1 = carve(174, (NT, D), BF16)
        q1t = carve(178, (KD, TOK), BF16)
        wf = [carve(104, (WS, D), F16), carve(115, (WS, D), F16)]
        kw_raw = carve(126, (KD, D))
        kw = [carve(134, (2, KD * D), F16), carve(142, (2, KD * D), F16)]
        up = carve(150, (FT, TOK))
        gate = carve(172, (FT, TOK))
        og = [carve(150, (FT, TOK), F16), carve(161, (FT, TOK), F16)]
        raw = carve(194, (RAW, D))
        deq = carve(202, (1, D))
        sq0 = carve(182, (2, D))
        kn0 = carve(186, (1, D))
        vf = carve(24 - 16, (2, D))
        sig = carve(12, (2, TOK))
        aq_raw = carve(24, (1, KD * D))
        ao_raw = carve(32, (1, R * D))
        aq = [carve(134, (2, KD * D), F16), carve(142, (2, KD * D), F16)]
        ao = [carve(126, (2, R * D), F16), carve(194, (2, R * D), F16)]
        sc = carve(150, (R, SKV))
        pr = carve(158, (R, SKV))
        pt = [carve(108, (KD, R * P), F16), carve(112, (KD, R * P), F16)]
        sqa = carve(166, (1, D))
        qn = carve(168, (1, D))
        qt = [carve(116, (R, P), F16), carve(117, (R, P), F16)]
        ot = [carve(118, (R, P), F16), carve(119, (R, P), F16)]
        mk = carve(104, (2, SKV))
        me_raw = carve(172, (ER, 3 * D))
        me = [carve(134, (2, 3 * D), F16), carve(140, (2, 3 * D), F16)]
        sg = carve(104, (2, TOK))
        hu = carve(108, (2, TOK))
        hv = carve(112, (2, TOK))
        ht = [carve(116, (2, TOK), F16), carve(118, (2, TOK), F16)]
        b3 = carve(120, (1, D))
        gt = carve(154, (1, TOK))
        rw_raw = carve(122, (KD, NE))
        rw = [carve(122.25, (KD, NE), F16), carve(122.375, (KD, NE), F16)]
        lg, score, masked = carve(156.5, (NT, NE)), carve(156.75, (NT, NE)), carve(157, (NT, NE))
        gmax, keep, kbig = carve(157.25, (NT, 4)), carve(157.5, (NT, 4)), carve(157.75, (NT, 4))
        lmax, lsum, linv = carve(158, (NT,)), carve(158.125, (NT,)), carve(158.25, (NT,))
        rank = carve(158.5, (NT, NE))
        gts, gsc = carve(158.75, (NT, EX)), carve(159.25, (NT, EX))
        tri = carve(123, (NE, NE))
        rbb = carve(122.5, (2, NE))
        rt_a = carve(160, (NT, NE * NE))
        rt_b = carve(164, (NT, NE * NE))

        def small(name, shape, dtype=F32):
            return es.enter_context(nc.sbuf_tensor(name, [P] + list(shape), dtype))

        ident = small("ident", [P])
        identb = small("identb", [P], BF16)
        onesf = small("onesf", [P])
        ones = small("ones", [P], BF16)
        nh = small("nh", [16])
        par = small("par", [4])
        pc = small("pc", [8])
        st6 = small("st6", [NT, 6])
        mv = small("mv", [NT, 2])
        ve = small("ve", [NT])
        rs = small("rs", [NT])
        rq = small("rq", [NT])
        rsum = small("rsum", [NT])
        mm2 = small("mm2", [2, FT])
        ext = small("ext", [2])
        row2 = small("row2", [4])
        aqp = small("aqp", [5, 8])
        dsc = small("dsc", [SC, 16])
        dsi = small("dsi", [SC, 16])
        ss = small("ss", [2, R])
        rk = small("rk", [2, R])
        nw = small("nw", [2])
        nws = small("nws", [2])
        mneg = small("mneg", [R])
        den = small("den", [R])
        rden = small("rden", [R])
        mb = small("mb", [2, EX])
        mbs = small("mbs", [2, EX])

        def one(v, i):
            return v[:, bass.ds(i, 1)].squeeze(1) if not isinstance(i, int) else v[:, i]

        def cols(v, a, n):
            return v[:, bass.ds(a, n)]

        ps = es.enter_context(nc.psum_tensor("ps", [P, 8, 512], F32))

        def bank(i):
            return one(ps, i)

        def hidden_bank(n, k):
            return bank(k + (KB if n == 0 else 0))

        def quarters(v):
            return v.rearrange("p (a b) -> p a b", a=4)

        names = set()

        def sem(name):
            assert name not in names
            names.add(name)
            return es.enter_context(nc.semaphore(name))

        in_x, in_par, in_ctx, in_ctt = sem("in_x"), sem("in_par"), sem("in_ctx"), sem("in_ctt")
        in_raw, in_kw, in_mask, in_aq, in_ao = sem("in_raw"), sem("in_kw"), sem("in_mask"), sem("in_aq"), sem("in_ao")
        in_me, in_mp, stored = sem("in_me"), sem("in_mp"), sem("stored")
        own_v, own_a, own_g = sem("own_v"), sem("own_a"), sem("own_g")
        const_g, const_v = sem("const_g"), sem("const_v")
        var_ready, rstd_ready = sem("var_ready"), sem("rstd_ready")
        q_consts, q1_ready, q1t_ps, q1t_ready = sem("q_consts"), sem("q1_ready"), sem("q1t_ps"), sem("q1t_ready")
        q2_ready, col_ps, col_added, x1_ps = sem("q2_ready"), sem("col_ps"), sem("col_added"), sem("x1_ps")
        ctx_scaled = sem("ctx_scaled")
        row_ps, row_terms, row_added = sem("row_ps"), sem("row_terms"), sem("row_added")
        ext_ready, ext_t, row_ready, ext_b = sem("ext_ready"), sem("ext_t"), sem("row_ready"), sem("ext_b")
        par_ready = sem("par_ready")
        xn_ready, xt_ps, xt_hi, xt_lo = sem("xn_ready"), sem("xt_ps"), sem("xt_hi"), sem("xt_lo")
        ct_sc, ct_hi, ct_lo, kw_sc, kw_hi, kw_lo = sem("ct_sc"), sem("ct_hi"), sem("ct_lo"), sem("kw_sc"), sem("kw_hi"), sem("kw_lo")
        k_ps, k_sq, k_ms, k_rs, k_nm, k_t, k_hi, k_lo = (sem("k_ps"), sem("k_sq"), sem("k_ms"), sem("k_rs"),
                                                         sem("k_nm"), sem("k_t"), sem("k_hi"), sem("k_lo"))
        v_ps, v_cp, v_lo = sem("v_ps"), sem("v_cp"), sem("v_lo")
        w_inv, w_div, w_mag, w_rnd, w_deq, w_t, w_hi, w_lo = (sem("w_inv"), sem("w_div"), sem("w_mag"), sem("w_rnd"), sem("w_deq"),
                                                       sem("w_t"), sem("w_hi"), sem("w_lo"))
        f_ps, f_cp = sem("f_ps"), sem("f_cp")
        u_y, u_cl, u_int = sem("u_y"), sem("u_cl"), sem("u_int")
        g_y, g_dq, s_y, gs_done = sem("g_y"), sem("g_dq"), sem("s_y"), sem("gs_done")
        p_y, p_cl, p_done = sem("p_y"), sem("p_cl"), sem("p_done")
        o_y, o_int, o_hi, o_lo, d_ps = sem("o_y"), sem("o_int"), sem("o_hi"), sem("o_lo"), sem("d_ps")
        aw_sc, aw_hi, aw_lo = sem("aw_sc"), sem("aw_hi"), sem("aw_lo")
        a_q, a_sq, a_ms, a_rs, a_qn, a_qt, a_qh, a_ql = (sem("a_q"), sem("a_sq"), sem("a_ms"), sem("a_rs"),
                                                         sem("a_qn"), sem("a_qt"), sem("a_qh"), sem("a_ql"))
        a_s, a_sm, a_e, a_rd, a_p, a_pt, a_ph, a_pl = (sem("a_s"), sem("a_sm"), sem("a_e"), sem("a_rd"),
                                                       sem("a_p"), sem("a_pt"), sem("a_ph"), sem("a_pl"))
        a_o, a_oh, a_ol, a_y, a_x = sem("a_o"), sem("a_oh"), sem("a_ol"), sem("a_y"), sem("a_x")
        r_ws, r_ps, r_sub, r_exp, gates_ready, g_t, g_c = (sem("r_ws"), sem("r_ps"), sem("r_sub"), sem("r_exp"),
                                                           sem("gates_ready"), sem("g_t"), sem("g_c"))
        b3_ps, b3_x = sem("b3_ps"), sem("b3_x")
        m_sc, m_hi_in, m_lo_in, m_hi_out, m_lo_out, m_h, m_sg, m_u, m_v, m_hh, m_hl, m_y, m_x = (
            sem("m_sc"), sem("m_hi_in"), sem("m_lo_in"), sem("m_hi_out"), sem("m_lo_out"), sem("m_h"), sem("m_sg"), sem("m_u"), sem("m_v"), sem("m_hh"),
            sem("m_hl"), sem("m_y"), sem("m_x"))

        block = es.enter_context(nc.Block())

        @block.sync
        def _(sp):
            sp.dma_start(xres, x).then_inc(in_x, 16)
            for t, s in ((par, quant_par), (ident, ident_in), (nw, norm_w)):
                sp.dma_start(t[:, :], s).then_inc(in_par, 16)
            sp.dma_start(ctx_raw, ctx).then_inc(in_ctx, 16)
            sp.dma_start(ctx_t_raw, ctx_t).then_inc(in_ctt, 16)

            def sp_wait(s, value):
                wait_apart(sp, s, value, (in_x, 16))

            def ring(n):
                if not isinstance(n, int) or n >= 1:
                    sp_wait(in_raw, n * 16)
                if not isinstance(n, int) or n >= RAW:
                    sp_wait(w_deq, n - RAW + 1)
                sp.dma_start(one(raw, n % RAW), one(ffn_w, n)).then_inc(in_raw, 16)

            def kw_load(c):
                if c >= 1:
                    sp.wait_ge(kw_lo, KD * c)
                sp.dma_start(kw_raw, kv_w[c]).then_inc(in_kw, 16)

            kw_load(0)
            for n in range(RAW):
                ring(n)
            kw_load(1)
            kw_load(2)
            plain_loop(sp, RAW, FT, ring)
            kw_load(3)
            plain_loop(sp, FT, NCH, ring)
            sp.wait_ge(v_ps, 2 * MT)
            sp.dma_start(aq_raw[:, 0], wq[0]).then_inc(in_aq, 16)
            sp.dma_start(ao_raw[:, 0], wo[0]).then_inc(in_ao, 16)
            sp.wait_ge(d_ps, NT)
            sp.dma_start(mk, mask).then_inc(in_mask, 16)
            sp.dma_start(mb[:, :, :], moe_b).then_inc(in_mp, 16)
            sp.dma_start(b3[0:NE + 1, 0], moe_b3).then_inc(in_mp, 16)
            sp.dma_start(rw_raw, router_w).then_inc(in_mp, 16)
            sp.dma_start(rbb, router_b).then_inc(in_mp, 16)
            sp.dma_start(tri, tri_in).then_inc(in_mp, 16)

            def attention_weights(g):
                sp_wait(aw_lo, g * 8 - 4)
                sp.dma_start(aq_raw[:, 0], wq[bass.ds(g, 1)].squeeze(0)).then_inc(in_aq, 16)
                sp_wait(aw_lo, g * 8)
                sp.dma_start(ao_raw[:, 0], wo[bass.ds(g, 1)].squeeze(0)).then_inc(in_ao, 16)

            plain_loop(sp, 1, HK, attention_weights)
            for e in range(ER):
                if e >= 1:
                    sp.wait_ge(in_me, 16 * e)
                sp.dma_start(me_raw[:, e], moe_w[e]).then_inc(in_me, 16)

            def expert_weights(e):
                sp_wait(in_me, e * 16)
                sp_wait(m_lo_out, e - ER + 1)
                sp.dma_start(one(me_raw, e % ER), moe_w[bass.ds(e, 1)].squeeze(0)).then_inc(in_me, 16)

            plain_loop(sp, ER, EX, expert_weights)
            for t in range(NT):
                sp.wait_ge(m_x, (EX - 1) * NT + t + 1)
                sp.dma_start(out[:, t], xres[:, t]).then_inc(stored, 16)
            sp.wait_ge(stored, 16 * NT)

        @block.gpsimd
        def _(g):
            own = Chain(g, own_g)
            g.memset(nh[:, :], -0.5).then_inc(const_g, 1)
            g.memset(ones[:, :], 1.0).then_inc(const_g, 1)
            g.wait_ge(const_g, 1)

            def rstd(k):
                g.wait_ge(var_ready, k + 1)
                g.tensor_tensor(rs[:, :], ve[:, :], nh[:, 0:NT], ALU.pow).then_inc(rstd_ready, 1)

            rstd(0)

            g.wait_ge(in_ctt, 16)
            for k in range(KD):
                g.tensor_scalar(ctx_t_raw[:, k], ctx_t_raw[:, k], SX, 1.0, ALU.mult, ALU.mult).then_inc(ct_sc, 1)

            def ct_low(k):
                g.wait_ge(ct_hi, k + 1)
                g.tensor_tensor(ct[1][:, k], ctx_t_raw[:, k], ct[0][:, k], ALU.subtract).then_inc(ct_lo, 1)

            def kw_scale(c, k):
                if k == 0:
                    g.wait_ge(in_kw, 16 * (c + 1))
                g.tensor_scalar(kw_raw[:, k], kw_raw[:, k], SW, 1.0, ALU.mult, ALU.mult).then_inc(kw_sc, 1)

            def kw_low(c, k):
                g.wait_ge(kw_hi, KD * c + k + 1)
                g.tensor_tensor(kw[1][:, c % 2, k * D:(k + 1) * D], kw_raw[:, k], kw[0][:, c % 2, k * D:(k + 1) * D],
                                ALU.subtract).then_inc(kw_lo, 1)

            def kw_split(c):
                for k in range(KD):
                    kw_scale(c, k)
                for k in range(KD):
                    kw_low(c, k)

            kw_split(0)
            ct_low(0)
            ct_low(1)
            rstd(1)
            ct_low(2)
            ct_low(3)
            kw_split(1)

            def divide(n):
                g.wait_ge(w_inv, n + 1)
                v = one(raw, n % RAW).rearrange("p (a b) -> p a b", b=QB)
                s = one(dsi, n % SC).unsqueeze(2).broadcast_to([P, D // QB, QB])
                g.tensor_tensor(v, v, s, ALU.mult).then_inc(w_div, 1)

            def scale_back(n):
                g.wait_ge(w_rnd, n + 1)
                v = one(raw, n % RAW).rearrange("p (a b) -> p a b", b=QB)
                s = one(dsc, n % SC).unsqueeze(2).broadcast_to([P, D // QB, QB])
                if not isinstance(n, int) or n >= 1:
                    g.wait_ge(w_t, n)
                g.tensor_tensor(deq[:, 0].rearrange("p (a b) -> p a b", b=QB), v, s, ALU.mult).then_inc(w_deq, 1)

            divide(0)
            divide(1)
            scale_back(0)
            divide(2)

            def k_pow(u):
                g.wait_ge(k_ms, u + 1)
                if not isinstance(u, int) or u >= 2:
                    g.wait_ge(k_nm, u - 1)
                g.tensor_tensor(one(rk, u % 2), one(ss, u % 2), nh[:, 0:R], ALU.pow).then_inc(k_rs, 1)

            k_pow(0)
            k_pow(1)
            plain_loop(g, 2, MT + 1, k_pow)
            for i in range(KD + 2):
                k_pow(MT + 1 + i)
                if i < KD:
                    kw_scale(2, i)
                if i >= 2:
                    kw_low(2, i - 2)
            plain_loop(g, MT + KD + 3, 2 * MT, k_pow)

            def divide(n):
                g.wait_ge(w_inv, n + 1)
                v = one(raw, n % RAW).rearrange("p (a b) -> p a b", b=QB)
                s = one(dsi, n % SC).unsqueeze(2).broadcast_to([P, D // QB, QB])
                g.tensor_tensor(v, v, s, ALU.mult).then_inc(w_div, 1)

            def scale_back(n):
                g.wait_ge(w_rnd, n + 1)
                v = one(raw, n % RAW).rearrange("p (a b) -> p a b", b=QB)
                s = one(dsc, n % SC).unsqueeze(2).broadcast_to([P, D // QB, QB])
                if not isinstance(n, int) or n >= 1:
                    g.wait_ge(w_t, n)
                g.tensor_tensor(deq[:, 0].rearrange("p (a b) -> p a b", b=QB), v, s, ALU.mult).then_inc(w_deq, 1)

            def weights(n, more=True):
                scale_back(n)
                if more:
                    divide(n + 2)

            weights(1)
            plain_loop(g, 2, FT + 2, weights)
            kw_split(3)
            plain_loop(g, FT + 2, 2 * FT + 1, weights)

            def v_low(u):
                g.wait_ge(v_cp, u + 1)
                c, m = u // MT, u % MT
                g.tensor_tensor(cols(one(vv[1], m), c * D, D), one(vf, u % 2), cols(one(vv[0], m), c * D, D),
                                ALU.subtract).then_inc(v_lo, 1)

            def down_turn(i, more=True):
                weights(2 * FT + 1 + i, more)
                v_low(i - 1)

            weights(2 * FT + 1)
            weights(2 * FT + 2)
            v_low(0)
            down_turn(2)
            plain_loop(g, 3, FT - 3, down_turn)
            down_turn(FT - 3, False)
            down_turn(FT - 2, False)
            plain_loop(g, FT - 2, 2 * MT, v_low)

            def attention_split(g_, part, half):
                pieces = []
                for k in (2 * half, 2 * half + 1):
                    src = (aq_raw, ao_raw)[part][:, 0, k * D:(k + 1) * D]
                    lo, hi = (cols(one(w, g_ % 2), k * D, D) for w in ((aq, ao)[part][1], (aq, ao)[part][0]))
                    pieces.append((k, src, lo, hi))
                    if k == 0:
                        wait_apart(g, (in_aq, in_ao)[part], (g_ + 1) * 16, (const_g, 2))
                    g.tensor_scalar(src, src, SW, 1.0, ALU.mult, ALU.mult).then_inc(aw_sc, 1)
                for k, src, lo, hi in pieces:
                    g.wait_ge(aw_hi, g_ * 8 + part * 4 + k + 1)
                    g.tensor_tensor(lo, src, hi, ALU.subtract).then_inc(aw_lo, 1)

            for part in range(2):
                for half in range(2):
                    attention_split(0, part, half)
            rstd(2)

            def q_pow(u):
                g.wait_ge(a_ms, u + 1)
                g.tensor_tensor(rk[:, 0], ss[:, 0], nh[:, 0:R], ALU.pow).then_inc(a_rs, 1)

            def attention_step(j, s):
                u = 4 * j + s
                for h in range(R):
                    wait_apart(g, a_rd, 4 * u + h + 1, (const_g, 2))
                    g.tensor_scalar(pr[:, h], pr[:, h], rden[:, h:h + 1], SP, ALU.mult, ALU.mult)\
                     .then_inc(a_p, 1)
                if not isinstance(j, int) or u + 1 < HK * NT:
                    q_pow(u + 1)
                if not isinstance(j, int):
                    attention_split(j + 1, (s - 1) // 2, (s - 1) % 2)

            q_pow(0)
            attention_step(0, 0)
            with g.Fori(0, HK - 1) as j:
                for s in range(1, 5):
                    attention_step(j, s)
            for s in range(1, 4):
                attention_step(HK - 1, s)

            def low_in(e, q):
                g.wait_ge(m_hi_in, e + 1)
                g.tensor_tensor(me[1][:, q, 0:2 * D], one(me_raw, e % ER)[:, 0:2 * D], me[0][:, q, 0:2 * D],
                                ALU.subtract).then_inc(m_lo_in, 1)

            def low_out(e, q):
                g.wait_ge(m_hi_out, e + 1)
                g.tensor_tensor(me[1][:, q, 2 * D:3 * D], one(me_raw, e % ER)[:, 2 * D:3 * D],
                                me[0][:, q, 2 * D:3 * D], ALU.subtract).then_inc(m_lo_out, 1)

            low_in(0, 0)
            low_out(0, 0)
            rstd(3)
            low_in(1, 1)

            def expert_turn(j):
                for s in range(2):
                    low_in(2 * j + s, s)
                    low_out(2 * j + s - 1, 1 - s)
            plain_loop(g, 1, EX // 2, expert_turn)
            low_out(EX - 1, 1)

        @block.scalar
        def _(a):
            def copy(out_, in_, scale=1.0, bias=0.0):
                return a.activation(out_, in_, ACT.Copy, scale=scale, bias=bias)

            a.wait_ge(in_ctx, 16)
            a.wait_ge(q_consts, 1)
            for b in range(B):
                half = ctx_raw[:, b * KD:(b + 1) * KD]
                a.activation(half, half, ACT.Identity, bias=par[:, 3:4], scale=pc[:, 1:2]).then_inc(ctx_scaled, 1)
            a.wait_ge(in_ctt, 16)
            for k in range(KD):
                a.wait_ge(ct_sc, k + 1)
                copy(ct[0][:, k], ctx_t_raw[:, k]).then_inc(ct_hi, 1)

            def kw_high(c, pieces=range(KD)):
                for k in pieces:
                    a.wait_ge(kw_sc, KD * c + k + 1)
                    if c >= 2:
                        a.wait_ge(k_ps, (c - 1) * MT)
                    copy(kw[0][:, c % 2, k * D:(k + 1) * D], kw_raw[:, k]).then_inc(kw_hi, 1)

            for k in range(KD):
                a.wait_ge(q1t_ps, k + 1)
                copy(q1t[:, k], bank(k).bitcast(BF16)[:, 0:TOK]).then_inc(q1t_ready, 1)
            kw_high(0)
            a.wait_ge(row_terms, 1)
            for t in range(NT):
                a.wait_ge(col_added, t + 1)
                a.activation(xres[:, t], xres[:, t], ACT.Identity, bias=rsum[:, t:t + 1], scale=1.0).then_inc(row_added, 1)
            kw_high(1)

            def hidden_high(n, scale):
                for k in range(KD):
                    a.wait_ge(xt_ps, KD * n + k + 1)
                    copy(xt[0][:, k], hidden_bank(n, k), scale).then_inc(xt_hi, 1)

            def round_weights(n):
                w = one(raw, n % RAW)
                wait_apart(a, w_div, n + 1, (in_ctt, 16))
                copy(w, w, 1.0, MAGIC).then_inc(w_mag, 1)
                wait_apart(a, w_mag, n + 1, (in_ctt, 16))
                copy(w, w, 1.0, -MAGIC).then_inc(w_rnd, 1)

            for n in range(3):
                round_weights(n)

            hidden_high(0, 1.0)

            def k_square(u):
                a.wait_ge(k_ps, u + 1)
                if not isinstance(u, int) or u >= 2:
                    a.wait_ge(k_ms, u - 1)
                a.activation(one(sq0, u % 2), bank(u % KB), ACT.Square).then_inc(k_sq, 1)

            def k_high(u):
                a.wait_ge(k_t, u + 1)
                c, m = u // MT, u % MT
                copy(kt[0][:, bass.ds(4 * c, 4), bass.ds(m * P, P)], quarters(bank(6)), nws[:, 1:2]).then_inc(k_hi, 1)

            a.wait_ge(const_v, 3)
            k_square(0)
            k_square(1)

            def k_turn(u):
                k_square(u + 2)
                k_high(u)
            k_turn(0)
            plain_loop(a, 1, MT + 1, k_turn)
            for i in range(KD):
                k_turn(MT + 1 + i)
                kw_high(2, [i])
            k_turn(MT + KD + 1)
            assert MT + KD + 2 == 2 * MT - 2
            k_high(2 * MT - 2)
            k_high(2 * MT - 1)

            def weight_high(n, reused=True):
                a.wait_ge(w_t, n + 1)
                if reused:
                    a.wait_ge(f_ps, n - WS + 1)
                copy(one(wf[0], n % WS), bank(2), SW).then_inc(w_hi, 1)

            def tile_out(n, dst, scale):
                a.wait_ge(f_ps, n + 1)
                copy(one(dst, n % FT), bank(n % 2), scale).then_inc(f_cp, 1)

            sx4 = aqp[:, 0, 4:5]

            def up_turn(n):
                weight_high(n + 1, reused=False)
                round_weights(n + 3)
                tile_out(n, up, sx4)

            weight_high(0, reused=False)
            plain_loop(a, 0, FT - 1, up_turn)
            weight_high(FT)
            round_weights(FT + 2)
            tile_out(FT - 1, up, sx4)

            def quantise(src, j, i, done):
                copy(one(src, i), one(src, i), aqp[:, j, 0:1], MAGIC).then_inc(done, 1)

            def up_integer(i):
                wait_apart(a, u_cl, i + 1, (in_ctt, 16))
                copy(one(up, i), one(up, i), 1.0, -MAGIC).then_inc(u_int, 1)

            def gate_turn(n):
                weight_high(n + 1)
                if not isinstance(n, int) or n >= FT + 3:
                    up_integer(n - FT - 3)
                round_weights(n + 3)
                tile_out(n, gate, sx4)
                if isinstance(n, int) and n == FT:
                    kw_high(3)
                    a.wait_ge(par_ready, 2)
                quantise(up, 1, n - FT, u_y)
            for i in range(3):
                gate_turn(FT + i)
            plain_loop(a, FT + 3, 2 * FT, gate_turn)

            def v_out(u):
                c, m = u // MT, u % MT
                a.wait_ge(v_ps, u + 1)
                copy(cols(one(vv[0], m), c * D, D), bank(4 + u % 2), 1.0 / SW)
                if not isinstance(u, int) or u >= 2:
                    a.wait_ge(v_lo, u - 1)
                copy(one(vf, u % 2), bank(4 + u % 2), 1.0 / SW).then_inc(v_cp, 1)

            def gate_front(i):
                quantise(gate, 2, i, g_y)

            def gate_sigmoid(i):
                wait_apart(a, g_dq, i + 1, (in_ctt, 16))
                a.activation(one(sig, i % 2), one(gate, i), ACT.Sigmoid).then_inc(own_a, 1)
                wait_apart(a, own_a, i + 1, (in_ctt, 16))
                copy(one(sig, i % 2), one(sig, i % 2), 65536.0, MAGIC).then_inc(s_y, 1)

            for i in range(FT - 3, FT):
                up_integer(i)
            v_out(0)
            a.wait_ge(par_ready, 3)
            gate_front(0)

            def down_turn(i, more=True, rounds=True):
                if more:
                    gate_front(i + 1)
                if not isinstance(i, int) or i >= 1:
                    if not isinstance(i, int) or i >= 3:
                        a.wait_ge(gs_done, i - 2)
                    gate_sigmoid(i - 1)
                if more:
                    weight_high(2 * FT + i + 1)
                    if rounds:
                        round_weights(2 * FT + i + 3)
                v_out(i + 1)

            for i in range(3):
                down_turn(i)
            plain_loop(a, 3, FT - 3, down_turn)
            down_turn(FT - 3, rounds=False)
            down_turn(FT - 2, rounds=False)
            down_turn(FT - 1, False)
            a.wait_ge(gs_done, FT - 2)
            gate_sigmoid(FT - 1)

            a.wait_ge(par_ready, 4)

            def product_quant(i):
                quantise(gate, 3, i, p_y)

            def product_turn(i):
                product_quant(i)
                v_out(FT + 1 + i)
            plain_loop(a, 0, 2 * MT - FT - 1, product_turn)
            plain_loop(a, 2 * MT - FT - 1, FT, product_quant)

            def attention_high(g_, part, k):
                n = g_ * 8 + part * 4 + k
                a.wait_ge(aw_sc, n + 1)
                copy(cols(one((aq, ao)[part][0], g_ % 2), k * D, D),
                     (aq_raw, ao_raw)[part][:, 0, k * D:(k + 1) * D]).then_inc(aw_hi, 1)

            for part in range(2):
                for k in range(4):
                    attention_high(0, part, k)
            a.wait_ge(par_ready, 5)

            def out_quant(i):
                quantise(gate, 4, i, o_y)

            def out_high(i):
                a.wait_ge(o_int, i + 1)
                copy(one(og[0], i), one(gate, i)).then_inc(o_hi, 1)
            out_quant(0)

            def out_turn(i):
                out_quant(i + 1)
                out_high(i)
            plain_loop(a, 0, FT - 1, out_turn)
            out_high(FT - 1)

            hidden_high(1, SX)

            def q_square(u):
                a.wait_ge(a_q, u + 1)
                a.activation(sqa[:, 0], bank(4), ACT.Square).then_inc(a_sq, 1)

            def q_high(u):
                a.wait_ge(a_qt, u + 1)
                copy(qt[0], quarters(bank(5)), nws[:, 0:1]).then_inc(a_qh, 1)

            def o_high(u):
                a.wait_ge(a_o, u + 1)
                copy(ot[0], quarters(bank(6)), 1.0 / SP).then_inc(a_oh, 1)

            def attention_step(j, s):
                u = 4 * j + s
                for h in range(R):
                    a.wait_ge(a_sm, 4 * u + h + 1)
                    if h == 0 and not (isinstance(j, int) and u == 0):
                        a.wait_ge(a_pt, 4 * u)
                    a.activation(pr[:, h], sc[:, h], ACT.Exp, bias=mneg[:, h:h + 1], scale=-1.0,
                                 accum_out=den[:, h:h + 1]).then_inc(a_e, 1)
                more = not isinstance(j, int) or u + 1 < HK * NT
                if more:
                    q_square(u + 1)
                if not isinstance(j, int) or u >= 1:
                    o_high(u - 1)
                for h in range(R):
                    if more and h == R - 1:
                        q_high(u + 1)
                    a.wait_ge(a_pt, 4 * u + h + 1)
                    if h == 0 and (not isinstance(j, int) or u >= 1):
                        a.wait_ge(a_o, u)
                    copy(pt[0][:, :, h * P:(h + 1) * P], quarters(bank(h))).then_inc(a_ph, 1)
                if not isinstance(j, int):
                    for i in range(2):
                        attention_high(j + 1, (s - 1) // 2, 2 * ((s - 1) % 2) + i)

            q_square(0)
            q_high(0)
            attention_step(0, 0)
            with a.Fori(0, HK - 1) as j:
                for s in range(1, 5):
                    attention_step(j, s)
            for s in range(1, 4):
                attention_step(HK - 1, s)
            o_high(HK * NT - 1)

            def scale(e):
                wait_apart(a, in_me, (e + 1) * 16, (in_ctt, 16))
                copy(one(me_raw, e % ER), one(me_raw, e % ER), SW).then_inc(m_sc, 1)

            def high_in(e, q):
                if not isinstance(e, int) or e >= 2:
                    wait_apart(a, m_h, (e - 1) * 2, (in_ctt, 16))
                wait_apart(a, m_sc, e + 1, (in_ctt, 16))
                copy(me[0][:, q, 0:2 * D], one(me_raw, e % ER)[:, 0:2 * D]).then_inc(m_hi_in, 1)

            def high_out(e, q):
                if not isinstance(e, int) or e >= 2:
                    wait_apart(a, m_y, (e - 1) * NT, (in_ctt, 16))
                wait_apart(a, m_sc, e + 1, (in_ctt, 16))
                copy(me[0][:, q, 2 * D:3 * D], one(me_raw, e % ER)[:, 2 * D:3 * D]).then_inc(m_hi_out, 1)

            scale(0)
            high_in(0, 0)
            high_out(0, 0)
            scale(1)
            high_in(1, 1)
            hidden_high(2, SX)
            a.wait_ge(r_sub, 1)
            a.activation(lg, lg, ACT.Exp).then_inc(r_exp, 1)

            def gates_out():
                a.wait_ge(g_t, 1)
                copy(gt[0:NE + 1, 0], bank(5)[0:NE + 1, :]).then_inc(g_c, 1)

            def expert_step(j, s):
                e, q = 2 * j + s, s % 2
                a.wait_ge(m_h, 2 * e + 1)
                if not isinstance(j, int) or e >= 2:
                    a.wait_ge(m_u, e - 1)
                a.activation(sg[:, q], bank(2 * q), ACT.Sigmoid, bias=mb[:, 0, bass.ds(e, 1)], scale=1.0 / SXW).then_inc(m_sg, 1)
                if not isinstance(j, int) or e + 2 < EX:
                    scale(e + 2)
                a.wait_ge(m_v, e + 1)
                if not isinstance(j, int) or e >= 2:
                    a.wait_ge(m_y, (e - 1) * NT)
                copy(ht[0][:, q], hv[:, q], 2.0 ** -16).then_inc(m_hh, 1)
                if isinstance(j, int) and e == 0:
                    gates_out()
                if not isinstance(j, int) or e + 2 < EX:
                    high_in(e + 2, q)
                if not isinstance(j, int) or e + 1 < EX:
                    high_out(e + 1, 1 - q)

            expert_step(0, 0)
            expert_step(0, 1)
            with a.Fori(1, EX // 2 - 1) as j:
                for s in range(2):
                    expert_step(j, s)
            expert_step(EX // 2 - 1, 0)
            expert_step(EX // 2 - 1, 1)

        @block.tensor
        def _(pe):
            def product(out_, lhs, rhs, first, last):
                pe.matmul(out_, lhs[0], rhs[0], start=first, stop=False)
                pe.matmul(out_, lhs[0], rhs[1], start=False, stop=False)
                return pe.matmul(out_, lhs[1], rhs[0], start=False, stop=last)

            pe.wait_ge(const_v, 2)
            pe.wait_ge(q1_ready, 1)
            for k in range(KD):
                for t in range(NT):
                    mm = pe.transpose(bank(k).bitcast(BF16)[:, t * P:(t + 1) * P], q1[:, t, k * P:(k + 1) * P],
                                      identb[:, :])
                mm.then_inc(q1t_ps, 1)
            pe.wait_ge(const_g, 2)
            for b in range(B):
                pe.wait_ge(q2_ready, b + 1)
                for k in range(KD):
                    mm = pe.matmul(bank(6 + b), ones[:, :], q2[:, b * KD + k], start=k == 0, stop=k == KD - 1)
                mm.then_inc(col_ps, 1)
            pe.wait_ge(q1t_ready, KD)
            for t in range(NT):
                for k in range(KD):
                    mm = pe.matmul(bank(2)[:, t:t + 1], q1t[:, k, t * P:(t + 1) * P], ones[:, 0:1],
                                   start=k == 0, stop=k == KD - 1)
            mm.then_inc(row_ps, 1)
            for t in range(NT):
                for k in range(KD):
                    mm = pe.matmul(bank((4, 5, 0, 1)[t]), q1t[:, k, t * P:(t + 1) * P], q2[:, t // 2 * KD + k],
                                   start=k == 0, stop=k == KD - 1)
                mm.then_inc(x1_ps, 1)

            def spread(k):
                pe.wait_ge(ext_ready, k + 1)
                pe.transpose(bank(7)[0:2, 0:P], ext[:, :], ident[:, :]).then_inc(ext_t, 1)
                pe.wait_ge(row_ready, k + 1)
                pe.matmul(bank(7)[:, P:P + 2], onesf[0:2, :], row2[0:2, 2:4], start=True, stop=True).then_inc(ext_b, 1)

            def hidden_transposes(n):
                pe.wait_ge(xn_ready, n + 1)
                for k in range(KD):
                    for t in range(NT):
                        mm = pe.transpose(hidden_bank(n, k)[:, t * P:(t + 1) * P], xn[:, t, k * P:(k + 1) * P], ident[:, :])
                    mm.then_inc(xt_ps, 1)

            def kv_product(c, m, dst):
                for k in range(KD):
                    lhs = [cols(h[:, k], m * P, P) for h in ct]
                    rhs = [cols(one(h, c), k * D, D) for h in kw]
                    mm = product(dst, lhs, rhs, k == 0, k == KD - 1)
                return mm

            def k_unit(c, m):
                u = c * MT + m
                if m == 0:
                    pe.wait_ge(kw_lo, KD * (c + 1))
                if not isinstance(c, int) or u >= KB:
                    pe.wait_ge(k_nm, u - KB + 1)
                kv_product(c, m, bank(m % KB)).then_inc(k_ps, 1)

            def k_transposes(u):
                pe.wait_ge(k_nm, u + 1)
                if u >= 1:
                    pe.wait_ge(k_lo, u)
                else:
                    pe.wait_ge(xt_lo, KD)
                for h in range(4):
                    mm = pe.transpose(bank(6)[:, h * P:(h + 1) * P], kn0[:, 0, h * P:(h + 1) * P], ident[:, :])
                mm.then_inc(k_t, 1)

            pe.wait_ge(ct_lo, KD)
            pe.wait_ge(var_ready, 2)
            units = [(c, m) for c in range(KW // 2) for m in range(MT)]
            for u, (c, m) in enumerate(units):
                if u == 1:
                    spread(0)
                if u == K_AHEAD:
                    hidden_transposes(0)
                k_unit(c, m)
                if u >= K_AHEAD:
                    k_transposes(u - K_AHEAD)
            for u in range(len(units) - K_AHEAD, len(units)):
                k_transposes(u)

            def weight_transposes(n):
                pe.wait_ge(w_deq, n + 1)
                if not isinstance(n, int) or n >= 1:
                    pe.wait_ge(w_lo, n)
                for k in range(4):
                    mm = pe.transpose(bank(2)[:, k * P:(k + 1) * P], deq[:, 0, k * P:(k + 1) * P],
                                      ident[:, :])
                mm.then_inc(w_t, 1)

            def tile(base, i, odd):
                n = base + i
                pe.wait_ge(w_lo, n + 1)
                if not isinstance(n, int) or n >= 2:
                    pe.wait_ge(f_cp, n - 1)
                for k in range(KD):
                    lhs = [cols(one(h, i), k * P, P) for h in wf]
                    mm = product(bank(odd), lhs, [h[:, k] for h in xt], k == 0, k == KD - 1)
                mm.then_inc(f_ps, 1)

            pe.wait_ge(xt_lo, KD)
            weight_transposes(0)

            def step(base, i, odd):
                weight_transposes(base + i + 1)
                tile(base, i, odd)

            def tiles(base):
                for i in range(1, 3):
                    step(base, i, (base + i) % 2)
                with pe.Fori(1, FT // 2) as j:
                    for s in range(2):
                        step(base, 2 * j + 1 + s, (base + 1 + s) % 2)

            assert FT % 2 == 1
            step(0, 0, 0)
            tiles(0)
            step(FT, 0, FT % 2)
            spread(1)
            tiles(FT)

            def v_unit(c, m, odd):
                u = c * MT + m
                pe.wait_ge(kw_lo, KD * (KW // 2 + c + 1))
                if not isinstance(u, int) or u >= 2:
                    pe.wait_ge(v_cp, u - 1)
                kv_product(c, m, bank(4 + odd)).then_inc(v_ps, 1)

            def v_turn(c, m, odd):
                weight_transposes(2 * FT + c * MT + m - 1)
                v_unit(c, m, odd)

            def by_two(c, lo, hi, turn):
                with pe.Fori(lo // 2, hi // 2) as j:
                    for s in range(2):
                        turn(c, 2 * j + s, s)

            last = FT + 1 - MT
            v_unit(0, 0, 0)
            weight_transposes(2 * FT + 1)
            spread(2)
            v_unit(0, 1, 1)
            v_unit(0, 2, 0)
            v_turn(0, 3, 1)
            by_two(0, 4, MT, v_turn)
            by_two(1, 0, last, v_turn)
            by_two(1, last, last + 2, v_unit)
            spread(3)
            by_two(1, last + 2, MT, v_unit)
            spread(4)

            def down(i, first=False, last=False):
                pe.wait_ge(o_lo, i + 1)
                for t in range(NT):
                    lhs = [cols(one(h, i), t * P, P) for h in og]
                    mm = product(bank(t), lhs, [one(h, i) for h in wf], first, last)
                    if last:
                        mm.then_inc(d_ps, 1)
            pe.wait_ge(w_lo, NCH)
            down(0, first=True)
            plain_loop(pe, 1, FT - 1, down)
            down(FT - 1, last=True)

            hidden_transposes(1)

            def q_unit(j, s):
                u, par_ = 4 * j + s, (j + s // 4) % 2
                if s % 4 == 0:
                    pe.wait_ge(aw_lo, (j + s // 4) * 8 + 4)
                if not isinstance(j, int) or u >= 1:
                    pe.wait_ge(a_qn, u)
                t = s % 4
                for k in range(KD):
                    rhs = [cols(one(h, par_), k * D, D) for h in aq]
                    mm = product(bank(4), [h[:, k, t * P:(t + 1) * P] for h in xt], rhs, k == 0, k == KD - 1)
                mm.then_inc(a_q, 1)

            def q_transposes(u):
                pe.wait_ge(a_qn, u + 1)
                if not isinstance(u, int) or u >= 1:
                    pe.wait_ge(a_ql, u)
                for h in range(R):
                    mm = pe.transpose(bank(5)[:, h * P:(h + 1) * P], qn[:, 0, h * P:(h + 1) * P], ident[:, :])
                mm.then_inc(a_qt, 1)

            def scores(j, s):
                u, grp, b = 4 * j + s, j + s // 4, s % 4 // 2
                pe.wait_ge(a_ql, u + 1)
                for h in range(R):
                    if not isinstance(j, int) or u >= 1:
                        pe.wait_ge(a_pl, 4 * u - 3 + h)
                    rhs = [cols(one(w, grp), b * SKV, SKV) for w in kt]
                    product(bank(h), [w[:, h] for w in qt], rhs, True, True).then_inc(a_s, 1)

            def values(j, s):
                u, grp, b = 4 * j + s, j + s // 4, s % 4 // 2
                pe.wait_ge(a_pl, 4 * u + 4)
                if not isinstance(j, int) or u >= 1:
                    pe.wait_ge(a_ol, u)
                for k in range(KD):
                    lhs = [cols(w[:, b * KD + k], grp * DH, DH) for w in vv]
                    mm = product(bank(6), lhs, [w[:, k] for w in pt], k == 0, k == KD - 1)
                mm.then_inc(a_o, 1)

            def p_transposes(u):
                for h in range(R):
                    pe.wait_ge(a_p, 4 * u + h + 1)
                    for k in range(KD):
                        mm = pe.transpose(bank(h)[:, k * P:(k + 1) * P], pr[:, h, k * P:(k + 1) * P], ident[:, :])
                    mm.then_inc(a_pt, 1)

            def project(j, s):
                u, par_ = 4 * j + s, (j + s // 4) % 2
                if s % 4 == 0:
                    pe.wait_ge(aw_lo, (j + s // 4) * 8 + 8)
                pe.wait_ge(a_ol, u + 1)
                if not isinstance(j, int) or u >= 1:
                    pe.wait_ge(a_x, u)
                for h in range(R):
                    rhs = [cols(one(w, par_), h * D, D) for w in ao]
                    mm = product(bank(7), [w[:, h] for w in ot], rhs, h == 0, h == R - 1)
                mm.then_inc(a_y, 1)

            def attention_step(j, s):
                u = 4 * j + s
                more = not isinstance(j, int) or u + 1 < HK * NT
                scores(j, s)
                if more:
                    q_unit(j, s + 1)
                if not isinstance(j, int) or u >= 1:
                    values(j, s - 1)
                p_transposes(u)
                if more:
                    q_transposes(u + 1)
                if not isinstance(j, int) or u >= 1:
                    project(j, s - 1)

            pe.wait_ge(xt_lo, 2 * KD)
            q_unit(0, 0)
            q_transposes(0)
            attention_step(0, 0)
            with pe.Fori(0, HK - 1) as j:
                for s in range(1, 5):
                    attention_step(j, s)
            for s in range(1, 4):
                attention_step(HK - 1, s)
            values(HK - 1, 3)
            project(HK - 1, 3)

            hidden_transposes(2)
            pe.wait_ge(xt_lo, 3 * KD)
            pe.wait_ge(r_ws, 2)
            for t in range(NT):
                for k in range(KD):
                    for i in range(2):
                        for w in range(2):
                            mm = pe.matmul(bank(4)[:, t * NE:(t + 1) * NE], xt[i][:, k, t * P:(t + 1) * P], rw[w][:, k],
                                           start=k + i + w == 0, stop=k == KD - 1 and i + w == 2)
            mm.then_inc(r_ps, 1)

            def hidden(e, q):
                pe.wait_ge(m_lo_in, e + 1)
                if not isinstance(e, int) or e >= 2:
                    pe.wait_ge(m_v, e - 1)
                for i in range(2):
                    for k in range(KD):
                        lhs = [w[:, q, i * D + k * P:i * D + (k + 1) * P] for w in me]
                        mm = product(bank(2 * q + i), lhs, [h[:, k] for h in xt], k == 0, k == KD - 1)
                    mm.then_inc(m_h, 1)

            def experts_out(e, q):
                pe.wait_ge(m_hl, e + 1)
                pe.wait_ge(m_lo_out, e + 1)
                for t in range(NT):
                    if not isinstance(e, int) or e >= 1:
                        pe.wait_ge(m_x, (e - 1) * NT + t + 1)
                    else:
                        pe.wait_ge(b3_x, t + 1)
                    product(bank(4 + t), [h[:, q, t * P:(t + 1) * P] for h in ht],
                            [w[:, q, 2 * D:3 * D] for w in me], True, True).then_inc(m_y, 1)

            hidden(0, 0)
            hidden(1, 1)
            pe.wait_ge(gates_ready, 1)
            for t in range(NT):
                mm = pe.transpose(bank(5)[0:NE + 1, t * P:(t + 1) * P], gts[:, t, 1:EX], ident[:, :])
            mm.then_inc(g_t, 1)
            pe.wait_ge(g_c, 1)
            for t in range(NT):
                pe.matmul(bank(4 + t), gt[0:NE + 1, 0, t * P:(t + 1) * P], b3[0:NE + 1, 0], start=True,
                          stop=True).then_inc(b3_ps, 1)
            experts_out(0, 0)
            with pe.Fori(0, EX // 2 - 1) as j:
                for s in range(1, 3):
                    hidden(2 * j + s + 1, (s + 1) % 2)
                    experts_out(2 * j + s, s % 2)
            experts_out(EX - 1, 1)

        @block.vector
        def _(v):
            own = Chain(v, own_v)

            def tt(out_, x_, y_, op):
                return v.tensor_tensor(out_, x_, y_, op)

            def ts(out_, x_, s1, o1, s2=None, o2=ALU.bypass):
                return v.tensor_scalar(out_, x_, s1, s2, o1, o2)

            def stt(out_, x_, s_, y_, o1, o2):
                return v.scalar_tensor_tensor(out_, x_, s_, y_, o1, o2)

            def flat(w):
                return w.rearrange("p a b -> p (a b)")

            v.memset(onesf[:, :], 1.0).then_inc(const_v, 1)
            v.wait_ge(in_par, 48)
            v.tensor_copy(identb[:, :], ident[:, :]).then_inc(const_v, 1)
            own.mark(ts(nws[:, 0:1], nw[:, 0:1], SW / DH ** 0.5, ALU.mult))
            ts(nws[:, 1:2], nw[:, 1:2], SX, ALU.mult).then_inc(const_v, 1)
            inv1, inv2, w1, w2, s12, c1, c2, k1 = (pc[:, i:i + 1] for i in range(8))
            own.mark(v.reciprocal(pc[:, 0:2], par[:, 0:2]))
            own.mark(ts(pc[:, 2:4], par[:, 2:4], -1.0, ALU.mult, 128.0, ALU.add))
            own.link(tt(s12, par[:, 0:1], par[:, 1:2], ALU.mult))
            own.mark(tt(c1, s12, w1, ALU.mult))
            own.mark(tt(c2, s12, w2, ALU.mult))
            ts(k1, w1, float(D), ALU.mult).then_inc(q_consts, 1)
            v.wait_ge(q_consts, 1)

            def norm_var():
                ts(ve[:, :], mv[:, :, 1], EPS, ALU.add).then_inc(var_ready, 1)

            def block_maxima(n):
                v.wait_ge(in_raw, 16 * (n + 1))
                src = one(raw, n % RAW).rearrange("p (a b) -> p a b", b=QB)
                return own.mark(v.tensor_reduce(one(dsc, n % SC), src, AX.X, ALU.max, apply_absolute_value=True))

            def scales(n, maxima):
                own.wait(maxima)
                s = one(dsc, n % SC)
                return own.mark(ts(s, s, 1.0 / 7.0, ALU.mult, TINY, ALU.max))

            def inverse_scales(n, scaled):
                own.wait(scaled)
                v.reciprocal(one(dsi, n % SC), one(dsc, n % SC)).then_inc(w_inv, 1)

            def block_scales(n):
                inverse_scales(n, scales(n, block_maxima(n)))

            def weight_low(n):
                v.wait_ge(w_hi, n + 1)
                stt(one(wf[1], n % WS), bank(2), SW, one(wf[0], n % WS), ALU.mult, ALU.subtract).then_inc(w_lo, 1)

            v.wait_ge(in_x, 16)
            for t in range(NT):
                own.mark(v.bn_stats(st6[:, t], xres[:, t]))
            own.wait(own.n)
            for t in range(NT):
                own.mark(v.bn_aggr(mv[:, t], st6[:, t]))
            own.wait(own.n)
            norm_var()
            v.wait_ge(rstd_ready, 1)
            own.link(ts(rq[:, :], rs[:, :], inv1, ALU.mult))
            for t in range(NT):
                own.mark(ts(xn[:, t], xres[:, t], mv[:, t, 0:1], ALU.subtract, rq[:, t:t + 1], ALU.mult))
            own.wait(own.n)
            own.link(ts(flat(xn), flat(xn), par[:, 2:3], ALU.add, MAGIC, ALU.add))
            own.link(ts(flat(xn), flat(xn), MAGIC, ALU.max, MAGIC + 255.0, ALU.min))
            ts(flat(q1), flat(xn), MAGIC + 128.0, ALU.subtract).then_inc(q1_ready, 1)
            for b in range(B):
                half = flat(ctx_raw[:, b * KD:(b + 1) * KD])
                v.wait_ge(ctx_scaled, b + 1)
                own.mark(ts(half, half, MAGIC, ALU.add, MAGIC, ALU.max))
            own.wait(own.n)
            for b in range(B):
                half = flat(ctx_raw[:, b * KD:(b + 1) * KD])
                ts(flat(q2[:, b * KD:(b + 1) * KD]), half, MAGIC + 255.0, ALU.min, MAGIC + 128.0, ALU.subtract)\
                    .then_inc(q2_ready, 1)
            for t in range(NT):
                v.wait_ge(col_ps, t // 2 + 1)
                stt(xres[:, t], bank(6 + t // 2), c1, xres[:, t], ALU.mult, ALU.add).then_inc(col_added, 1)
            v.wait_ge(row_ps, 1)
            own.link(ts(rsum[:, :], bank(2)[:, 0:NT], k1, ALU.add))
            ts(rsum[:, :], rsum[:, :], c2, ALU.mult).then_inc(row_terms, 1)

            for t in range(NT):
                v.wait_ge(row_added, t + 1)
                v.wait_ge(x1_ps, t + 1)
                own.link(stt(xres[:, t], bank((4, 5, 0, 1)[t]), s12, xres[:, t], ALU.mult, ALU.add))
                own.link(v.bn_stats(st6[:, t], xres[:, t]))
                own.link(v.bn_aggr(mv[:, t], st6[:, t]))
            norm_var()
            for n in range(3):
                block_scales(n)

            def normalise(k):
                v.wait_ge(rstd_ready, k + 1)
                for t in range(NT):
                    i = ts(xn[:, t], xres[:, t], mv[:, t, 0:1], ALU.subtract, rs[:, t:t + 1], ALU.mult)
                    if k != 1 and t == NT - 1:
                        i.then_inc(xn_ready, 1)
                    else:
                        own.mark(i)

            normalise(1)
            own.wait(own.n)

            def extrema(src, col):
                own.mark(v.tensor_reduce(mm2[:, 0, bass.ds(col, 1)], src, AX.X, ALU.max))
                own.mark(v.tensor_reduce(mm2[:, 1, bass.ds(col, 1)], src, AX.X, ALU.min, negate=True))

            for t in range(NT):
                extrema(xn[:, t], t)
            own.wait(own.n)

            def parameters(k, n, factor):
                v.tensor_reduce(ext[:, :], mm2[:, :, 0:n], AX.X, ALU.max).then_inc(ext_ready, 1)
                v.wait_ge(ext_t, k + 1)
                own.link(v.tensor_reduce(row2[0:2, 0:1], bank(7)[0:2, 0:P], AX.X, ALU.max))
                ts(row2[0:2, 2:4], ident[0:2, 0:2], row2[0:2, 0:1], ALU.mult).then_inc(row_ready, 1)
                v.wait_ge(ext_b, k + 1)
                yinv, lo, hi, s, s4, inv, z = (aqp[:, k, i:i + 1] for i in range(7))
                own.link(ts(ext[:, :], bank(7)[:, P:P + 2], 0.0, ALU.max, factor, ALU.mult))
                own.link(tt(s, ext[:, 0:1], ext[:, 1:2], ALU.add))
                own.link(ts(s, s, 1.0 / QMAX, ALU.mult, TINY, ALU.max))
                own.link(v.reciprocal(inv, s))
                own.mark(ts(s4, s, 4.0, ALU.mult))
                own.mark(ts(yinv, inv, factor, ALU.mult))
                own.link(ts(z, ext[:, 1:2], inv, ALU.mult, MAGIC, ALU.add))
                own.link(ts(z, z, MAGIC + QMAX, ALU.min, MAGIC, ALU.subtract))
                own.link(ts(lo, z, -1.0, ALU.mult, MAGIC, ALU.add))
                ts(hi, lo, QMAX, ALU.add).then_inc(par_ready, 1)
                v.wait_ge(par_ready, k + 1)

            def clip(dst, k):
                return ts(dst, dst, aqp[:, k, 1:2], ALU.max, aqp[:, k, 2:3], ALU.min)

            parameters(0, NT, 1.0)
            own.link(ts(flat(xn), flat(xn), aqp[:, 0, 0:1], ALU.mult, MAGIC, ALU.add))
            own.link(clip(flat(xn), 0))
            ts(flat(xn), flat(xn), MAGIC, ALU.subtract, SINT, ALU.mult).then_inc(xn_ready, 1)

            def hidden_low(n, scale):
                for k in range(KD):
                    v.wait_ge(xt_hi, KD * n + k + 1)
                    stt(xt[1][:, k], hidden_bank(n, k), scale, xt[0][:, k], ALU.mult, ALU.subtract).then_inc(xt_lo, 1)

            hidden_low(0, 1.0)


            def k_mean(u):
                v.wait_ge(k_sq, u + 1)
                ms = one(ss, u % 2)
                own.link(v.tensor_reduce(ms, quarters(one(sq0, u % 2)), AX.X, ALU.add))
                ts(ms, ms, 1.0 / DH, ALU.mult, EPS * SXW * SXW, ALU.add).then_inc(k_ms, 1)

            def k_norm(u):
                v.wait_ge(k_rs, u + 1)
                if not isinstance(u, int) or u >= 1:
                    v.wait_ge(k_t, u)
                tt(quarters(kn0[:, 0]), quarters(bank(u % KB)), one(rk, u % 2).unsqueeze(2).broadcast_to([P, R, DH]),
                   ALU.mult).then_inc(k_nm, 1)

            def k_low(u):
                c, m = u // MT, u % MT
                v.wait_ge(k_hi, u + 1)
                dst = [w[:, bass.ds(4 * c, 4), bass.ds(m * P, P)] for w in kt]
                stt(dst[1], quarters(bank(6)), nws[:, 1:2], dst[0], ALU.mult, ALU.subtract).then_inc(k_lo, 1)

            def k_turn(u):
                k_mean(u + 2)
                k_norm(u + 1)
                k_low(u)
            k_mean(0)
            k_mean(1)
            k_norm(0)
            k_turn(0)
            own.loop(1, 2 * MT - 2, 1, k_turn)
            k_norm(2 * MT - 1)
            k_low(2 * MT - 2)
            k_low(2 * MT - 1)

            def weights(n, between=None):
                m = block_maxima(n + 3)
                weight_low(n)
                m = scales(n + 3, m)
                if between:
                    between()
                inverse_scales(n + 3, m)

            def dequantise(dst, k, i, ready, done):
                v.wait_ge(ready, i + 1)
                own.link(clip(one(dst, i), k))
                ts(one(dst, i), one(dst, i), MAGIC, ALU.subtract, aqp[:, k, 3:4], ALU.mult).then_inc(done, 1)

            def with_tiles(base, after, per):
                def turn(i):
                    weights(base + i, lambda: after(i - 2))
                weights(base + 1)
                own.loop(2, FT, 2 + per, turn)
                weights(base + FT)
                after(FT - 2)
                after(FT - 1)
                own.wait(own.n)

            def up_after(i):
                v.wait_ge(f_cp, i + 1)
                extrema(one(up, i), i)

            def gate_after(i):
                v.wait_ge(f_cp, FT + i + 1)
                extrema(one(gate, i), i)
                v.wait_ge(u_y, i + 1)
                clip(one(up, i), 1).then_inc(u_cl, 1)

            weights(0)
            with_tiles(0, up_after, 2)
            parameters(1, FT, 1.0)
            with_tiles(FT, gate_after, 2)
            parameters(2, FT, 1.0)

            def gate_front(i):
                dequantise(gate, 2, i, g_y, g_dq)

            def sigmoid_clip(i):
                v.wait_ge(s_y, i + 1)
                return own.mark(ts(one(sig, i % 2), one(sig, i % 2), MAGIC, ALU.max, MAGIC + QMAX, ALU.min))

            def gated(i, clipped):
                own.wait(clipped)
                stt(one(gate, i), one(sig, i % 2), MAGIC, one(gate, i), ALU.subtract, ALU.mult).then_inc(gs_done, 1)

            def gated_extrema(i):
                v.wait_ge(gs_done, i + 1)
                extrema(one(gate, i), i)

            def down_turn(i):
                v.wait_ge(g_y, i + 1)
                bounded = own.mark(clip(one(gate, i), 2))
                clipped = sigmoid_clip(i - 2)
                own.wait(bounded)
                ts(one(gate, i), one(gate, i), MAGIC, ALU.subtract, aqp[:, 2, 3:4], ALU.mult).then_inc(g_dq, 1)
                gated(i - 2, clipped)
                if isinstance(i, int) and i + 3 >= FT:
                    weight_low(2 * FT + i)
                    gated_extrema(i - 2)
                else:
                    weights(2 * FT + i, lambda: gated_extrema(i - 2))

            for i in range(2):
                gate_front(i)
            weights(2 * FT + 1)
            own.loop(2, FT - 3, 6, down_turn)
            for i in range(FT - 3, FT):
                down_turn(i)
            for i in (FT - 2, FT - 1):
                gated(i, sigmoid_clip(i))
                gated_extrema(i)
            own.wait(own.n)
            parameters(3, FT, 2.0 ** -16)

            v.wait_ge(u_int, FT)
            own.link(tt(aqp[:, 3, 7:8], aqp[:, 3, 3:4], aqp[:, 1, 3:4], ALU.mult))
            def product_clip(i):
                v.wait_ge(p_y, i + 1)
                clip(one(gate, i), 3).then_inc(p_cl, 1)

            def times_up(i, more=True):
                v.wait_ge(p_cl, i + 1)
                stt(one(gate, i), one(gate, i), MAGIC, one(up, i), ALU.subtract, ALU.mult).then_inc(p_done, 1)
                if more:
                    product_clip(i + 1)
                v.wait_ge(p_done, i + 1)
                extrema(one(gate, i), i)

            product_clip(0)
            own.loop(0, FT - 1, 2, times_up)
            times_up(FT - 1, False)
            own.wait(own.n)
            parameters(4, FT, aqp[:, 3, 7:8])

            def out_int(i):
                v.wait_ge(o_y, i + 1)
                own.link(clip(one(gate, i), 4))
                ts(one(gate, i), one(gate, i), MAGIC, ALU.subtract, SINT, ALU.mult).then_inc(o_int, 1)

            def out_low(i):
                v.wait_ge(o_hi, i + 1)
                tt(one(og[1], i), one(gate, i), one(og[0], i), ALU.subtract).then_inc(o_lo, 1)

            out_int(0)

            def out_turn(i):
                out_int(i + 1)
                out_low(i)
            own.loop(0, FT - 1, 1, out_turn)
            out_low(FT - 1)

            for t in range(NT):
                v.wait_ge(d_ps, t + 1)
                own.link(stt(xres[:, t], bank(t), aqp[:, 4, 4:5], xres[:, t], ALU.mult, ALU.add))
                own.link(v.bn_stats(st6[:, t], xres[:, t]))
                own.link(v.bn_aggr(mv[:, t], st6[:, t]))
            norm_var()
            normalise(2)
            hidden_low(1, SX)

            v.wait_ge(in_mask, 16)
            own.link(ts(flat(mk), flat(mk), SXW, ALU.mult))

            def q_mean(u):
                v.wait_ge(a_sq, u + 1)
                own.link(v.tensor_reduce(ss[:, 0], quarters(sqa[:, 0]), AX.X, ALU.add))
                ts(ss[:, 0], ss[:, 0], 1.0 / DH, ALU.mult, EPS * SXW * SXW, ALU.add).then_inc(a_ms, 1)

            def q_norm(u):
                v.wait_ge(a_rs, u + 1)
                if not isinstance(u, int) or u >= 1:
                    v.wait_ge(a_qt, u)
                tt(quarters(qn[:, 0]), quarters(bank(4)), rk[:, 0].unsqueeze(2).broadcast_to([P, R, DH]),
                   ALU.mult).then_inc(a_qn, 1)

            def q_low(u):
                v.wait_ge(a_qh, u + 1)
                stt(qt[1], quarters(bank(5)), nws[:, 0:1], qt[0], ALU.mult, ALU.subtract).then_inc(a_ql, 1)

            def o_low(u):
                v.wait_ge(a_oh, u + 1)
                stt(ot[1], quarters(bank(6)), 1.0 / SP, ot[0], ALU.mult, ALU.subtract).then_inc(a_ol, 1)

            def add_out(j, s):
                t = s % 4
                v.wait_ge(a_y, 4 * j + s + 1)
                stt(xres[:, t], bank(7), 1.0 / SXW, xres[:, t], ALU.mult, ALU.add).then_inc(a_x, 1)

            def attention_step(j, s):
                u, t = 4 * j + s, s % 4
                more = not isinstance(j, int) or u + 1 < HK * NT
                for h in range(R):
                    if not isinstance(j, int) or u >= 1:
                        v.wait_ge(a_e, 4 * u - 3 + h)
                    wait_apart(v, a_s, 4 * u + h + 1, (in_mask, 16))
                    v.tensor_tensor_reduce(sc[:, h], bank(h), mk[:, t % 2], -1.0 / SXW, 3.0e38, ALU.add, ALU.min,
                                           mneg[:, h:h + 1]).then_inc(a_sm, 1)
                for h in range(R):
                    v.wait_ge(a_e, 4 * u + h + 1)
                    if h == 0 and (not isinstance(j, int) or u >= 1):
                        v.wait_ge(a_p, 4 * u)
                    v.reciprocal(rden[:, h:h + 1], den[:, h:h + 1]).then_inc(a_rd, 1)
                if more:
                    q_mean(u + 1)
                if more:
                    q_norm(u + 1)
                if not isinstance(j, int) or u >= 1:
                    o_low(u - 1)
                for h in range(R):
                    if more and h == R - 1:
                        q_low(u + 1)
                    v.wait_ge(a_ph, 4 * u + h + 1)
                    tt(pt[1][:, :, h * P:(h + 1) * P], quarters(bank(h)), pt[0][:, :, h * P:(h + 1) * P],
                       ALU.subtract).then_inc(a_pl, 1)
                if not isinstance(j, int) or u >= 1:
                    add_out(j, s - 1)

            q_mean(0)
            q_norm(0)
            q_low(0)
            attention_step(0, 0)

            def four_steps(j):
                for s in range(1, 5):
                    attention_step(j, s)
            own.loop(0, HK - 1, 4, four_steps)
            for s in range(1, 4):
                attention_step(HK - 1, s)
            o_low(HK * NT - 1)
            v.wait_ge(in_mp, 16 * 5)
            own.mark(ts(flat(mbs[:, :, :]), flat(mb[:, :, :]), SXW, ALU.mult))
            own.link(ts(flat(rw_raw), flat(rw_raw), SW, ALU.mult))
            v.tensor_copy(flat(rw[0]), flat(rw_raw)).then_inc(r_ws, 1)
            v.wait_ge(r_ws, 1)
            tt(flat(rw[1]), flat(rw_raw), flat(rw[0]), ALU.subtract).then_inc(r_ws, 1)

            v.wait_ge(a_x, HK * NT - 1)
            for t in range(NT - 1):
                own.mark(v.bn_stats(st6[:, t], xres[:, t]))
            add_out(HK - 1, 3)
            v.wait_ge(a_x, HK * NT)
            own.link(v.bn_stats(st6[:, NT - 1], xres[:, NT - 1]))
            for t in range(NT):
                own.mark(v.bn_aggr(mv[:, t], st6[:, t]))
            own.wait(own.n)
            norm_var()
            normalise(3)
            hidden_low(2, SX)

            def over(w, n):
                return w.unsqueeze(2).broadcast_to([P, NT, n])

            rb, rbias = (rbb[:, i].unsqueeze(1).broadcast_to([P, NT, NE]) for i in range(2))
            v.wait_ge(r_ps, 1)
            own.link(stt(lg, bank(4)[:, 0:NT * NE].rearrange("p (a b) -> p a b", a=NT), 1.0 / SXW, rb, ALU.mult, ALU.add))
            own.link(v.tensor_reduce(lmax, lg, AX.X, ALU.max))
            tt(lg, lg, over(lmax, NE), ALU.subtract).then_inc(r_sub, 1)
            v.wait_ge(r_exp, 1)
            own.link(v.tensor_reduce(lsum, lg, AX.X, ALU.add))
            own.link(v.reciprocal(linv, lsum))
            own.link(tt(score, lg, over(linv, NE), ALU.mult))
            own.link(tt(score, score, rbias, ALU.add))

            def ranks(dst, src, n):
                ra, rb_ = (w[:, :, 0:n * n].rearrange("p t (a b) -> p t a b", a=n) for w in (rt_a, rt_b))
                mine = src.unsqueeze(3).broadcast_to([P, NT, n, n])
                other = src.unsqueeze(2).broadcast_to([P, NT, n, n])
                low = tri[:, 0:n, 0:n].unsqueeze(1).broadcast_to([P, NT, n, n])
                own.mark(tt(ra, other, mine, ALU.is_gt))
                own.link(tt(rb_, other, mine, ALU.is_equal))
                own.link(tt(rb_, rb_, low, ALU.mult))
                own.link(tt(ra, ra, rb_, ALU.add))
                own.link(v.tensor_reduce(dst, ra, AX.X, ALU.add))

            own.link(v.tensor_reduce(flat(gmax), flat(score).rearrange("p (a b) -> p a b", b=4), AX.X, ALU.max))
            ranks(keep, gmax, 4)
            own.link(ts(keep, keep, 2.0, ALU.is_lt))
            own.link(ts(kbig, keep, -1.0, ALU.add, 1.0e30, ALU.mult))

            def groups(w):
                return flat(w).rearrange("p (a b) -> p a b", b=4)

            def spread4(w):
                return flat(w).unsqueeze(2).broadcast_to([P, NT * 4, 4])

            own.link(tt(groups(masked), groups(score), spread4(keep), ALU.mult))
            own.link(tt(groups(masked), groups(masked), spread4(kbig), ALU.add))
            ranks(rank, masked, NE)
            own.link(ts(rank, rank, 2.0, ALU.is_lt))
            own.mark(v.memset(gts[:, :, 0:NS], 1.0))
            own.link(tt(gts[:, :, NS:EX], score, rank, ALU.mult))
            ts(gsc, gts, 1.0 / SXW, ALU.mult).then_inc(gates_ready, 1)
            def expert_step(j, s):
                e, q = 2 * j + s, s % 2
                v.wait_ge(m_sg, e + 1)
                stt(hu[:, q], bank(2 * q), mbs[:, 0, bass.ds(e, 1)], sg[:, q], ALU.add, ALU.mult).then_inc(m_u, 1)
                v.wait_ge(m_u, e + 1)
                v.wait_ge(m_h, 2 * e + 2)
                stt(hv[:, q], bank(2 * q + 1), mbs[:, 1, bass.ds(e, 1)], hu[:, q], ALU.add, ALU.mult).then_inc(m_v, 1)
                v.wait_ge(m_hh, e + 1)
                stt(ht[1][:, q], hv[:, q], 2.0 ** -16, ht[0][:, q], ALU.mult, ALU.subtract).then_inc(m_hl, 1)

            def expert_add(j, s):
                e = 2 * j + s
                for t in range(NT):
                    v.wait_ge(m_y, e * NT + t + 1)
                    stt(xres[:, t], bank(4 + t), gsc[:, t, bass.ds(e, 1)], xres[:, t], ALU.mult, ALU.add)\
                        .then_inc(m_x, 1)

            expert_step(0, 0)
            for t in range(NT):
                v.wait_ge(b3_ps, t + 1)
                stt(xres[:, t], bank(4 + t), 1.0, xres[:, t], ALU.mult, ALU.add).then_inc(b3_x, 1)
            v.wait_ge(b3_x, NT)
            with v.Fori(0, EX // 2 - 1) as j:
                for s in range(1, 3):
                    expert_step(j, s)
                    expert_add(j, s - 1)
            expert_step(EX // 2 - 1, 1)
            expert_add(EX // 2 - 1, 0)
            expert_add(EX // 2 - 1, 1)


def kernel(**inputs):
    import numpy as np
    import concourse.bacc as bacc
    from concourse.bass_utils import run_bass_kernel_spmd

    get = {k: np.asarray(a) for k, a in inputs.items()}

    def rows(a, n):
        return a.reshape(n, P, -1).transpose(1, 0, 2)

    def every(a):
        return np.broadcast_to(a, (P,) + a.shape)

    x = rows(get["x"].reshape(TOK, D), NT)
    ctx = rows(get["ctx_4096"].reshape(KV, D), MT)
    ctx_t = rows(get["ctx_4096"].reshape(KV, D).T, KD)
    quant_par = every(np.concatenate([get["L0_xattn_x1_scale"], get["L0_xattn_x2_scale"],
                                      get["L0_xattn_x1_zp"], get["L0_xattn_x2_zp"]]))
    ident = np.eye(P, dtype=np.float32)
    ffn = np.zeros((NCH * P, D), np.float32)
    ffn[0:F] = get["L0_ffn_w_up"]
    ffn[FT * P:FT * P + F] = get["L0_ffn_w_gate"]
    down = np.zeros((D, FT * P), np.float32)
    down[:, 0:F] = get["L0_ffn_w_down"]
    ffn[2 * FT * P:] = down.reshape(KD, P, FT, P).transpose(2, 1, 0, 3).reshape(FT * P, D)
    ffn_w = ffn.reshape(NCH, P, D).transpose(1, 0, 2)
    kv = np.concatenate([get["L1_xattn_k_proj_w"], get["L1_xattn_v_proj_w"]]).T
    kv_w = kv.reshape(KD, P, 4, D).transpose(2, 1, 0, 3)
    mask = rows(get["mask_1x1xSxS2_ff0"].reshape(SQ, SKV), 2)
    norm_w = np.stack([get["L1_xattn_q_norm_w"], get["L1_xattn_k_norm_w"]], 1)
    wq = get["L1_xattn_q_proj_w"].T.reshape(KD, P, HK, R * DH).transpose(2, 1, 0, 3).reshape(HK, P, KD * D)
    wo = get["L1_xattn_o_proj_w"].T.reshape(HK, R, P, D).transpose(0, 2, 1, 3).reshape(HK, P, R * D)
    router_w = rows(get["L1_ffn_router_w"], KD)
    router_b = every(np.stack([get["L1_ffn_router_b"], get["L1_ffn_router_bias"]]))

    def first(shared, experts):
        return np.concatenate([shared.reshape(D, NS, INTER).transpose(1, 0, 2), experts])

    w1 = first(get["L1_ffn_sw1"], get["L1_ffn_ew1"]).reshape(EX, KD, P, INTER).transpose(0, 2, 1, 3)
    w2 = first(get["L1_ffn_sw2"], get["L1_ffn_ew2"]).reshape(EX, KD, P, INTER).transpose(0, 2, 1, 3)
    w3 = np.concatenate([get["L1_ffn_sw3"].reshape(NS, INTER, D), get["L1_ffn_ew3"]])
    moe_w = np.concatenate([w1.reshape(EX, P, D), w2.reshape(EX, P, D), w3], 2)
    moe_b = np.stack([np.concatenate([get["L1_ffn_sb1"].reshape(NS, INTER), get["L1_ffn_eb1"]]).T,
                      np.concatenate([get["L1_ffn_sb2"].reshape(NS, INTER), get["L1_ffn_eb2"]]).T], 1)
    moe_b3 = np.concatenate([get["L1_ffn_sb3"][None], get["L1_ffn_eb3"]])
    tri = every(np.tril(np.ones((NE, NE), np.float32), -1))

    given = dict(x=x, ctx=ctx, ctx_t=ctx_t, quant_par=quant_par, ident_in=ident, ffn_w=ffn_w, kv_w=kv_w,
                 mask=mask, norm_w=norm_w, wq=wq, wo=wo, router_w=router_w, router_b=router_b, moe_w=moe_w,
                 moe_b=moe_b, moe_b3=moe_b3, tri_in=tri)
    nc = bacc.Bacc("TRN2", target_bir_lowering=False, num_devices=1)
    arrays, args = {}, {}
    for name, a in given.items():
        a = np.ascontiguousarray(a)
        arrays[f"in_{name}"] = a
        args[name] = nc.dram_tensor(f"in_{name}", a.shape, mybir.dt.from_np(a.dtype), kind="ExternalInput").ap()
    out = nc.dram_tensor("out_x", (P, NT, D), F32, kind="ExternalOutput").ap()
    block_kernel(nc, out=out, **args)
    r = run_bass_kernel_spmd(nc, [arrays], core_ids=[0])
    return r.results[0]["out_x"].transpose(1, 0, 2).reshape(B, SQ, D)
```
